# Optimizing a Trainium2 kernel written in Bass

```python
import numpy as np
import jax
import jax.numpy as jnp

def _softmax(x, axis=-1):
    return jax.nn.softmax(x, axis=axis)

def _gelu(x):
    return jax.nn.gelu(x, approximate=True)

def _silu(x):
    return jax.nn.silu(x)

def _sigmoid(x):
    return jax.nn.sigmoid(x)

def _layernorm(x, axis=-1, eps=1e-05):
    m = jnp.mean(x, axis=axis, keepdims=True)
    v = jnp.var(x, axis=axis, keepdims=True)
    return (x - m) / jnp.sqrt(v + eps)

def _scatter_add(tgt, idx, src, axis=0):
    return tgt.at[idx].add(src)

def _segment_sum(src, seg, n):
    return jax.ops.segment_sum(src, seg, n)
kernel_name = 'mk_vit_tower_d2_tok_img1024_r4_328528'

def setup_inputs(seed: int=0):
    np.random.seed(seed)
    _w = jnp.asarray

    def _rec_inputs():
        import jax
        import jax.numpy as jnp
        _rk = jax.random.key(seed)
        x = -0.00016672 + 0.999947 * jax.random.normal(jax.random.fold_in(_rk, 1), (64, 3, 112, 112), jnp.float32)
        return x
    x = _rec_inputs()

    def _L0_tok_setup():
        import jax, jax.numpy as jnp
        import numpy as np
        IMG = 96
        P = 16
        C = 3
        D = 256
        B = 64
        key = jax.random.key(seed)
        kx, kw, kb = jax.random.split(key, 3)
        fan_in = C * P * P
        bound = 1.0 / np.sqrt(fan_in)
        x = jax.random.normal(kx, (B, C, IMG, IMG), dtype=jnp.float32)
        W = jax.random.uniform(kw, (D, fan_in), dtype=jnp.float32, minval=-bound, maxval=bound)
        b = jax.random.uniform(kb, (D,), dtype=jnp.float32, minval=-bound, maxval=bound)
        return {'x': x, 'W': W, 'b': b}
    _L0_tok_all = _L0_tok_setup()
    _L0_tok_in = {k: v for k, v in _L0_tok_all.items() if k in ('W', 'b')}
    del _L0_tok_all

    def _L0_attn_setup():
        import jax, jax.numpy as jnp
        import numpy as np
        NUM_HEADS = 1
        LN_EPS = 1e-05
        key = jax.random.key(seed)
        ks = jax.random.split(key, 4)
        B, L, D = (8, 1024, 256)
        x = jax.random.normal(ks[0], (B, L, D), dtype=jnp.float32)
        qkv_w = jax.random.normal(ks[1], (3 * D, D), dtype=jnp.float32) * np.float32(np.sqrt(1.0 / D))
        qkv_b = jnp.zeros((3 * D,), dtype=jnp.float32)
        proj_w = jax.random.normal(ks[2], (D, D), dtype=jnp.float32) * np.float32(np.sqrt(1.0 / D))
        proj_b = jnp.zeros((D,), dtype=jnp.float32)
        return {'x': x, 'norm_w': jnp.ones((D,), dtype=jnp.float32), 'norm_b': jnp.zeros((D,), dtype=jnp.float32), 'qkv_w': qkv_w, 'qkv_b': qkv_b, 'proj_w': proj_w, 'proj_b': proj_b}
    _L0_attn_all = _L0_attn_setup()
    _L0_attn_in = {k: v for k, v in _L0_attn_all.items() if k in ('norm_w', 'norm_b', 'qkv_w', 'qkv_b', 'proj_w', 'proj_b')}
    del _L0_attn_all

    def _L0_ffn_setup():
        import jax, jax.numpy as jnp
        import numpy as np
        B, P, D, D_MLP, E, K = (2, 512, 256, 1024, 8, 2)
        key = jax.random.key(seed)
        k_x, k_g, k_in, k_out = jax.random.split(key, 4)
        s_in = 1.0 / np.sqrt(D).astype(np.float32)
        s_out = 1.0 / np.sqrt(D_MLP).astype(np.float32)
        return {'x': jax.random.normal(k_x, (B, P, D), dtype=jnp.float32), 'W_gate': jax.random.normal(k_g, (D, E), dtype=jnp.float32) * s_in, 'W_in': jax.random.normal(k_in, (E, D, D_MLP), dtype=jnp.float32) * s_in, 'b_in': jnp.zeros((E, D_MLP), dtype=jnp.float32), 'W_out': jax.random.normal(k_out, (E, D_MLP, D), dtype=jnp.float32) * s_out, 'b_out': jnp.zeros((E, D), dtype=jnp.float32)}
    _L0_ffn_all = _L0_ffn_setup()
    _L0_ffn_in = {k: v for k, v in _L0_ffn_all.items() if k in ('W_gate', 'W_in', 'b_in', 'W_out', 'b_out')}
    del _L0_ffn_all

    def _L1_attn_setup():
        import jax, jax.numpy as jnp
        import numpy as np
        N_LAYER = 12
        N_HEAD = 16
        N_EMBD = 256
        key = jax.random.key(seed)
        k0, k1, k2 = jax.random.split(key, 3)
        B, T, C = (4, 512, N_EMBD)
        inputs_embeds = jax.random.normal(k0, (B, T, C), dtype=jnp.float32)
        Wqkv = jax.random.normal(k1, (N_LAYER, 3 * C, C), dtype=jnp.float32) * 0.0002
        bqkv = jnp.zeros((N_LAYER, 3 * C), dtype=jnp.float32)
        Wproj = jax.random.normal(k2, (N_LAYER, C, C), dtype=jnp.float32) * 0.0002
        bproj = jnp.zeros((N_LAYER, C), dtype=jnp.float32)
        return {'inputs_embeds': inputs_embeds, 'Wqkv': Wqkv, 'bqkv': bqkv, 'Wproj': Wproj, 'bproj': bproj}
    _L1_attn_all = _L1_attn_setup()
    _L1_attn_in = {k: v for k, v in _L1_attn_all.items() if k in ('Wqkv', 'bqkv', 'Wproj', 'bproj')}
    del _L1_attn_all

    def _L1_ffn_setup():
        import jax, jax.numpy as jnp
        import numpy as np
        B, S, IN, OUT, E, R = (8, 1024, 256, 256, 8, 8)
        LORA_ALPHA = 16
        SCALING = LORA_ALPHA / R
        key = jax.random.key(seed)
        k = jax.random.split(key, 6)
        x = jax.random.normal(k[0], (B, S, IN), dtype=jnp.float32)
        base_w = jax.random.normal(k[1], (OUT, IN), dtype=jnp.float32) * 0.02
        base_b = jnp.zeros((OUT,), dtype=jnp.float32)
        lora_A = jax.random.normal(k[2], (IN, R), dtype=jnp.float32) * 0.02
        lora_B = jax.random.normal(k[3], (E, R, OUT), dtype=jnp.float32) * 0.02
        router_w = jax.random.normal(k[4], (E, IN), dtype=jnp.float32) * 0.02
        router_b = jnp.zeros((E,), dtype=jnp.float32)
        return {'x': x, 'base_w': base_w, 'base_b': base_b, 'lora_A': lora_A, 'lora_B': lora_B, 'router_w': router_w, 'router_b': router_b}
    _L1_ffn_all = _L1_ffn_setup()
    _L1_ffn_in = {k: v for k, v in _L1_ffn_all.items() if k in ('base_w', 'base_b', 'lora_A', 'lora_B', 'router_w', 'router_b')}
    del _L1_ffn_all
    return {'x': x, 'L0_tok_W': _L0_tok_in['W'], 'L0_tok_b': _L0_tok_in['b'], 'L0_attn_norm_w': _L0_attn_in['norm_w'], 'L0_attn_norm_b': _L0_attn_in['norm_b'], 'L0_attn_qkv_w': _L0_attn_in['qkv_w'], 'L0_attn_qkv_b': _L0_attn_in['qkv_b'], 'L0_attn_proj_w': _L0_attn_in['proj_w'], 'L0_attn_proj_b': _L0_attn_in['proj_b'], 'L0_ffn_W_gate': _L0_ffn_in['W_gate'], 'L0_ffn_W_in': _L0_ffn_in['W_in'], 'L0_ffn_b_in': _L0_ffn_in['b_in'], 'L0_ffn_W_out': _L0_ffn_in['W_out'], 'L0_ffn_b_out': _L0_ffn_in['b_out'], 'L1_attn_Wqkv': _L1_attn_in['Wqkv'], 'L1_attn_bqkv': _L1_attn_in['bqkv'], 'L1_attn_Wproj': _L1_attn_in['Wproj'], 'L1_attn_bproj': _L1_attn_in['bproj'], 'L1_ffn_base_w': _L1_ffn_in['base_w'], 'L1_ffn_base_b': _L1_ffn_in['base_b'], 'L1_ffn_lora_A': _L1_ffn_in['lora_A'], 'L1_ffn_lora_B': _L1_ffn_in['lora_B'], 'L1_ffn_router_w': _L1_ffn_in['router_w'], 'L1_ffn_router_b': _L1_ffn_in['router_b']}

def reference(x, L0_tok_W, L0_tok_b, L0_attn_norm_w, L0_attn_norm_b, L0_attn_qkv_w, L0_attn_qkv_b, L0_attn_proj_w, L0_attn_proj_b, L0_ffn_W_gate, L0_ffn_W_in, L0_ffn_b_in, L0_ffn_W_out, L0_ffn_b_out, L1_attn_Wqkv, L1_attn_bqkv, L1_attn_Wproj, L1_attn_bproj, L1_ffn_base_w, L1_ffn_base_b, L1_ffn_lora_A, L1_ffn_lora_B, L1_ffn_router_w, L1_ffn_router_b):
    import jax
    import jax.numpy as jnp

    def _L0_tok_ref(x, W, b):
        import jax, jax.numpy as jnp
        import numpy as np
        IMG = 96
        P = 16
        C = 3
        D = 256
        B = 64
        Bsz, Cc, H, Wd = x.shape
        gh, gw = (H // P, Wd // P)
        patches = x.reshape(Bsz, Cc, gh, P, gw, P).transpose(0, 2, 4, 1, 3, 5)
        patches = patches.reshape(Bsz, gh * gw, Cc * P * P)
        return jnp.einsum('bnf,df->bnd', patches, W) + b

    def _L0_attn_ref(x, norm_w, norm_b, qkv_w, qkv_b, proj_w, proj_b):
        import jax, jax.numpy as jnp
        import numpy as np
        NUM_HEADS = 1
        LN_EPS = 1e-05
        B, L, D = x.shape
        H = NUM_HEADS
        mu = jnp.mean(x, axis=-1, keepdims=True)
        var = jnp.mean(jnp.square(x - mu), axis=-1, keepdims=True)
        h = (x - mu) / jnp.sqrt(var + LN_EPS) * norm_w + norm_b
        qkv = h @ qkv_w.T + qkv_b
        qkv = qkv.reshape(B * H, L // H, 3, D)
        q, k, v = (qkv[..., 0, :], qkv[..., 1, :], qkv[..., 2, :])
        scale = np.float32(1.0 / np.sqrt(L // H))
        w = jax.nn.softmax(jnp.einsum('ncq,nck->nqk', q, k * scale), axis=2)
        a = jnp.einsum('nqk,nck->ncq', w, v)
        a = a.reshape(B, L, D)
        return a @ proj_w.T + proj_b + x

    def _L0_ffn_ref(x, W_gate, W_in, b_in, W_out, b_out):
        import jax, jax.numpy as jnp
        import numpy as np
        B, P, D, D_MLP, E, K = (2, 512, 256, 1024, 8, 2)
        gate_logits = jnp.einsum('bpd,de->bpe', x, W_gate)
        top_w, top_idx = jax.lax.top_k(gate_logits, K)
        top_w = jax.nn.softmax(top_w, axis=-1)
        combine = jnp.einsum('bpke,bpk->bpe', jax.nn.one_hot(top_idx, E, dtype=x.dtype), top_w)
        out = jnp.zeros_like(x)
        for e in range(E):
            h = jax.nn.gelu(jnp.einsum('bpd,dm->bpm', x, W_in[e]) + b_in[e], approximate=False)
            y = jnp.einsum('bpm,md->bpd', h, W_out[e]) + b_out[e]
            out = out + combine[..., e, None] * y
        return out

    def _L1_attn_ref(inputs_embeds, Wqkv, bqkv, Wproj, bproj):
        import jax, jax.numpy as jnp
        import numpy as np
        N_LAYER = 12
        N_HEAD = 16
        N_EMBD = 256
        B, T, C = inputs_embeds.shape
        H = N_HEAD
        D = C // H
        scale = 1.0 / np.sqrt(D).astype(np.float32)
        x = inputs_embeds
        for i in range(N_LAYER):
            qkv = x @ Wqkv[i].T + bqkv[i]
            q, k, v = jnp.split(qkv, 3, axis=-1)
            q = q.reshape(B, T, H, D).transpose(0, 2, 1, 3)
            k = k.reshape(B, T, H, D).transpose(0, 2, 1, 3)
            v = v.reshape(B, T, H, D).transpose(0, 2, 1, 3)
            att = jnp.einsum('bhqd,bhkd->bhqk', q, k) * scale
            y = jnp.einsum('bhqk,bhkd->bhqd', att, v)
            y = y.transpose(0, 2, 1, 3).reshape(B, T, C)
            x = y @ Wproj[i].T + bproj[i] + x
        return x

    def _L1_ffn_ref(x, base_w, base_b, lora_A, lora_B, router_w, router_b):
        import jax, jax.numpy as jnp
        import numpy as np
        B, S, IN, OUT, E, R = (8, 1024, 256, 256, 8, 8)
        LORA_ALPHA = 16
        SCALING = LORA_ALPHA / R
        result = jnp.einsum('bsd,od->bso', x, base_w) + base_b
        logits = jnp.einsum('bsd,ed->bse', x, router_w) + router_b
        gating = jax.nn.softmax(logits, axis=-1).astype(jnp.bfloat16)
        mid = jnp.einsum('bsd,dr->bsr', x, lora_A)
        lora_out = jnp.einsum('bsr,erd,bse->bsd', mid, lora_B, gating.astype(jnp.float32))
        return result + lora_out * SCALING
    h = _L0_tok_ref(x, L0_tok_W, L0_tok_b)
    h = h + _L0_attn_ref(_layernorm(h, axis=-1), L0_attn_norm_w, L0_attn_norm_b, L0_attn_qkv_w, L0_attn_qkv_b, L0_attn_proj_w, L0_attn_proj_b)
    h = h + _L0_ffn_ref(_layernorm(h, axis=-1), L0_ffn_W_gate, L0_ffn_W_in, L0_ffn_b_in, L0_ffn_W_out, L0_ffn_b_out)
    h = h + _L1_attn_ref(_layernorm(h, axis=-1), L1_attn_Wqkv, L1_attn_bqkv, L1_attn_Wproj, L1_attn_bproj)
    h = h + _L1_ffn_ref(_layernorm(h, axis=-1), L1_ffn_base_w, L1_ffn_base_b, L1_ffn_lora_A, L1_ffn_lora_B, L1_ffn_router_w, L1_ffn_router_b)
    return h

_drawn_inputs = setup_inputs


def setup_inputs(seed=0):
    import zlib

    import numpy as np

    out = dict(_drawn_inputs(seed))
    spreads = {'L0_attn_norm_w': (1.0, 0.2),
     'L0_attn_norm_b': (0.0, 0.1),
     'L0_attn_qkv_b': (0.0, 0.1),
     'L0_attn_proj_b': (0.0, 0.1),
     'L0_ffn_b_in': (0.0, 0.281),
     'L0_ffn_b_out': (0.0, 0.1),
     'L1_attn_bqkv': (0.0, 0.8),
     'L1_attn_bproj': (0.0, 0.1),
     'L1_ffn_base_b': (0.0, 0.289),
     'L1_ffn_router_b': (0.0, 0.8)}
    factors = {'L1_attn_Wqkv': 8.0,
     'L1_attn_Wproj': 8.0,
     'L1_ffn_lora_A': 8.0,
     'L1_ffn_lora_B': 8.0,
     'L1_ffn_router_w': 8.0}
    for name, (base, spread) in spreads.items():
        noise = np.random.default_rng([zlib.crc32(name.encode()), seed]).standard_normal(out[name].shape)
        drawn = base * np.exp(spread * noise) if base else spread * noise
        out[name] = jnp.asarray(drawn.astype(out[name].dtype))
    for name, factor in factors.items():
        out[name] = (out[name] * factor).astype(out[name].dtype)
    return out
```

```python
from contextlib import ExitStack

import numpy as np

import concourse.bass as bass
from concourse import mybir

F32 = mybir.dt.float32
F16 = mybir.dt.float16
I32 = mybir.dt.int32
ACT = mybir.ActivationFunctionType
ALU = mybir.AluOpType
AX = mybir.AxisListType

P = 128
IMAGES, SIDE, PATCH, CHANS = 64, 7, 16, 3
TOK = SIDE * SIDE
N = IMAGES * TOK
TILES = -(-N // P)
NPAD = TILES * P
FEAT = CHANS * PATCH * PATCH
FC = FEAT // P
D = 256
DC = D // P
PAIRS = IMAGES // 2
PT = 2 * TOK
EPS = 1e-5
WS = 256.0
HI, LO = 0, 1
EXPERTS, TOP, HIDDEN = 8, 2, 1024
MC = HIDDEN // P
ROWS = 2 * P
LEAST_TILES = 2
EXPERT_TILES = (TOP * N + EXPERTS * LEAST_TILES * ROWS) // ROWS
MOST_OF_ONE = -(-N // ROWS)
QUEUE_TILES = EXPERT_TILES + MOST_OF_ONE + 1
SURE_TILES = TOP * N // ROWS
ZERO_ROWS = 4
ZERO_PART = P * ZERO_ROWS


def in_loop(eng, first, last, step):
    if first < last and first % 2:
        step(first, 1)
        first += 1
    rounds = (last - first) // 2
    if rounds >= 2:
        with eng.Fori(0, rounds) as j:
            step(first + 2 * j, 0)
            step(first + 2 * j + 1, 1)
        first += 2 * rounds
    for i in range(first, last):
        step(i, i % 2)


def skewed(eng, n, *stages):
    deepest = max(lag for lag, _ in stages)

    def step(i, parity):
        for lag, f in stages:
            if not isinstance(i, int) or 0 <= i - lag < n:
                f(i - lag, (parity - lag) % 2)

    peeled = deepest + SLOTS
    for i in range(peeled):
        step(i, i % 2)
    in_loop(eng, peeled, n, step)
    for i in range(n, n + deepest):
        step(i, i % 2)


def wait_apart(eng, sem, value, passed):
    eng.wait_ge(sem, value)
    eng.sem_inc(passed, 1)


SLOTS = 2


def free(i):
    return i + 1


def made(i):
    return i + 1 + SLOTS


def landed(i, parity):
    return 8 * i + 16 - 8 * parity


def split_matmuls(pe, out, left, right, chunks, first_start=True, check=True):
    terms = [(c, a, b) for c in range(chunks) for a, b in ((HI, HI), (HI, LO), (LO, HI))]
    for n, (c, a, b) in enumerate(terms):
        mm = pe.matmul(out, left(a, c), right(b, c), start=first_start and n == 0, stop=n == len(terms) - 1,
                       skip_group_check=not check)
    return mm


def embed_and_norm(nc, d, keep):
    residual, normed_t = keep["residual"], keep["chan_a"]
    with ExitStack() as ctx:
        def sb(name, shape, dt=F32):
            return ctx.enter_context(nc.sbuf_tensor(name, shape, dt))

        def sem(name):
            return ctx.enter_context(nc.semaphore(name))

        patches = sb("patches", [P, 2, FC, P])
        patches_pair = sb("patches_pair", [P, 2, 2, FC, P], F16)
        w_raw = sb("tok_w_raw", [P, FC, D])
        w_pair = sb("tok_w_pair", [P, 2, FC, D], F16)
        tok_b = sb("tok_b_all", [P, D])
        norm_w = sb("norm_w_all", [P, D])
        norm_b = sb("norm_b_all", [P, D])
        ident = sb("ident_a", [P, P])
        eps = sb("eps_a", [P, 1])
        stats = sb("stats", [P, 2, 6])
        mean_var = sb("mean_var", [P, 2, 2])
        std = sb("std", [P, 2])
        rstd = sb("rstd", [P, 2])
        x0 = sb("x0", [P, 2, D])
        stats2 = sb("stats2", [P, 2, 6])
        mean_var2 = sb("mean_var2", [P, 2, 2])
        std2 = sb("std2", [P, 2])
        rstd2 = sb("rstd2", [P, 2])
        n0 = sb("n0", [P, 2, D])
        n1 = sb("n1", [P, 2, D])
        ps_embed = ctx.enter_context(nc.psum_tensor("ps_embed", [P, 2, 512], F32))
        ps_t = ctx.enter_context(nc.psum_tensor("ps_normed_t", [P, 2, 512], F32))

        consts_loaded, w_loaded = sem("consts_loaded"), sem("w_loaded")
        patches_loaded = [sem("patches_loaded0"), sem("patches_loaded1")]
        w_hi, w_split, ident_made = sem("w_hi"), sem("w_split"), sem("ident_made")
        patches_hi, patches_split = sem("patches_hi"), sem("patches_split")
        embedded, h_made, h_stats = sem("embedded"), sem("h_made"), sem("h_stats")
        std_made, rstd_made, x0_made, x0_stats = sem("std_made"), sem("rstd_made"), sem("x0_made"), sem("x0_stats")
        residual_made, std2_made, n_steps = sem("residual_made"), sem("std2_made"), sem("n_steps")
        transposed, t_hi, t_split, passed = sem("transposed"), sem("t_hi"), sem("t_split"), sem("a_passed")
        block = ctx.enter_context(nc.Block())

        @block.sync
        def _(sp):
            sp.dma_start(w_raw[:, :, :], d["tok_w"]).then_inc(w_loaded, 16)

            def load(t, s):
                sp.wait_ge(patches_split, free(t))
                sp.dma_start(patches[:, s:s + 1, :, :].rearrange("p a c t -> p (a c t)"),
                             d["patches"][bass.ds(t, 1)].rearrange("a p n -> (a p) n")).then_inc(patches_loaded[s], 16)

            in_loop(sp, 0, TILES, load)

        @block.scalar
        def _(act):
            act.dma_start(tok_b[:, :], d["tok_b"].partition_broadcast(P)).then_inc(consts_loaded, 16)
            act.dma_start(norm_w[:, :], d["norm_w"].partition_broadcast(P)).then_inc(consts_loaded, 16)
            act.dma_start(norm_b[:, :], d["norm_b"].partition_broadcast(P)).then_inc(consts_loaded, 16)
            act.wait_ge(w_loaded, 16)
            act.activation(w_pair[:, HI, :, :], w_raw[:, :, :], ACT.Copy, scale=WS).then_inc(w_hi, 1)

            def hi(t, s):
                act.wait_ge(patches_loaded[s], landed(t, s))
                act.wait_ge(embedded, free(t))
                act.activation(patches_pair[:, s, HI, :, :], patches[:, s, :, :], ACT.Copy).then_inc(patches_hi, 1)

            def root(t, s):
                act.wait_ge(h_stats, 2 * t + 2)
                act.activation(std[:, s:s + 1], mean_var[:, s, 1:2], ACT.Sqrt, bias=eps[:, 0:1]).then_inc(std_made, 1)

            def root2(t, s):
                act.wait_ge(x0_stats, 2 * t + 2)
                act.activation(std2[:, s:s + 1], mean_var2[:, s, 1:2], ACT.Sqrt, bias=eps[:, 0:1]).then_inc(std2_made, 1)

            def out_hi(t, s):
                act.wait_ge(transposed, made(t))
                act.activation(normed_t[:, HI, :, bass.ds(t * P, P)],
                               ps_t[:, s, 0:D].rearrange("p (c t) -> p c t", c=DC), ACT.Copy).then_inc(t_hi, 1)

            act.wait_ge(ident_made, 3)
            skewed(act, TILES, (0, hi), (1, root), (2, root2), (4, out_hi))

        @block.gpsimd
        def _(pool):
            pool.memset(ident[:, :], 0.0).then_inc(ident_made, 1)
            pool.wait_ge(ident_made, 1)
            pool.affine_select(out=ident[:, :], in_=ident[:, :], compare_op=ALU.not_equal, fill=1.0,
                               base=0, pattern=[[-1, P]], channel_multiplier=1).then_inc(ident_made, 1)
            pool.memset(eps[:, :], EPS).then_inc(ident_made, 1)
            pool.sem_inc(patches_split, SLOTS)

            def lo(t, s):
                pool.wait_ge(patches_hi, t + 1)
                pool.tensor_tensor(patches_pair[:, s, LO, :, :], patches[:, s, :, :], patches_pair[:, s, HI, :, :],
                                   ALU.subtract).then_inc(patches_split, 1)

            def add_x0(t, s):
                pool.wait_ge(x0_made, t + 1)
                row = residual[:, bass.ds(t, 1), :]
                pool.tensor_tensor(row, row, x0[:, s:s + 1, :], ALU.add).then_inc(residual_made, 1)

            skewed(pool, TILES, (0, lo), (2, add_x0))

        @block.vector
        def _(dve):
            dve.sem_inc(h_made, SLOTS)
            dve.sem_inc(t_split, SLOTS)
            dve.wait_ge(w_hi, 1)
            dve.scalar_tensor_tensor(w_pair[:, LO, :, :].rearrange("p c n -> p (c n)"), w_raw[:, :, :].rearrange("p c n -> p (c n)"), WS,
                                     w_pair[:, HI, :, :].rearrange("p c n -> p (c n)"), ALU.mult, ALU.subtract).then_inc(w_split, 1)
            dve.wait_ge(consts_loaded, 48)

            def h_and_stats(t, s):
                dve.wait_ge(embedded, made(t))
                dve.scalar_tensor_tensor(residual[:, bass.ds(t, 1), :], ps_embed[:, s:s + 1, 0:D], 1.0 / WS, tok_b[:, None, :],
                                         ALU.mult, ALU.add).then_inc(h_made, 1)
                wait_apart(dve, h_made, made(t), passed)
                dve.bn_stats(stats[:, s, :], residual[:, bass.ds(t, 1), :]).then_inc(h_stats, 1)
                wait_apart(dve, h_stats, 2 * t + 1, passed)
                dve.bn_aggr(mean_var[:, s, :], stats[:, s, :]).then_inc(h_stats, 1)

            def norm_and_stats(t, s):
                dve.wait_ge(std_made, t + 1)
                dve.reciprocal(rstd[:, s:s + 1], std[:, s:s + 1]).then_inc(rstd_made, 1)
                dve.wait_ge(rstd_made, t + 1)
                if not isinstance(t, int) or t >= 2:
                    dve.wait_ge(residual_made, t - 1)
                dve.tensor_scalar(x0[:, s:s + 1, :], residual[:, bass.ds(t, 1), :], mean_var[:, s, 0:1], rstd[:, s:s + 1],
                                  ALU.subtract, ALU.mult).then_inc(x0_made, 1)
                wait_apart(dve, x0_made, t + 1, passed)
                dve.bn_stats(stats2[:, s, :], x0[:, s, :]).then_inc(x0_stats, 1)
                wait_apart(dve, x0_stats, 2 * t + 1, passed)
                dve.bn_aggr(mean_var2[:, s, :], stats2[:, s, :]).then_inc(x0_stats, 1)

            def norm2(t, s):
                dve.wait_ge(std2_made, t + 1)
                dve.reciprocal(rstd2[:, s:s + 1], std2[:, s:s + 1]).then_inc(n_steps, 1)
                dve.wait_ge(n_steps, 4 * t + 1)
                dve.tensor_scalar(n0[:, s, :], x0[:, s, :], mean_var2[:, s, 0:1], rstd2[:, s:s + 1],
                                  ALU.subtract, ALU.mult).then_inc(n_steps, 1)
                dve.wait_ge(n_steps, 4 * t + 2)
                dve.tensor_tensor(n0[:, s, :], n0[:, s, :], norm_w[:, :], ALU.mult).then_inc(n_steps, 1)
                dve.wait_ge(n_steps, 4 * t + 3)
                dve.wait_ge(transposed, free(t))
                dve.tensor_tensor(n1[:, s, :], n0[:, s, :], norm_b[:, :], ALU.add).then_inc(n_steps, 1)

            def out_lo(t, s):
                dve.wait_ge(t_hi, t + 1)
                dve.tensor_tensor(normed_t[:, LO, :, bass.ds(t * P, P)],
                                  ps_t[:, s, 0:D].rearrange("p (c t) -> p c t", c=DC),
                                  normed_t[:, HI, :, bass.ds(t * P, P)], ALU.subtract).then_inc(t_split, 1)

            skewed(dve, TILES, (0, h_and_stats), (1, norm_and_stats), (2, norm2), (4, out_lo))

        @block.tensor
        def _(pe):
            pe.sem_inc(embedded, SLOTS)
            pe.sem_inc(transposed, SLOTS)
            pe.wait_ge(w_split, 1)
            pe.wait_ge(ident_made, 2)

            def embed(t, s):
                pe.wait_ge(patches_split, made(t))
                pe.wait_ge(h_made, free(t))
                split_matmuls(pe, ps_embed[:, s, 0:D], lambda a, c: patches_pair[:, s, a, c, :],
                              lambda b, c: w_pair[:, b, c, :], FC).then_inc(embedded, 1)

            def turn(t, s):
                pe.wait_ge(n_steps, 4 * t + 4)
                pe.wait_ge(t_split, free(t))
                for c in range(DC):
                    mm = pe.transpose(ps_t[:, s, c * P:(c + 1) * P], n1[:, s, c * P:(c + 1) * P], ident[:, :])
                mm.then_inc(transposed, 1)

            skewed(pe, TILES, (0, embed), (3, turn))


def channel_attention(nc, d, keep):
    normed_t, attended_t = keep["chan_a"], keep["chan_b"]
    scale = 1.0 / float(np.sqrt(TOK))
    with ExitStack() as ctx:
        def sb(name, shape, dt=F32):
            return ctx.enter_context(nc.sbuf_tensor(name, shape, dt))

        def psum(name, shape, dt=F32):
            return ctx.enter_context(nc.psum_tensor(name, shape, dt))

        def sem(name):
            return ctx.enter_context(nc.semaphore(name))

        w_raw = sb("qkv_w_raw", [P, DC, 3 * D])
        w_pair = sb("qkv_w_pair", [P, 2, DC, 3 * D], F16)
        bias_raw = sb("qk_b_raw", [33, 2 * D])
        bias_hi = sb("qk_b_hi", [33, 2 * D], F16)
        bias_rows = sb("qk_bias_rows", [P, 2 * D], F16)
        ones = sb("ones_b", [P, P], F16)
        v_b = sb("v_b", [P, 6])
        v_bs = sb("v_b_scaled", [P, DC])
        ident = sb("ident_b", [P, P])
        own = sb("own_image", [PT, 2])
        q_pair = sb("q_pair", [PT, 2, 2, 2, D], F16)
        k_pair = sb("k_pair", [PT, 2, 2, D], F16)
        v_pair = sb("v_pair", [P, 2, 2, DC, PT], F16)
        neg_max = sb("neg_max", [P, 2, DC])
        neg_scaled = sb("neg_scaled", [P, 2, DC])
        exps = sb("exps", [P, 2, DC, D])
        sums = sb("sums", [P, 2, DC])
        sums_s = sb("sums_scaled", [P, 2, DC])
        inv = sb("inv_sums", [P, 2, DC])
        et_pair = sb("exps_t_pair", [P, 2, 2, DC, D], F16)
        zeros = sb("zeros", [P, ZERO_ROWS * D])
        queue_rows, answer_rows = [keep[name].rearrange("(g p r) n -> g p (r n)", p=P, r=ZERO_ROWS) for name in ("queue", "answers")]
        zeros_made, cleared = sem("zeros_made"), sem("queue_cleared")
        ps_qk = psum("ps_qk", [P, 512])
        ps_v = psum("ps_v", [P, 512])
        ps_s = psum("ps_scores", [P, 2, DC, D])
        ps_e = psum("ps_exps_t", [P, 2, DC, D])
        ps_a = psum("ps_attended", [P, 2, 512])

        loaded, prep = sem("qkv_loaded"), sem("qkv_prep")
        w_hi, prep_v, prep_g = sem("qkv_w_hi"), sem("qkv_prep_v"), sem("qkv_prep_g")
        projected_qk, projected_v = sem("projected_qk"), sem("projected_v")
        qk_hi, qk_split, v_hi, v_split = sem("qk_hi"), sem("qk_split"), sem("v_hi"), sem("v_split")
        scored, max_steps, exp_steps = sem("scored"), sem("max_steps"), sem("exp_steps")
        turned, et_hi, et_split = sem("turned"), sem("et_hi"), sem("et_split")
        inv_steps, attended, a_hi, a_split = sem("inv_steps"), sem("attended"), sem("a_hi"), sem("a_split")
        block = ctx.enter_context(nc.Block())

        @block.sync
        def _(sp):
            sp.dma_start(w_raw[:, :, :], d["qkv0_w"]).then_inc(loaded, 16)
            sp.dma_start(bias_raw[0:1, :], d["qkv0_b"][:, 0:2 * D]).then_inc(loaded, 16)
            sp.dma_start(bias_raw[32:33, :], d["qkv0_b"][:, 0:2 * D]).then_inc(loaded, 16)
            sp.dma_start(v_b[:, :], d["qkv0_bcol"]).then_inc(loaded, 16)
            sp.wait_ge(zeros_made, 1)
            parts = 0
            for rows, first, last in ((queue_rows, 0, EXPERT_TILES + 1), (answer_rows, SURE_TILES, EXPERT_TILES)):
                for g in range(first * ROWS // ZERO_PART, -(-last * ROWS // ZERO_PART)):
                    sp.dma_start(rows[g], zeros[:, :]).then_inc(cleared, 16)
                    parts += 1
            sp.wait_ge(cleared, 16 * parts)

        @block.gpsimd
        def _(pool):
            pool.memset(ident[:, :], 0.0).then_inc(prep_g, 1)
            pool.memset(zeros[:, :], 0.0).then_inc(zeros_made, 1)
            pool.memset(own[:, :], 1.0 / WS).then_inc(prep_g, 1)
            pool.memset(ones[:, :], 1.0).then_inc(prep_g, 1)
            pool.wait_ge(prep_g, 2)
            pool.affine_select(out=ident[:, :], in_=ident[:, :], compare_op=ALU.not_equal, fill=1.0,
                               base=0, pattern=[[-1, P]], channel_multiplier=1).then_inc(prep_g, 1)
            pool.affine_select(out=own[:, 0:1], in_=own[:, 0:1], compare_op=ALU.is_ge, fill=0.0,
                               base=TOK - 1, pattern=[[0, 1]], channel_multiplier=-1).then_inc(prep_g, 1)
            pool.affine_select(out=own[:, 1:2], in_=own[:, 1:2], compare_op=ALU.is_ge, fill=0.0,
                               base=-TOK, pattern=[[0, 1]], channel_multiplier=1).then_inc(prep_g, 1)

        @block.scalar
        def _(act):
            act.wait_ge(loaded, 64)
            act.activation(w_pair[:, HI, :, :], w_raw[:, :, :], ACT.Copy, scale=WS).then_inc(w_hi, 1)
            act.wait_ge(prep_v, 1)
            act.activation(bias_rows[0:1, :], bias_raw[0:1, :], ACT.Copy, scale=WS).then_inc(w_hi, 1)
            act.activation(bias_hi[32:33, :], bias_raw[32:33, :], ACT.Copy, scale=WS).then_inc(w_hi, 1)
            act.activation(v_bs[:, :], v_b[:, 4:6], ACT.Copy, scale=WS).then_inc(w_hi, 1)
            act.wait_ge(w_hi, 4)
            act.wait_ge(prep_g, 6)

            def project_hi(p, s):
                act.wait_ge(projected_qk, p + 1)
                if not isinstance(p, int) or p >= 2:
                    act.wait_ge(scored, 2 * p - 2)
                for image in (0, 1):
                    act.activation(q_pair[:, s, HI, image, :], ps_qk[0:PT, 0:D], ACT.Copy, scale=own[:, image:image + 1])
                act.activation(k_pair[:, s, HI, :], ps_qk[0:PT, D:2 * D], ACT.Copy, scale=1.0 / WS).then_inc(qk_hi, 1)
                act.wait_ge(projected_v, p + 1)
                if not isinstance(p, int) or p >= 2:
                    act.wait_ge(attended, 2 * p - 2)
                for c in range(DC):
                    out = act.activation(v_pair[:, s, HI, c, :], ps_v[:, c * PT:(c + 1) * PT], ACT.Identity, bias=v_bs[:, c:c + 1])
                out.then_inc(v_hi, 1)

            def exp(n, s):
                act.wait_ge(max_steps, 2 * n + 2)
                if not isinstance(n, int) or n >= 2:
                    act.wait_ge(turned, n - 1)
                for c in range(DC):
                    act.activation(exps[:, s, c, :], ps_s[:, s, c, :], ACT.Exp, bias=neg_scaled[:, s, c:c + 1], scale=scale,
                                   accum_out=sums[:, s, c:c + 1]).then_inc(exp_steps, 1)

            def turned_hi(n, s):
                act.wait_ge(turned, n + 1)
                if not isinstance(n, int) or n >= 2:
                    act.wait_ge(attended, n - 1)
                act.activation(et_pair[:, s, HI, :, :], ps_e[:, s, :, :], ACT.Copy).then_inc(et_hi, 1)

            def attended_hi(n, s):
                act.wait_ge(attended, n + 1)
                act.wait_ge(inv_steps, 2 * n + 2)
                for c in range(DC):
                    out = act.activation(attended_t[:, HI, c, bass.ds(n * TOK, TOK)], ps_a[:, s, c * TOK:(c + 1) * TOK], ACT.Copy,
                                         scale=inv[:, s, c:c + 1])
                out.then_inc(a_hi, 1)

            def round_(p, s):
                exp(2 * p, 0)
                if not (isinstance(p, int) and p == PAIRS - 1):
                    project_hi(p + 1, 1 - s)
                turned_hi(2 * p, 0)
                exp(2 * p + 1, 1)
                if not (isinstance(p, int) and p == 0):
                    attended_hi(2 * p - 1, 1)
                turned_hi(2 * p + 1, 1)
                attended_hi(2 * p, 0)

            project_hi(0, 0)
            round_(0, 0)
            in_loop(act, 1, PAIRS - 1, round_)
            round_(PAIRS - 1, (PAIRS - 1) % 2)
            attended_hi(IMAGES - 1, 1)

        @block.vector
        def _(dve):
            dve.memset(bias_rows[:, :], 0.0).then_inc(prep_v, 1)
            dve.wait_ge(w_hi, 4)
            dve.wait_ge(loaded, 64)
            dve.scalar_tensor_tensor(w_pair[:, LO, :, :].rearrange("p c n -> p (c n)"), w_raw[:, :, :].rearrange("p c n -> p (c n)"), WS,
                                     w_pair[:, HI, :, :].rearrange("p c n -> p (c n)"), ALU.mult, ALU.subtract).then_inc(prep_v, 1)
            dve.wait_ge(prep_v, 1)
            dve.scalar_tensor_tensor(bias_rows[32:33, :], bias_raw[32:33, :], WS, bias_hi[32:33, :],
                                     ALU.mult, ALU.subtract).then_inc(prep_v, 1)
            dve.wait_ge(prep_g, 6)

            def project_lo(p, s):
                dve.wait_ge(qk_hi, p + 1)
                for image in (0, 1):
                    dve.scalar_tensor_tensor(q_pair[:, s, LO, image, :], ps_qk[0:PT, 0:D], own[:, image:image + 1],
                                             q_pair[:, s, HI, image, :], ALU.mult, ALU.subtract)
                dve.scalar_tensor_tensor(k_pair[:, s, LO, :], ps_qk[0:PT, D:2 * D], 1.0 / WS, k_pair[:, s, HI, :],
                                         ALU.mult, ALU.subtract).then_inc(qk_split, 1)
                dve.wait_ge(v_hi, p + 1)
                for c in range(DC):
                    out = dve.scalar_tensor_tensor(v_pair[:, s, LO, c, :], ps_v[:, c * PT:(c + 1) * PT], v_bs[:, c:c + 1],
                                                   v_pair[:, s, HI, c, :], ALU.add, ALU.subtract)
                out.then_inc(v_split, 1)

            def row_max(n, s):
                dve.wait_ge(scored, n + 1)
                if not isinstance(n, int) or n >= 2:
                    dve.wait_ge(exp_steps, 2 * n - 2)
                dve.tensor_reduce(neg_max[:, s, :], ps_s[:, s, :, :], AX.X, ALU.max).then_inc(max_steps, 1)
                dve.wait_ge(max_steps, 2 * n + 1)
                dve.tensor_scalar(neg_scaled[:, s, :], neg_max[:, s, :], -scale, None, ALU.mult).then_inc(max_steps, 1)

            def turned_lo(n, s):
                dve.wait_ge(et_hi, n + 1)
                dve.tensor_tensor(et_pair[:, s, LO, :, :], ps_e[:, s, :, :], et_pair[:, s, HI, :, :],
                                  ALU.subtract).then_inc(et_split, 1)

            def inverse(n, s):
                dve.wait_ge(exp_steps, 2 * n + 2)
                if not isinstance(n, int) or n >= 2:
                    dve.wait_ge(a_hi, n - 1)
                dve.tensor_scalar(sums_s[:, s, :], sums[:, s, :], WS, None, ALU.mult).then_inc(inv_steps, 1)
                dve.wait_ge(inv_steps, 2 * n + 1)
                dve.reciprocal(inv[:, s, :], sums_s[:, s, :]).then_inc(inv_steps, 1)

            def attended_lo(n, s):
                dve.wait_ge(a_hi, n + 1)
                for c in range(DC):
                    out = dve.scalar_tensor_tensor(attended_t[:, LO, c, bass.ds(n * TOK, TOK)], ps_a[:, s, c * TOK:(c + 1) * TOK],
                                                   inv[:, s, c:c + 1], attended_t[:, HI, c, bass.ds(n * TOK, TOK)],
                                                   ALU.mult, ALU.subtract)
                out.then_inc(a_split, 1)

            def round_(p, s):
                if not (isinstance(p, int) and p == PAIRS - 1):
                    project_lo(p + 1, 1 - s)
                row_max(2 * p + 1, 1)
                inverse(2 * p, 0)
                turned_lo(2 * p, 0)
                if not (isinstance(p, int) and p == 0):
                    attended_lo(2 * p - 1, 1)
                if not (isinstance(p, int) and p == PAIRS - 1):
                    row_max(2 * p + 2, 0)
                inverse(2 * p + 1, 1)
                turned_lo(2 * p + 1, 1)
                attended_lo(2 * p, 0)

            project_lo(0, 0)
            row_max(0, 0)
            round_(0, 0)
            in_loop(dve, 1, PAIRS - 1, round_)
            round_(PAIRS - 1, (PAIRS - 1) % 2)
            attended_lo(IMAGES - 1, 1)

        @block.tensor
        def _(pe):
            pe.wait_ge(prep_v, 3)
            pe.wait_ge(prep_g, 6)

            def project(p, s):
                if not (isinstance(p, int) and p == 0):
                    pe.wait_ge(qk_split, p)
                    pe.wait_ge(v_split, p)
                first = True
                for c in range(DC):
                    for a in (HI, LO):
                        x = normed_t[:, a, c, bass.ds(p * PT, PT)]
                        for b in ((HI, LO) if a == HI else (HI,)):
                            pe.matmul(ps_qk[0:PT, :], x, w_pair[:, b, c, 0:2 * D], start=first, stop=False)
                            for m in range(DC):
                                v = pe.matmul(ps_v[:, m * PT:(m + 1) * PT], w_pair[:, b, c, 2 * D + m * P:2 * D + (m + 1) * P], x,
                                              start=first and m == 0, stop=(c == DC - 1 and a == LO), skip_group_check=True)
                            first = False
                v.then_inc(projected_v, 1)
                pe.matmul(ps_qk[0:PT, :], ones[:, 0:PT], bias_rows[:, :], start=False, stop=True).then_inc(projected_qk, 1)

            def score(p, image, pair_slot):
                n, s = 2 * p + image, image
                if image == 0:
                    pe.wait_ge(qk_split, p + 1)
                if not isinstance(n, int) or n >= 2:
                    pe.wait_ge(exp_steps, 2 * n - 2)
                for m in range(DC):
                    mm = split_matmuls(pe, ps_s[:, s, m, :], lambda a, c: q_pair[:, pair_slot, a, image, m * P:(m + 1) * P],
                                       lambda b, c: k_pair[:, pair_slot, b, :], 1, first_start=(m == 0), check=False)
                mm.then_inc(scored, 1)

            def turn(n, s):
                pe.wait_ge(exp_steps, 2 * n + 2)
                if not isinstance(n, int) or n >= 2:
                    pe.wait_ge(et_split, n - 1)
                for c in range(DC):
                    for m in range(DC):
                        mm = pe.transpose(ps_e[:, s, c, m * P:(m + 1) * P], exps[:, s, m, c * P:(c + 1) * P], ident[:, :])
                mm.then_inc(turned, 1)

            def attend(p, image, pair_slot):
                n, s = 2 * p + image, image
                pe.wait_ge(et_split, n + 1)
                if image == 0:
                    pe.wait_ge(v_split, p + 1)
                if not isinstance(n, int) or n >= 2:
                    pe.wait_ge(a_split, n - 1)
                for m in range(DC):
                    mm = split_matmuls(pe, ps_a[:, s, m * TOK:(m + 1) * TOK],
                                       lambda a, c: et_pair[:, s, a, c, m * P:(m + 1) * P],
                                       lambda b, c: v_pair[:, pair_slot, b, c, image * TOK:(image + 1) * TOK], DC,
                                       first_start=(m == 0), check=False)
                mm.then_inc(attended, 1)

            def round_(p, s):
                dyn = not isinstance(p, int)
                last = not dyn and p == PAIRS - 1
                if not last:
                    project(p + 1, 1 - s)
                score(p, 1, s)
                turn(2 * p, 0)
                if dyn or p > 0:
                    attend(p - 1, 1, 1 - s)
                if not last:
                    score(p + 1, 0, 1 - s)
                turn(2 * p + 1, 1)
                attend(p, 0, s)

            project(0, 0)
            score(0, 0, 0)
            round_(0, 0)
            in_loop(pe, 1, PAIRS - 1, round_)
            round_(PAIRS - 1, (PAIRS - 1) % 2)
            attend(PAIRS - 1, 1, (PAIRS - 1) % 2)



def project_and_route(nc, d, keep):
    residual, attended_t, x1 = keep["residual"], keep["chan_b"], keep["rows"]
    weights, places, bounds, queue = keep["weights"], keep["places"], keep["bounds"], keep["queue"]
    with ExitStack() as ctx:
        def sb(name, shape, dt=F32):
            return ctx.enter_context(nc.sbuf_tensor(name, shape, dt))

        def psum(name, shape, dt=F32):
            return ctx.enter_context(nc.psum_tensor(name, shape, dt))

        def sem(name):
            return ctx.enter_context(nc.semaphore(name))

        w_raw = sb("proj_w_raw", [P, DC, D])
        w_pair = sb("proj_w_pair", [P, 2, DC, D], F16)
        g_raw = sb("gate_w_raw", [P, DC, EXPERTS])
        g_pair = sb("gate_w_pair", [P, 2, DC, EXPERTS], F16)
        bias_raw = sb("proj_b_raw", [33, D])
        bias_hi = sb("proj_b_hi", [33, D], F16)
        bias_rows = sb("proj_bias_rows", [P, D], F16)
        ones = sb("ones_c", [P, P], F16)
        before = sb("before", [P, P], F16)
        ident = sb("ident_c", [P, P])
        eps = sb("eps_c", [P, 1])
        stats = sb("stats_c", [P, 2, 6])
        mean_var = sb("mean_var_c", [P, 2, 2])
        std = sb("std_c", [P, 2])
        rstd = sb("rstd_c", [P, 2])
        x1_tile = sb("x1_tile", [P, 2, D])
        xt_pair = sb("x1_t_pair", [P, 2, 2, DC, P], F16)
        logits = sb("logits", [P, 2, EXPERTS])
        best = sb("best", [P, 2, 8])
        best_at = sb("best_at", [P, 2, 8], mybir.dt.uint32)
        best_two = sb("best_two", [P, TOP, TILES])
        names_i = sb("expert_names_i", [P, EXPERTS], I32)
        names = sb("expert_names", [P, EXPERTS])
        limits_i = sb("tile_limits_i", [P, MOST_OF_ONE], I32)
        limits = sb("tile_limits", [P, MOST_OF_ONE])
        at_f = sb("best_at_f", [P, TOP, TILES])
        is_best = sb("is_best", [P, TOP, TILES, EXPERTS])
        chosen = sb("chosen", [P, TILES, EXPERTS], F16)
        diff = sb("logit_difference", [P, TILES])
        ratio = sb("exp_difference", [P, TILES])
        total = sb("exp_total", [P, TILES])
        over = sb("over_limit", [P, EXPERTS, MOST_OF_ONE])
        tiles_f = sb("tiles_of_expert", [P, EXPERTS])
        start_f = sb("first_tile_of_expert", [P, EXPERTS])
        place = sb("place", [P, TILES, EXPERTS])
        place_of = sb("place_of_choice", [P, TILES, EXPERTS])
        place_f = sb("place_f", [P, TOP, TILES])
        ps_p = psum("ps_proj", [P, 2, 512])
        ps_t = psum("ps_x1_t", [P, 2, 512])
        ps_g = psum("ps_gate", [P, 2, 512])
        ps_rank = psum("ps_rank", [P, 512])
        ps_r = ps_rank[:, 0:(TILES + 1) * EXPERTS].rearrange("p (t e) -> p t e", e=EXPERTS)

        loaded, cleared, prep_a, prep_v, prep_g = sem("c_loaded"), sem("c_cleared"), sem("c_prep_a"), sem("c_prep_v"), sem("c_prep_g")
        projected, h_steps, std_made, rstd_made, x1_made = sem("c_projected"), sem("c_h_steps"), sem("c_std"), sem("c_rstd"), sem("x1_made")
        x1_kept = sem("x1_kept")
        turned, t_hi, t_split, gated, picked = sem("c_turned"), sem("c_t_hi"), sem("c_t_split"), sem("gated"), sem("picked")
        passed = sem("c_passed")
        chain, ratio_made, ranked, scattered = sem("route_chain"), sem("ratio_made"), sem("ranked"), sem("scattered")
        CHOSEN = 4 + (N % P > 0)
        ROUTED = CHOSEN + 11 + EXPERTS + 3 * TOP
        block = ctx.enter_context(nc.Block())

        @block.sync
        def _(sp):
            sp.dma_start(w_raw[:, :, :], d["proj0_w"]).then_inc(loaded, 16)
            sp.dma_start(g_raw[:, :, :], d["gate_w"]).then_inc(loaded, 16)
            sp.dma_start(bias_raw[0:1, :], d["proj0_b"]).then_inc(loaded, 16)
            sp.dma_start(bias_raw[32:33, :], d["proj0_b"]).then_inc(loaded, 16)

        @block.gpsimd
        def _(pool):
            pool.memset(ident[:, :], 0.0).then_inc(prep_g, 1)
            pool.memset(before[:, :], 1.0).then_inc(prep_g, 1)
            pool.wait_ge(prep_g, 2)
            pool.affine_select(out=ident[:, :], in_=ident[:, :], compare_op=ALU.not_equal, fill=1.0,
                               base=0, pattern=[[-1, P]], channel_multiplier=1).then_inc(prep_g, 1)
            pool.affine_select(out=before[:, :], in_=before[:, :], compare_op=ALU.is_ge, fill=0.0,
                               base=-1, pattern=[[1, P]], channel_multiplier=-1).then_inc(prep_g, 1)
            pool.memset(eps[:, :], EPS).then_inc(prep_g, 1)
            pool.memset(ones[:, :], 1.0).then_inc(prep_g, 1)
            pool.iota(names_i[:, :], [[1, EXPERTS]], base=0, channel_multiplier=0).then_inc(prep_g, 1)
            pool.iota(limits_i[:, :], [[ROWS, MOST_OF_ONE]], base=0, channel_multiplier=0).then_inc(prep_g, 1)
            pool.wait_ge(prep_g, 8)
            pool.tensor_copy(names[:, :], names_i[:, :]).then_inc(prep_g, 1)
            pool.tensor_copy(limits[:, :], limits_i[:, :]).then_inc(prep_g, 1)

            def keep_x1(t, s):
                pool.wait_ge(x1_made, t + 1)
                pool.tensor_copy(x1[:, bass.ds(t, 1), :], x1_tile[:, s:s + 1, :]).then_inc(x1_kept, 1)

            in_loop(pool, 0, TILES, keep_x1)
            pool.wait_ge(chain, ROUTED)
            pool.wait_ge(x1_kept, TILES)
            for k in range(TOP):
                for t in range(TILES):
                    rows = min(P, N - t * P)
                    pool.indirect_dma_start(queue[:, :], bass.IndirectOffsetOnAxis(places[0:rows, k, t:t + 1], 0),
                                            x1[0:rows, t, :], None).then_inc(scattered, 16)
            pool.wait_ge(scattered, 16 * TOP * TILES)

        @block.scalar
        def _(act):
            act.wait_ge(loaded, 64)
            act.activation(w_pair[:, HI, :, :], w_raw[:, :, :], ACT.Copy, scale=WS).then_inc(prep_a, 1)
            act.activation(g_pair[:, HI, :, :], g_raw[:, :, :], ACT.Copy, scale=WS).then_inc(prep_a, 1)
            act.wait_ge(cleared, 2)
            act.activation(bias_rows[0:1, :], bias_raw[0:1, :], ACT.Copy, scale=WS).then_inc(prep_a, 1)
            act.activation(bias_hi[32:33, :], bias_raw[32:33, :], ACT.Copy, scale=WS).then_inc(prep_a, 1)
            act.wait_ge(prep_g, 10)

            def root(t, s):
                act.wait_ge(h_steps, 3 * t + 3)
                act.activation(std[:, s:s + 1], mean_var[:, s, 1:2], ACT.Sqrt, bias=eps[:, 0:1]).then_inc(std_made, 1)

            def t_hi_(t, s):
                act.wait_ge(turned, t + 1)
                act.wait_ge(gated, free(t))
                act.activation(xt_pair[:, s, HI, :, :], ps_t[:, s, 0:D].rearrange("p (c t) -> p c t", c=DC), ACT.Copy).then_inc(t_hi, 1)

            skewed(act, TILES, (0, root), (3, t_hi_))
            act.wait_ge(chain, 1)
            act.activation(ratio[:, :], diff[:, :], ACT.Exp).then_inc(ratio_made, 1)

        @block.vector
        def _(dve):
            dve.memset(bias_rows[:, :], 0.0).then_inc(cleared, 1)
            dve.memset(attended_t[:, :, :, N:NPAD], 0.0).then_inc(cleared, 1)
            dve.wait_ge(prep_a, 4)
            dve.wait_ge(cleared, 2)

            def flat(ap):
                return ap.rearrange("p c n -> p (c n)")

            dve.scalar_tensor_tensor(flat(w_pair[:, LO, :, :]), flat(w_raw[:, :, :]), WS, flat(w_pair[:, HI, :, :]),
                                     ALU.mult, ALU.subtract).then_inc(prep_v, 1)
            dve.scalar_tensor_tensor(flat(g_pair[:, LO, :, :]), flat(g_raw[:, :, :]), WS, flat(g_pair[:, HI, :, :]),
                                     ALU.mult, ALU.subtract).then_inc(prep_v, 1)
            dve.scalar_tensor_tensor(bias_rows[32:33, :], bias_raw[32:33, :], WS, bias_hi[32:33, :],
                                     ALU.mult, ALU.subtract).then_inc(prep_v, 1)
            dve.wait_ge(prep_g, 10)

            def h_and_stats(t, s):
                dve.wait_ge(projected, made(t))
                h = residual[:, bass.ds(t, 1), :]
                dve.scalar_tensor_tensor(h, ps_p[:, s:s + 1, 0:D], 1.0 / WS, h, ALU.mult, ALU.add).then_inc(h_steps, 1)
                wait_apart(dve, h_steps, 3 * t + 1, passed)
                dve.bn_stats(stats[:, s, :], h).then_inc(h_steps, 1)
                wait_apart(dve, h_steps, 3 * t + 2, passed)
                dve.bn_aggr(mean_var[:, s, :], stats[:, s, :]).then_inc(h_steps, 1)

            def norm(t, s):
                dve.wait_ge(std_made, t + 1)
                dve.reciprocal(rstd[:, s:s + 1], std[:, s:s + 1]).then_inc(rstd_made, 1)
                dve.wait_ge(rstd_made, t + 1)
                if not isinstance(t, int) or t >= 2:
                    dve.wait_ge(turned, t - 1)
                    dve.wait_ge(x1_kept, t - 1)
                dve.tensor_scalar(x1_tile[:, s:s + 1, :], residual[:, bass.ds(t, 1), :], mean_var[:, s, 0:1], rstd[:, s:s + 1],
                                  ALU.subtract, ALU.mult).then_inc(x1_made, 1)

            def t_lo(t, s):
                dve.wait_ge(t_hi, t + 1)
                dve.tensor_tensor(xt_pair[:, s, LO, :, :], ps_t[:, s, 0:D].rearrange("p (c t) -> p c t", c=DC),
                                  xt_pair[:, s, HI, :, :], ALU.subtract).then_inc(t_split, 1)

            def pick(t, s):
                dve.wait_ge(gated, made(t))
                dve.tensor_scalar(logits[:, s, :], ps_g[:, s, 0:EXPERTS], 1.0 / WS, None, ALU.mult).then_inc(picked, 1)
                wait_apart(dve, picked, 5 * t + 1, passed)
                dve.max(best[:, s, :], logits[:, s, :]).then_inc(picked, 1)
                wait_apart(dve, picked, 5 * t + 2, passed)
                dve.max_index(best_at[:, s, :], best[:, s, :], logits[:, s, :]).then_inc(picked, 1)
                dve.tensor_copy(best_two[:, :, bass.ds(t, 1)], best[:, s, 0:TOP, None]).then_inc(picked, 1)
                dve.wait_ge(picked, 5 * t + 3)
                dve.tensor_copy(at_f[:, :, bass.ds(t, 1)], best_at[:, s, 0:TOP, None]).then_inc(picked, 1)

            skewed(dve, TILES, (0, h_and_stats), (1, norm), (3, t_lo), (4, pick))

            steps = [0]

            def then(ins):
                steps[0] += 1
                ins.then_inc(chain, 1)
                dve.wait_ge(chain, steps[0])

            def wide(ap):
                return ap[:, :, None].to_broadcast([P, TILES, EXPERTS])

            dve.wait_ge(picked, 5 * TILES)
            then(dve.tensor_tensor(diff[:, :], best_two[:, 1, :], best_two[:, 0, :], ALU.subtract))
            for k in range(TOP):
                then(dve.tensor_tensor(is_best[:, k, :, :], wide(at_f[:, k, :]),
                                       names[:, None, :].to_broadcast([P, TILES, EXPERTS]), ALU.is_equal))
            then(dve.tensor_tensor(chosen[:, :, :], is_best[:, 0, :, :], is_best[:, 1, :, :], ALU.add))
            if N % P:
                then(dve.memset(chosen[N % P:P, TILES - 1, :], 0.0))
            assert steps[0] == CHOSEN
            dve.wait_ge(ratio_made, 1)
            then(dve.tensor_scalar(total[:, :], ratio[:, :], 1.0, None, ALU.add))
            then(dve.reciprocal(weights[:, 0, :], total[:, :]))
            then(dve.tensor_tensor(weights[:, 1, :], weights[:, 0, :], ratio[:, :], ALU.mult))
            dve.wait_ge(ranked, 1)
            counts = ps_r[:, TILES, :]
            then(dve.tensor_copy(start_f[:, :], counts))
            then(dve.tensor_tensor(over[:, :, :], start_f[:, :, None].to_broadcast([P, EXPERTS, MOST_OF_ONE]),
                                   limits[:, None, :].to_broadcast([P, EXPERTS, MOST_OF_ONE]), ALU.is_gt))
            then(dve.tensor_reduce(tiles_f[:, :], over[:, :, :], AX.X, ALU.add))
            then(dve.tensor_scalar(tiles_f[:, :], tiles_f[:, :], float(LEAST_TILES), None, ALU.max))
            then(dve.memset(start_f[:, 0:1], 0.0))
            for e in range(1, EXPERTS):
                then(dve.tensor_tensor(start_f[:, e:e + 1], start_f[:, e - 1:e], tiles_f[:, e - 1:e], ALU.add))
            then(dve.tensor_copy(bounds[:, 0, :], start_f[:, :]))
            then(dve.tensor_copy(bounds[:, 1, :], tiles_f[:, :]))
            then(dve.tensor_scalar(start_f[:, :], start_f[:, :], float(ROWS), None, ALU.mult))
            then(dve.tensor_tensor(place[:, :, :], ps_r[:, 0:TILES, :], start_f[:, None, :].to_broadcast([P, TILES, EXPERTS]), ALU.add))
            for k in range(TOP):
                then(dve.tensor_tensor(place_of[:, :, :], place[:, :, :], is_best[:, k, :, :], ALU.mult))
                then(dve.tensor_reduce(place_f[:, k, :], place_of[:, :, :], AX.X, ALU.add))
                then(dve.tensor_copy(places[:, k, :], place_f[:, k, :]))
            assert steps[0] == ROUTED, steps[0]

        @block.tensor
        def _(pe):
            pe.sem_inc(projected, SLOTS)
            pe.sem_inc(gated, SLOTS)
            pe.wait_ge(prep_v, 3)
            pe.wait_ge(cleared, 2)
            pe.wait_ge(prep_g, 10)

            def project(t, s):
                if not isinstance(t, int) or t >= 2:
                    pe.wait_ge(h_steps, 3 * t - 5)
                split = [(c, a) for c in range(DC) for a in (HI, LO)]
                for n, (c, a) in enumerate(split):
                    x = attended_t[:, a, c, bass.ds(t * P, P)]
                    for b in ((HI, LO) if a == HI else (HI,)):
                        pe.matmul(ps_p[:, s, 0:D], x, w_pair[:, b, c, :], start=(n == 0 and b == HI), stop=False)
                pe.matmul(ps_p[:, s, 0:D], ones[:, :], bias_rows[:, :], start=False, stop=True).then_inc(projected, 1)

            def turn(t, s):
                pe.wait_ge(x1_made, t + 1)
                if not isinstance(t, int) or t >= 2:
                    pe.wait_ge(t_split, t - 1)
                for c in range(DC):
                    mm = pe.transpose(ps_t[:, s, c * P:(c + 1) * P], x1_tile[:, s, c * P:(c + 1) * P], ident[:, :])
                mm.then_inc(turned, 1)

            def gate(t, s):
                pe.wait_ge(t_split, t + 1)
                if not isinstance(t, int) or t >= 2:
                    pe.wait_ge(picked, 5 * t - 9)
                split_matmuls(pe, ps_g[:, s, 0:EXPERTS], lambda a, c: xt_pair[:, s, a, c, :],
                              lambda b, c: g_pair[:, b, c, :], DC).then_inc(gated, 1)

            skewed(pe, TILES, (0, project), (2, turn), (3, gate))
            pe.wait_ge(chain, CHOSEN)
            pe.matmul(ps_r[:, 0:TILES, :], before[:, :], chosen[:, :, :], start=True, stop=False, skip_group_check=True)
            for t in range(TILES):
                mm = pe.matmul(ps_r[:, t + 1:TILES + 1, :], ones[:, :],
                               chosen[:, t:t + 1, :].to_broadcast([P, TILES - t, EXPERTS]),
                               start=False, stop=(t == TILES - 1), skip_group_check=True)
            mm.then_inc(ranked, 1)


def experts(nc, d, keep):
    bounds, queue, answers = keep["bounds"], keep["queue"], keep["answers"]
    WIDE = DC * HIDDEN
    PAIRED = MC // 2
    with ExitStack() as ctx:
        def sb(name, shape, dt=F32):
            return ctx.enter_context(nc.sbuf_tensor(name, shape, dt))

        def psum(name, shape, dt=F32):
            return ctx.enter_context(nc.psum_tensor(name, shape, dt))

        def sem(name):
            return ctx.enter_context(nc.semaphore(name))

        w_raw = sb("expert_w_raw", [P, 2, WIDE])
        w_pair = sb("expert_w_pair", [P, 2, 2, 2, WIDE], F16)
        in_b = sb("in_b", [P, EXPERTS, MC])
        out_b_raw = sb("out_b_raw", [33, EXPERTS * D])
        out_b_hi = sb("out_b_hi", [33, EXPERTS * D], F16)
        out_b_rows = sb("out_b_rows", [P, EXPERTS, D], F16)
        ones = sb("ones_d", [P, P], F16)
        ident = sb("ident_d", [P, P])
        x_tile = sb("x_tile", [P, 2, D])
        xt_pair = sb("x_t_pair", [P, 2, DC, ROWS], F16)
        hidden = sb("hidden", [P, 2, 2, ROWS])
        hidden_pair = sb("hidden_pair", [P, 2, MC, ROWS], F16)
        y_tile = sb("y_tile", [P, 2, D])
        ps_t = psum("ps_x_t", [P, DC, ROWS])
        ps_h = psum("ps_hidden", [P, PAIRED, 2, ROWS])
        ps_y = psum("ps_y", [P, 2, D])

        loaded, prep_g, prep_a, prep_v = sem("e_loaded"), sem("e_prep_g"), sem("e_prep_a"), sem("e_prep_v")
        w_loaded, w_hi, w_split = sem("expert_w_loaded"), sem("expert_w_hi"), sem("expert_w_split")
        x_loaded, turned, x_hi, x_split = sem("x_loaded"), sem("e_turned"), sem("x_hi"), sem("x_split")
        hidden_summed, gelu_made, hidden_hi, hidden_split = sem("hidden_summed"), sem("gelu_made"), sem("hidden_hi"), sem("hidden_split")
        hidden_used, y_made, y_stored, passed = sem("hidden_used"), sem("y_made"), sem("y_stored"), sem("e_passed")
        PART = 2 * WIDE // PAIRED
        queue_tiles = queue.rearrange("(g h p) n -> g p h n", h=2, p=P)
        answer_tiles = answers.rearrange("(g h p) n -> g p h n", h=2, p=P)
        block = ctx.enter_context(nc.Block())

        def start_of(eng, e):
            return eng.value_load(bounds[0:1, 0, bass.ds(e, 1)], min_val=0, max_val=EXPERT_TILES - 1)

        def tiles_of(eng, e):
            return eng.value_load(bounds[0:1, 1, bass.ds(e, 1)], min_val=LEAST_TILES, max_val=MOST_OF_ONE)

        def all_tiles(eng, tile):
            def expert(e, s):
                start, count = start_of(eng, e), tiles_of(eng, e)
                tile(start, e, s, not (isinstance(e, int) and e == EXPERTS - 1))
                with eng.Fori(1, count) as i:
                    g = eng.snap(start + i, min_val=0, max_val=EXPERT_TILES - 1)
                    tile(g, e, s, False)

            return expert

        def all_experts(eng, expert):
            in_loop(eng, 0, EXPERTS - 1, expert)
            expert(EXPERTS - 1, (EXPERTS - 1) % 2)

        def part(s, half, k):
            return w_pair[:, s, half, :, :].rearrange("p a n -> p (a n)")[:, k * PART:(k + 1) * PART]

        def raw_part(k):
            return w_raw[:, :, :].rearrange("p a n -> p (a n)")[:, k * PART:(k + 1) * PART]

        @block.sync
        def _(sp):
            sp.dma_start(in_b[:, :, :], d["in_b"]).then_inc(loaded, 16)
            sp.dma_start(out_b_raw[0:1, :], d["out_b"]).then_inc(loaded, 16)
            sp.dma_start(out_b_raw[32:33, :], d["out_b"]).then_inc(loaded, 16)

            def load(e, s):
                sp.wait_ge(w_split, PAIRED * e)
                for which, w in enumerate(("in_w", "out_w")):
                    sp.dma_start(w_raw[:, which:which + 1, :].rearrange("p a n -> p (a n)"),
                                 d[w][bass.ds(e, 1)].rearrange("a p c n -> (a p) (c n)")).then_inc(w_loaded, 16)

            in_loop(sp, 0, EXPERTS, load)

        @block.gpsimd
        def _(pool):
            pool.memset(ident[:, :], 0.0).then_inc(prep_g, 1)
            pool.wait_ge(prep_g, 1)
            pool.affine_select(out=ident[:, :], in_=ident[:, :], compare_op=ALU.not_equal, fill=1.0,
                               base=0, pattern=[[-1, P]], channel_multiplier=1).then_inc(prep_g, 1)
            pool.memset(ones[:, :], 1.0).then_inc(prep_g, 1)

        @block.scalar
        def _(act):
            act.sem_inc(gelu_made, PAIRED)
            act.sem_inc(y_made, 1)
            act.wait_ge(loaded, 48)
            act.wait_ge(prep_v, 1)
            act.activation(out_b_rows[0:1, :, :].rearrange("p e n -> p (e n)"), out_b_raw[0:1, :], ACT.Copy, scale=WS).then_inc(prep_a, 1)
            act.activation(out_b_hi[32:33, :], out_b_raw[32:33, :], ACT.Copy, scale=WS).then_inc(prep_a, 1)

            def part_hi(e, s, k):
                act.wait_ge(w_loaded, 32 * e + 32)
                act.activation(part(s, HI, k), raw_part(k), ACT.Copy, scale=WS).then_inc(w_hi, 1)

            def load_x(g):
                act.dma_start(x_tile[:, :, :], queue_tiles[bass.ds(g, 1)].rearrange("a p h n -> (a p) h n")).then_inc(x_loaded, 16)

            def x_hi_(g):
                act.wait_ge(turned, g + 1)
                act.activation(xt_pair[:, HI, :, :], ps_t[:, :, :], ACT.Copy).then_inc(x_hi, 1)

            load_x(0)
            for k in range(PAIRED):
                part_hi(0, 0, k)
            x_hi_(0)

            def tile(g, e, s, ahead):
                act.wait_ge(turned, g + 1)
                load_x(g + 1)
                for q in range(PAIRED):
                    act.wait_ge(hidden_split, PAIRED * g + q + 1)
                    wait_apart(act, hidden_summed, PAIRED * g + q + 1, passed)
                    for m in range(2):
                        out = act.activation(hidden[:, q % 2, m, :], ps_h[:, q, m, :], ACT.Gelu, scale=1.0 / WS,
                                             bias=in_b[:, bass.ds(e, 1), 2 * q + m:2 * q + m + 1].rearrange("p a b -> p (a b)"))
                    out.then_inc(gelu_made, 1)
                    if ahead:
                        part_hi(e + 1, 1 - s, q)
                x_hi_(g + 1)
                act.wait_ge(hidden_used, PAIRED * (g + 1) + PAIRED)
                act.wait_ge(y_stored, 16 * g)
                act.activation(y_tile[:, :, :], ps_y[:, :, :], ACT.Copy, scale=1.0 / WS).then_inc(y_made, 1)
                act.wait_ge(y_made, g + 2)
                act.dma_start(answer_tiles[bass.ds(g, 1)].rearrange("a p h n -> (a p) h n"), y_tile[:, :, :]).then_inc(y_stored, 16)

            all_experts(act, all_tiles(act, tile))
            wait_apart(act, y_stored, 16 * (start_of(act, EXPERTS - 1) + tiles_of(act, EXPERTS - 1)), passed)

        @block.vector
        def _(dve):
            dve.sem_inc(hidden_split, SLOTS)
            dve.memset(out_b_rows[:, :, :], 0.0).then_inc(prep_v, 1)
            dve.wait_ge(prep_a, 2)
            dve.wait_ge(prep_v, 1)
            dve.scalar_tensor_tensor(out_b_rows[32:33, :, :].rearrange("p e n -> p (e n)"), out_b_raw[32:33, :], WS, out_b_hi[32:33, :],
                                     ALU.mult, ALU.subtract).then_inc(prep_v, 1)

            def x_lo(g):
                dve.wait_ge(x_hi, g + 1)
                dve.tensor_tensor(xt_pair[:, LO, :, :], ps_t[:, :, :], xt_pair[:, HI, :, :], ALU.subtract).then_inc(x_split, 1)

            def part_lo(e, s, k):
                dve.wait_ge(w_hi, PAIRED * e + k + 1)
                dve.scalar_tensor_tensor(part(s, LO, k), raw_part(k), WS, part(s, HI, k), ALU.mult, ALU.subtract).then_inc(w_split, 1)

            for k in range(PAIRED):
                part_lo(0, 0, k)
            x_lo(0)

            def tile(g, e, s, ahead):
                for q in range(PAIRED):
                    dve.wait_ge(gelu_made, PAIRED * g + q + 1 + PAIRED)
                    dve.wait_ge(hidden_used, PAIRED * g + q + 1)
                    dve.tensor_copy(hidden_pair[:, HI, 2 * q:2 * q + 2, :], hidden[:, q % 2, :, :]).then_inc(hidden_hi, 1)
                    dve.wait_ge(hidden_hi, PAIRED * g + q + 1)
                    dve.tensor_tensor(hidden_pair[:, LO, 2 * q:2 * q + 2, :], hidden[:, q % 2, :, :], hidden_pair[:, HI, 2 * q:2 * q + 2, :],
                                      ALU.subtract).then_inc(hidden_split, 1)
                    if ahead:
                        part_lo(e + 1, 1 - s, q)
                x_lo(g + 1)

            all_experts(dve, all_tiles(dve, tile))

        @block.tensor
        def _(pe):
            pe.sem_inc(hidden_used, PAIRED)
            pe.wait_ge(prep_g, 3)
            pe.wait_ge(prep_v, 2)

            def turn(g):
                pe.wait_ge(x_loaded, 16 * g + 16)
                pe.wait_ge(x_split, g)
                for c in range(DC):
                    for h in range(2):
                        mm = pe.transpose(ps_t[:, c, h * P:(h + 1) * P], x_tile[:, h, c * P:(c + 1) * P], ident[:, :])
                mm.then_inc(turned, 1)

            turn(0)

            def tile(g, e, s, ahead):
                w_in = w_pair[:, s, :, 0, :].rearrange("p a (c m) -> p a c m", c=DC)
                w_out = w_pair[:, s, :, 1, :].rearrange("p a (m c) -> p a m c", m=MC)

                def first_layer(q):
                    pe.wait_ge(gelu_made, PAIRED * g + q + 1)
                    for m in range(2):
                        mm = split_matmuls(pe, ps_h[:, q, m, :], lambda a, c: w_in[:, a, c, (2 * q + m) * P:(2 * q + m + 1) * P],
                                           lambda b, c: xt_pair[:, b, c, :], DC, first_start=(m == 0), check=False)
                    mm.then_inc(hidden_summed, 1)

                def second_layer(q):
                    pe.wait_ge(hidden_split, PAIRED * g + q + 1 + SLOTS)
                    if q == 0:
                        pe.wait_ge(y_made, g + 1)
                    for h in range(2):
                        if q == 0:
                            pe.matmul(ps_y[:, h, :], ones[:, :], out_b_rows[:, bass.ds(e, 1), :], start=(h == 0), stop=False, skip_group_check=True)
                        for m in (2 * q, 2 * q + 1):
                            for a, b in ((HI, HI), (HI, LO), (LO, HI)):
                                mm = pe.matmul(ps_y[:, h, :], hidden_pair[:, a, m, h * P:(h + 1) * P], w_out[:, b, m, :],
                                               start=False, stop=(m == MC - 1 and a == LO), skip_group_check=True)
                    mm.then_inc(hidden_used, 1)

                pe.wait_ge(x_split, g + 1)
                first_layer(0)
                first_layer(1)
                turn(g + 1)
                first_layer(2)
                second_layer(0)
                first_layer(3)
                second_layer(1)
                second_layer(2)
                second_layer(3)

            body = all_tiles(pe, tile)

            def expert(e, s):
                pe.wait_ge(w_split, PAIRED * e + PAIRED)
                body(e, s)

            all_experts(pe, expert)


def gather_and_norm(nc, d, keep):
    residual, weights, places, answers = keep["residual"], keep["weights"], keep["places"], keep["answers"]
    state, pair = keep["state"], keep["chan_a"]
    with ExitStack() as ctx:
        def sb(name, shape, dt=F32):
            return ctx.enter_context(nc.sbuf_tensor(name, shape, dt))

        def sem(name):
            return ctx.enter_context(nc.semaphore(name))

        ident = sb("ident_f", [P, P])
        eps = sb("eps_f", [P, 1])
        rows_of = sb("answer_rows", [P, 2, TOP, D])
        stats = sb("stats_f", [P, 2, 6])
        mean_var = sb("mean_var_f", [P, 2, 2])
        std = sb("std_f", [P, 2])
        rstd = sb("rstd_f", [P, 2])
        x2 = sb("x2_tile", [P, 2, D])
        ps_t = ctx.enter_context(nc.psum_tensor("ps_x2_t", [P, 2, 512], F32))

        prep_g, passed = sem("f_prep_g"), sem("f_passed")
        gathered = [sem("gathered0"), sem("gathered1")]
        h_steps, std_made, rstd_made, x2_made = sem("f_h_steps"), sem("f_std"), sem("f_rstd"), sem("x2_made")
        turned, state_made, t_hi, t_split = sem("f_turned"), sem("state_made"), sem("f_t_hi"), sem("f_t_split")
        block = ctx.enter_context(nc.Block())

        @block.gpsimd
        def _(pool):
            pool.memset(ident[:, :], 0.0).then_inc(prep_g, 1)
            pool.wait_ge(prep_g, 1)
            pool.affine_select(out=ident[:, :], in_=ident[:, :], compare_op=ALU.not_equal, fill=1.0,
                               base=0, pattern=[[-1, P]], channel_multiplier=1).then_inc(prep_g, 1)
            pool.memset(eps[:, :], EPS).then_inc(prep_g, 1)
            for t in range(TILES):
                rows = min(P, N - t * P)
                if t >= 2:
                    pool.wait_ge(h_steps, 4 * t - 6)
                for k in range(TOP):
                    pool.indirect_dma_start(rows_of[0:rows, t % 2, k, :], None, answers[0:EXPERT_TILES * ROWS, :],
                                            bass.IndirectOffsetOnAxis(places[0:rows, k, t:t + 1], 0)).then_inc(gathered[t % 2], 16)

        @block.scalar
        def _(act):
            act.wait_ge(prep_g, 3)

            def root(t, s):
                act.wait_ge(h_steps, 4 * t + 4)
                act.activation(std[:, s:s + 1], mean_var[:, s, 1:2], ACT.Sqrt, bias=eps[:, 0:1]).then_inc(std_made, 1)

            def out_hi(t, s):
                act.wait_ge(turned, t + 1)
                turned_rows = ps_t[:, s, 0:D].rearrange("p (c t) -> p c t", c=DC)
                act.activation(state[:, :, bass.ds(t * P, P)], turned_rows, ACT.Copy).then_inc(state_made, 1)
                act.activation(pair[:, HI, :, bass.ds(t * P, P)], turned_rows, ACT.Copy).then_inc(t_hi, 1)

            skewed(act, TILES, (0, root), (3, out_hi))

        @block.vector
        def _(dve):
            def add_answers(t, s):
                rows = P if not isinstance(t, int) else min(P, N - t * P)
                dve.wait_ge(gathered[s], 16 * t + 32 - 16 * s)
                h = residual[0:rows, bass.ds(t, 1), :]
                for k in range(TOP):
                    dve.scalar_tensor_tensor(h, rows_of[0:rows, s, k:k + 1, :], weights[0:rows, k, bass.ds(t, 1)], h,
                                             ALU.mult, ALU.add).then_inc(h_steps, 1)
                    wait_apart(dve, h_steps, 4 * t + k + 1, passed)
                dve.bn_stats(stats[:, s, :], residual[:, bass.ds(t, 1), :]).then_inc(h_steps, 1)
                wait_apart(dve, h_steps, 4 * t + 3, passed)
                dve.bn_aggr(mean_var[:, s, :], stats[:, s, :]).then_inc(h_steps, 1)

            def norm(t, s):
                dve.wait_ge(std_made, t + 1)
                dve.reciprocal(rstd[:, s:s + 1], std[:, s:s + 1]).then_inc(rstd_made, 1)
                dve.wait_ge(rstd_made, t + 1)
                if not isinstance(t, int) or t >= 2:
                    dve.wait_ge(turned, t - 1)
                dve.tensor_scalar(x2[:, s:s + 1, :], residual[:, bass.ds(t, 1), :], mean_var[:, s, 0:1], rstd[:, s:s + 1],
                                  ALU.subtract, ALU.mult).then_inc(x2_made, 1)

            def out_lo(t, s):
                dve.wait_ge(t_hi, t + 1)
                dve.tensor_tensor(pair[:, LO, :, bass.ds(t * P, P)], ps_t[:, s, 0:D].rearrange("p (c t) -> p c t", c=DC),
                                  pair[:, HI, :, bass.ds(t * P, P)], ALU.subtract).then_inc(t_split, 1)

            skewed(dve, TILES, (0, add_answers), (1, norm), (3, out_lo))

        @block.tensor
        def _(pe):
            pe.wait_ge(prep_g, 2)

            def turn(t, s):
                pe.wait_ge(x2_made, t + 1)
                if not isinstance(t, int) or t >= 2:
                    pe.wait_ge(t_split, t - 1)
                for c in range(DC):
                    mm = pe.transpose(ps_t[:, s, c * P:(c + 1) * P], x2[:, s, c * P:(c + 1) * P], ident[:, :])
                mm.then_inc(turned, 1)

            skewed(pe, TILES, (2, turn))


LAYERS, HEADS = 12, 16
HD = D // HEADS
CHUNKS = 8
CT = N // CHUNKS
CP = PAIRS // CHUNKS
PIECES = CHUNKS
PIECE = (4 * D * DC) // PIECES


def linear_attention_layers(nc, d, keep):
    state, pair, bias_sum = keep["state"], keep["chan_a"], keep["bias_sum"]
    with ExitStack() as ctx:
        def sb(name, shape, dt=F32):
            return ctx.enter_context(nc.sbuf_tensor(name, shape, dt))

        def psum(name, shape, dt=F32):
            return ctx.enter_context(nc.psum_tensor(name, shape, dt))

        def sem(name):
            return ctx.enter_context(nc.semaphore(name))

        w_raw = sb("layer_w_raw", [P, PIECES, PIECE])
        w_pair = sb("layer_w_pair", [P, 2, 2, PIECES * PIECE], F16)
        kv_b_raw = sb("kv_b_raw", [33, 2 * D])
        kv_b_hi = sb("kv_b_hi", [33, 2 * D], F16)
        kv_b_rows = sb("kv_b_rows", [P, 2, 2 * D], F16)
        q_b_raw = sb("q_b_raw", [P, LAYERS, DC])
        q_b = sb("q_b", [P, LAYERS, DC])
        proj_b = sb("proj_b", [P, LAYERS, DC])
        ones = sb("ones_g", [P, P], F16)
        own = sb("own_image_g", [PT, 2])
        mask = sb("head_mask", [P, 2, DC, P])
        k_pair = sb("k_pair_g", [PT, CP, 2, D], F16)
        v_pair = sb("v_pair_g", [PT, CP, 2, 2, D], F16)
        q_pair = sb("q_pair_g", [P, 2, 2, DC, CT], F16)
        outer = sb("outer", [P, 2, 2, DC, P])
        outer_pair = sb("outer_pair", [P, 2, 2, 2, DC, P], F16)
        y_pair = sb("y_pair", [P, 2, DC, CT], F16)
        ps_kv = psum("ps_kv", [P, 2, 512])
        ps_o = psum("ps_outer", [P, 2, 2, DC, P])
        ps_y = psum("ps_y_g", [P, DC, 512])
        ps_x = psum("ps_q_or_x", [P, DC, 512])

        loaded, prep_g, prep_a, prep_v = sem("g_loaded"), sem("g_prep_g"), sem("g_prep_a"), sem("g_prep_v")
        w_loaded, b_loaded, w_hi, w_split = sem("g_w_loaded"), sem("g_b_loaded"), sem("g_w_hi"), sem("g_w_split")
        b_hi, b_split = sem("g_b_hi"), sem("g_b_split")
        kv_summed, q_summed, outer_summed, applied, x_summed = sem("kv_summed"), sem("q_summed"), sem("outer_summed"), sem("applied"), sem("x_summed")
        kv_hi, q_hi, outer_hi, y_hi, x_hi = sem("kv_hi"), sem("q_hi"), sem("outer_hi"), sem("y_hi"), sem("g_x_hi")
        kv_split, q_split, outer_masked, outer_split = sem("kv_split"), sem("q_split"), sem("outer_masked"), sem("outer_split")
        y_split, x_made, x_split, passed = sem("y_split"), sem("g_x_made"), sem("g_x_split"), sem("g_passed")
        block = ctx.enter_context(nc.Block())

        def all_steps(eng, step):
            def layer(l, s):
                for c in (0, 1):
                    step(CHUNKS * l + c, l, s, c, c)
                in_loop(eng, 2, CHUNKS, lambda c, parity: step(CHUNKS * l + c, l, s, c, parity))

            layer(0, 0)
            with eng.Fori(0, (LAYERS - 2) // 2) as j:
                layer(1 + 2 * j, 1)
                layer(2 + 2 * j, 0)
            layer(LAYERS - 1, 1)
            step(CHUNKS * LAYERS, LAYERS, 0, 0, 0)
            step(CHUNKS * LAYERS + 1, LAYERS, 0, 1, 1)

        def w_pieces(s, half, n):
            return w_pair[:, s, half, :].rearrange("p (a n) -> p a n", n=PIECE)[:, bass.ds(n, 1), :]

        def known(value, least):
            return not isinstance(value, int) or value >= least

        def has(g, l, c, back):
            if isinstance(l, int) and l == 0 and isinstance(c, int) and c < back:
                return None
            if isinstance(l, int) and l == LAYERS and c >= back:
                return None
            if isinstance(c, int) and c < back:
                return c - back + CHUNKS, 1
            return c - back, 0

        @block.sync
        def _(sp):
            sp.dma_start(q_b_raw[:, :, :], d["q1_bcol"]).then_inc(loaded, 16)
            sp.dma_start(proj_b[:, :, :], d["proj1_bcol"]).then_inc(loaded, 16)

            def load(l, s):
                sp.wait_ge(w_split, PIECES * l)
                sp.wait_ge(b_split, l)
                sp.dma_start(w_raw[:, 0:6, :].rearrange("p a n -> p (a n)"),
                             d["qkv1_w"][bass.ds(l, 1)].rearrange("a p c n -> (a p) (c n)")).then_inc(w_loaded, 16)
                sp.dma_start(w_raw[:, 6:8, :].rearrange("p a n -> p (a n)"),
                             d["proj1_w"][bass.ds(l, 1)].rearrange("a p c n -> (a p) (c n)")).then_inc(w_loaded, 16)
                sp.dma_start(kv_b_raw[0:1, :], d["qkv1_b"][bass.ds(l, 1), D:3 * D]).then_inc(b_loaded, 16)
                sp.dma_start(kv_b_raw[32:33, :], d["qkv1_b"][bass.ds(l, 1), D:3 * D]).then_inc(b_loaded, 16)

            in_loop(sp, 0, LAYERS, load)

        @block.gpsimd
        def _(pool):
            pool.memset(own[:, :], 1.0 / WS).then_inc(prep_g, 1)
            pool.memset(ones[:, :], 1.0).then_inc(prep_g, 1)
            pool.memset(mask[:, :, :, :], float(HD) ** -0.5).then_inc(prep_g, 1)
            pool.wait_ge(prep_g, 3)
            pool.affine_select(out=own[:, 0:1], in_=own[:, 0:1], compare_op=ALU.is_ge, fill=0.0,
                               base=TOK - 1, pattern=[[0, 1]], channel_multiplier=-1).then_inc(prep_g, 1)
            pool.affine_select(out=own[:, 1:2], in_=own[:, 1:2], compare_op=ALU.is_ge, fill=0.0,
                               base=-TOK, pattern=[[0, 1]], channel_multiplier=1).then_inc(prep_g, 1)
            for i in range(2):
                for c in range(DC):
                    m = mask[:, i, c, :].rearrange("p (h j) -> p h j", j=HD)
                    pool.affine_select(out=m, in_=m, compare_op=ALU.is_ge, fill=0.0, base=0,
                                       pattern=[[-HD, P // HD], [0, HD]], channel_multiplier=1).then_inc(prep_g, 1)
                    pool.wait_ge(prep_g, 6 + 2 * (DC * i + c))
                    pool.affine_select(out=m, in_=m, compare_op=ALU.is_ge, fill=0.0, base=HD - 1,
                                       pattern=[[HD, P // HD], [0, HD]], channel_multiplier=-1).then_inc(prep_g, 1)

            def step(g, l, s, c, parity):
                if has(g, l, c, 1) is None:
                    return
                for p in range(CP):
                    q = CP * (g - 1) + p
                    pool.wait_ge(outer_hi, q + 1)
                    pool.tensor_tensor(outer_pair[:, p % 2, LO], outer[:, p % 2], outer_pair[:, p % 2, HI], ALU.subtract).then_inc(outer_split, 1)

            all_steps(pool, step)

        @block.scalar
        def _(act):
            def biases_hi(l, s):
                act.wait_ge(b_loaded, 32 * l + 32)
                act.activation(kv_b_rows[0:1, s, :], kv_b_raw[0:1, :], ACT.Copy, scale=WS)
                act.activation(kv_b_hi[32:33, :], kv_b_raw[32:33, :], ACT.Copy, scale=WS).then_inc(b_hi, 1)

            act.wait_ge(loaded, 32)
            act.activation(q_b[:, :, :], q_b_raw[:, :, :], ACT.Copy, scale=WS).then_inc(prep_a, 1)
            act.wait_ge(prep_v, 1)
            act.wait_ge(w_loaded, 32)
            for n in range(PIECES):
                act.activation(w_pieces(0, HI, n), w_raw[:, n:n + 1, :], ACT.Copy, scale=WS).then_inc(w_hi, 1)
            biases_hi(0, 0)
            act.wait_ge(prep_g, 5)
            act.wait_ge(prep_a, 1)
            act.wait_ge(prep_v, 2 + LAYERS)

            def split_next_hi(l, s, c):
                act.wait_ge(w_loaded, 32 * l + 64)
                act.activation(w_pieces(1 - s, HI, c), w_raw[:, bass.ds(c, 1), :], ACT.Copy, scale=WS).then_inc(w_hi, 1)
                if isinstance(c, int) and c == 1:
                    biases_hi(l + 1, 1 - s)

            def step(g, l, s, c, parity):
                first = has(g, l, c, 0)
                older, oldest = has(g, l, c, 1), has(g, l, c, 2)
                for p in range(CP):
                    if older:
                        q = CP * (g - 1) + p
                        act.wait_ge(outer_masked, q + 1)
                        if known(q, 2):
                            act.wait_ge(applied, q - 1)
                        act.activation(outer_pair[:, p % 2, HI], outer[:, p % 2], ACT.Copy).then_inc(outer_hi, 1)
                    if first:
                        act.wait_ge(kv_summed, CP * g + p + 1)
                        act.activation(k_pair[:, p, HI, :], ps_kv[0:PT, p % 2, 0:D], ACT.Copy, scale=1.0 / WS)
                        for i in range(2):
                            out = act.activation(v_pair[:, p, HI, i, :], ps_kv[0:PT, p % 2, D:2 * D], ACT.Copy, scale=own[:, i:i + 1])
                        out.then_inc(kv_hi, 1)
                    if oldest and p == 2:
                        chunk, back = oldest
                        wait_apart(act, x_made, g - 1, passed)
                        for m in range(DC):
                            out = act.activation(pair[:, HI, m, bass.ds(chunk * CT, CT)], state[:, m, bass.ds(chunk * CT, CT)], ACT.Identity,
                                                 bias=bias_sum[:, bass.ds(l - back + 1, 1), m:m + 1].rearrange("p a b -> p (a b)"))
                        out.then_inc(x_hi, 1)
                if first:
                    if known(g, 2):
                        act.wait_ge(applied, CP * (g - 1))
                    wait_apart(act, q_summed, g + 1, passed)
                    for m in range(DC):
                        out = act.activation(q_pair[:, parity, HI, m, :], ps_x[:, m, 0:CT], ACT.Identity,
                                             bias=q_b[:, bass.ds(l, 1), m:m + 1].rearrange("p a b -> p (a b)"))
                    out.then_inc(q_hi, 1)
                if older:
                    act.wait_ge(applied, CP * g)
                    if known(g, 2):
                        act.wait_ge(x_summed, g - 1)
                    act.activation(y_pair[:, HI], ps_y[:, :, 0:CT], ACT.Copy, scale=1.0 / WS).then_inc(y_hi, 1)
                if first and not (isinstance(l, int) and l == LAYERS - 1):
                    split_next_hi(l, s, c)

            all_steps(act, step)

        @block.vector
        def _(dve):
            dve.memset(kv_b_rows[:, :, :], 0.0).then_inc(prep_v, 1)
            dve.memset(bias_sum[:, 0:1, :], 0.0).then_inc(prep_v, 1)
            dve.wait_ge(loaded, 32)
            for l in range(LAYERS):
                dve.wait_ge(prep_v, 2 + l)
                dve.tensor_tensor(bias_sum[:, l + 1, :], bias_sum[:, l, :], proj_b[:, l, :], ALU.add).then_inc(prep_v, 1)

            def piece_lo(count, s, n):
                dve.wait_ge(w_hi, count)
                dve.scalar_tensor_tensor(w_pieces(s, LO, n), w_raw[:, bass.ds(n, 1), :], WS, w_pieces(s, HI, n),
                                         ALU.mult, ALU.subtract).then_inc(w_split, 1)

            def biases_lo(l, s):
                dve.wait_ge(b_hi, l + 1)
                dve.scalar_tensor_tensor(kv_b_rows[32:33, s, :], kv_b_raw[32:33, :], WS, kv_b_hi[32:33, :],
                                         ALU.mult, ALU.subtract).then_inc(b_split, 1)

            for n in range(PIECES):
                piece_lo(n + 1, 0, n)
            biases_lo(0, 0)
            dve.wait_ge(prep_g, 5 + 4 * DC)
            dve.wait_ge(prep_a, 1)
            dve.wait_ge(prep_v, 2 + LAYERS)

            def step(g, l, s, c, parity):
                first = has(g, l, c, 0)
                older, oldest = has(g, l, c, 1), has(g, l, c, 2)
                for p in range(CP):
                    if older:
                        q = CP * (g - 1) + p
                        dve.wait_ge(outer_summed, q + 1)
                        if known(q, 2):
                            dve.wait_ge(outer_split, q - 1)
                        dve.tensor_tensor(outer[:, p % 2], ps_o[:, p % 2], mask[:, :, :, :], ALU.mult).then_inc(outer_masked, 1)
                    if oldest and p == 2:
                        chunk, back = oldest
                        dve.wait_ge(x_summed, g - 1)
                        x = state[:, :, bass.ds(chunk * CT, CT)]
                        dve.scalar_tensor_tensor(x, ps_x[:, :, 0:CT], 1.0 / WS, x, ALU.mult, ALU.add).then_inc(x_made, 1)
                    if first:
                        dve.wait_ge(kv_hi, CP * g + p + 1)
                        dve.scalar_tensor_tensor(k_pair[:, p, LO, :], ps_kv[0:PT, p % 2, 0:D], 1.0 / WS, k_pair[:, p, HI, :],
                                                 ALU.mult, ALU.subtract)
                        for i in range(2):
                            out = dve.scalar_tensor_tensor(v_pair[:, p, LO, i, :], ps_kv[0:PT, p % 2, D:2 * D], own[:, i:i + 1],
                                                           v_pair[:, p, HI, i, :], ALU.mult, ALU.subtract)
                        out.then_inc(kv_split, 1)
                    if oldest and p == 3:
                        chunk, back = oldest
                        dve.wait_ge(x_hi, g - 1)
                        for m in range(DC):
                            out = dve.scalar_tensor_tensor(pair[:, LO, m, bass.ds(chunk * CT, CT)], state[:, m, bass.ds(chunk * CT, CT)],
                                                           bias_sum[:, bass.ds(l - back + 1, 1), m:m + 1].rearrange("p a b -> p (a b)"),
                                                           pair[:, HI, m, bass.ds(chunk * CT, CT)], ALU.add, ALU.subtract)
                        out.then_inc(x_split, 1)
                if first:
                    dve.wait_ge(q_hi, g + 1)
                    for m in range(DC):
                        out = dve.scalar_tensor_tensor(q_pair[:, parity, LO, m, :], ps_x[:, m, 0:CT],
                                                       q_b[:, bass.ds(l, 1), m:m + 1].rearrange("p a b -> p (a b)"),
                                                       q_pair[:, parity, HI, m, :], ALU.add, ALU.subtract)
                    out.then_inc(q_split, 1)
                if older:
                    dve.wait_ge(y_hi, g)
                    dve.scalar_tensor_tensor(y_pair[:, LO], ps_y[:, :, 0:CT], 1.0 / WS, y_pair[:, HI],
                                             ALU.mult, ALU.subtract).then_inc(y_split, 1)
                if first and not (isinstance(l, int) and l == LAYERS - 1):
                    piece_lo(PIECES * (l + 1) + c + 1, 1 - s, c)
                    if isinstance(c, int) and c == 1:
                        biases_lo(l + 1, 1 - s)

            all_steps(dve, step)

        @block.tensor
        def _(pe):
            pe.wait_ge(prep_g, 2)

            def step(g, l, s, c, parity):
                first = has(g, l, c, 0)
                older, oldest = has(g, l, c, 1), has(g, l, c, 2)
                w_qkv = w_pair[:, s, :, 0:6 * PIECE].rearrange("p a (c n) -> p a c n", c=DC)

                def outer_products(p):
                    q = CP * (g - 1) + p
                    pe.wait_ge(kv_split, q + 1)
                    if known(q, 2):
                        pe.wait_ge(outer_masked, q - 1)
                    for i in range(2):
                        for m in range(DC):
                            mm = split_matmuls(pe, ps_o[:, p % 2, i, m, :], lambda a, _: k_pair[:, p, a, m * P:(m + 1) * P],
                                               lambda b, _: v_pair[:, p, b, i, m * P:(m + 1) * P], 1,
                                               first_start=(i == 0 and m == 0), check=False)
                    mm.then_inc(outer_summed, 1)

                def keys_and_values(p):
                    if known(CP * g + p, 2):
                        pe.wait_ge(kv_split, CP * g + p - 1)
                    pe.matmul(ps_kv[0:PT, p % 2, :], ones[:, 0:PT], kv_b_rows[:, s, :], start=True, stop=False)
                    for n, (m, a, b) in enumerate((m, a, b) for m in range(DC) for a, b in ((HI, HI), (HI, LO), (LO, HI))):
                        mm = pe.matmul(ps_kv[0:PT, p % 2, :], pair[:, a, m, bass.ds(c * CT + p * PT, PT)], w_qkv[:, b, m, D:3 * D],
                                       start=False, stop=(n == 3 * DC - 1))
                    mm.then_inc(kv_summed, 1)

                def queries():
                    if known(g, 2):
                        pe.wait_ge(x_made, g - 1)
                    for m in range(DC):
                        mm = split_matmuls(pe, ps_x[:, m, 0:CT], lambda a, k: w_qkv[:, a, k, m * P:(m + 1) * P],
                                           lambda b, k: pair[:, b, k, bass.ds(c * CT, CT)], DC)
                    mm.then_inc(q_summed, 1)

                def apply(p):
                    q = CP * (g - 1) + p
                    pe.wait_ge(outer_split, q + 1)
                    if p == 0:
                        pe.wait_ge(q_split, g)
                        if known(g, 2):
                            pe.wait_ge(y_split, g - 1)
                    for i in range(2):
                        cols = slice((2 * p + i) * TOK, (2 * p + i + 1) * TOK)
                        for m in range(DC):
                            mm = split_matmuls(pe, ps_y[:, m, cols], lambda a, _: outer_pair[:, p % 2, a, i, m, :],
                                               lambda b, _: q_pair[:, 1 - parity, b, m, cols], 1,
                                               first_start=(p == 0 and i == 0), check=False)
                    mm.then_inc(applied, 1)

                def project():
                    chunk, back = oldest
                    slot = s if back == 0 else 1 - s
                    w_proj = w_pair[:, slot, :, 6 * PIECE:8 * PIECE].rearrange("p a (c n) -> p a c n", c=DC)
                    pe.wait_ge(w_split, PIECES * (l - back + 1))
                    pe.wait_ge(y_split, g - 1)
                    pe.wait_ge(q_split, g if older else g - 1)
                    for m in range(DC):
                        mm = split_matmuls(pe, ps_x[:, m, 0:CT], lambda a, k: w_proj[:, a, k, m * P:(m + 1) * P],
                                           lambda b, k: y_pair[:, b, k, :], DC)
                    mm.then_inc(x_summed, 1)

                if first:
                    if isinstance(c, int) and c == 0:
                        pe.wait_ge(w_split, PIECES * l + 6)
                        pe.wait_ge(b_split, l + 1)
                    if not (isinstance(l, int) and l == 0):
                        pe.wait_ge(x_split, g - CHUNKS + 1)
                for p in range(CP):
                    if older:
                        outer_products(p)
                    if first:
                        keys_and_values(p)
                    if older and p >= 1:
                        apply(p - 1)
                    if oldest and p == 1:
                        project()
                if first:
                    queries()
                if older:
                    apply(CP - 1)

            all_steps(pe, step)


GATED = 8
RANK = 8


def final_block(nc, d, keep):
    residual, state, bias_sum = keep["residual"], keep["state"], keep["bias_sum"]
    with ExitStack() as ctx:
        def sb(name, shape, dt=F32):
            return ctx.enter_context(nc.sbuf_tensor(name, shape, dt))

        def psum(name, shape, dt=F32):
            return ctx.enter_context(nc.psum_tensor(name, shape, dt))

        def sem(name):
            return ctx.enter_context(nc.semaphore(name))

        MIX = RANK + GATED
        base_raw = sb("base_raw", [P, DC, D])
        base_pair = sb("base_pair", [P, 2, DC, D], F16)
        mix_raw = sb("mix_raw", [P, DC, MIX])
        mix_pair = sb("mix_pair", [P, 2, DC, MIX], F16)
        lora_raw = sb("lora_raw", [P, D])
        lora_pair = sb("lora_pair", [P, 2, D], F16)
        b_raw = sb("final_b_raw", [33, D + MIX])
        b_hi = sb("final_b_hi", [33, D + MIX], F16)
        b_rows = sb("final_b_rows", [P, D + MIX], F16)
        ones = sb("ones_h", [P, P], F16)
        ident = sb("ident_h", [P, P])
        eps = sb("eps_h", [P, 1])
        xb = sb("x_with_bias", [P, 2, DC, P])
        stats = sb("stats_h", [P, 2, 6])
        mean_var = sb("mean_var_h", [P, 2, 2])
        std = sb("std_h", [P, 2])
        rstd = sb("rstd_h", [P, 2])
        x3 = sb("x3", [P, 2, D])
        x3_pair = sb("x3_pair", [P, 2, 2, DC, P], F16)
        top = sb("top_h", [P, 2])
        neg_top = sb("neg_top_h", [P, 2])
        exps = sb("exps_h", [P, 2, GATED])
        sums = sb("sums_h", [P, 2])
        inv = sb("inv_h", [P, 2])
        gates = sb("gates", [P, 2, GATED], mybir.dt.bfloat16)
        mid = sb("mid", [P, 2, RANK])
        gated = sb("gated", [P, 2, P])
        gated_pair = sb("gated_pair", [P, 2, 2, P], F16)
        out_tile = sb("out_tile", [P, 2, D])
        ps_x = psum("ps_x_back", [P, 2, 512])
        ps_t = psum("ps_x3_t", [P, 2, 512])
        ps_m = psum("ps_mixed", [P, 2, MIX])
        ps_g = psum("ps_gated_t", [P, 2, P])
        ps_b = psum("ps_out", [P, 2, 512])

        loaded, prep_g, prep_a, prep_v = sem("h_loaded"), sem("h_prep_g"), sem("h_prep_a"), sem("h_prep_v")
        xb_made, turned_back, h_steps = sem("xb_made"), sem("turned_back"), sem("h_h_steps")
        std_made, rstd_made, x3_made = sem("h_std"), sem("h_rstd"), sem("x3_made")
        turned, x3_hi, x3_split, mixed = sem("h_turned"), sem("x3_hi"), sem("x3_split"), sem("mixed")
        top_steps, exp_made, gate_steps = sem("top_steps"), sem("h_exp_made"), sem("gate_steps")
        gated_turned, gated_hi, gated_split = sem("gated_turned"), sem("gated_hi"), sem("gated_split")
        based, summed, out_made = sem("based"), sem("out_summed"), sem("out_made")
        passed = sem("h_passed")
        stored = [sem("stored0"), sem("stored1")]
        block = ctx.enter_context(nc.Block())

        def later(t):
            return not isinstance(t, int) or t >= 2

        @block.sync
        def _(sp):
            sp.wait_ge(prep_g, 3)
            sp.dma_start(base_raw[:, :, :], d["base_w"]).then_inc(loaded, 16)
            sp.dma_start(mix_raw[:, :, 0:RANK], d["lora_a"]).then_inc(loaded, 16)
            sp.dma_start(mix_raw[:, :, RANK:MIX], d["router_w"]).then_inc(loaded, 16)
            sp.dma_start(lora_raw[0:GATED * RANK, :], d["lora_b"]).then_inc(loaded, 16)
            for row in (0, 32):
                sp.dma_start(b_raw[row:row + 1, 0:D], d["base_b"]).then_inc(loaded, 16)
                sp.dma_start(b_raw[row:row + 1, D + RANK:D + MIX], d["router_b"]).then_inc(loaded, 16)

            def store(t, s):
                rows = P if not isinstance(t, int) else min(P, N - t * P)
                sp.wait_ge(out_made, t + 1)
                sp.dma_start(d["out"][bass.ds(t * P, rows), :], out_tile[0:rows, s, :]).then_inc(stored[s], 16)

            in_loop(sp, 0, TILES - 1, store)
            store(TILES - 1, (TILES - 1) % 2)
            sp.wait_ge(stored[0], 16 * ((TILES + 1) // 2))
            sp.wait_ge(stored[1], 16 * (TILES // 2))

        @block.gpsimd
        def _(pool):
            pool.memset(lora_raw[:, :], 0.0).then_inc(prep_g, 1)
            pool.memset(b_raw[:, :], 0.0).then_inc(prep_g, 1)
            pool.memset(ident[:, :], 0.0).then_inc(prep_g, 1)
            pool.wait_ge(prep_g, 3)
            pool.affine_select(out=ident[:, :], in_=ident[:, :], compare_op=ALU.not_equal, fill=1.0,
                               base=0, pattern=[[-1, P]], channel_multiplier=1).then_inc(prep_g, 1)
            pool.memset(eps[:, :], EPS).then_inc(prep_g, 1)
            pool.memset(ones[:, :], 1.0).then_inc(prep_g, 1)
            pool.memset(b_rows[:, :], 0.0).then_inc(prep_g, 1)
            pool.memset(gated[:, :, :], 0.0).then_inc(prep_g, 1)

        @block.scalar
        def _(act):
            act.wait_ge(prep_g, 8)
            act.wait_ge(loaded, 128)
            act.activation(base_pair[:, HI], base_raw[:, :, :], ACT.Copy, scale=WS).then_inc(prep_a, 1)
            act.activation(mix_pair[:, HI], mix_raw[:, :, :], ACT.Copy, scale=WS).then_inc(prep_a, 1)
            act.activation(lora_pair[:, HI, :], lora_raw[:, :], ACT.Copy, scale=2.0 * WS).then_inc(prep_a, 1)
            act.activation(b_rows[0:1, :], b_raw[0:1, :], ACT.Copy, scale=WS).then_inc(prep_a, 1)
            act.activation(b_hi[32:33, :], b_raw[32:33, :], ACT.Copy, scale=WS).then_inc(prep_a, 1)

            def add_bias(t, s):
                if later(t):
                    act.wait_ge(turned_back, t - 1)
                for c in range(DC):
                    out = act.activation(xb[:, s, c, :], state[:, c, bass.ds(t * P, P)], ACT.Identity,
                                         bias=bias_sum[:, LAYERS, c:c + 1])
                out.then_inc(xb_made, 1)

            def root(t, s):
                act.wait_ge(h_steps, 3 * t + 3)
                act.activation(std[:, s:s + 1], mean_var[:, s, 1:2], ACT.Sqrt, bias=eps[:, 0:1]).then_inc(std_made, 1)

            def turned_hi(t, s):
                act.wait_ge(turned, t + 1)
                if later(t):
                    act.wait_ge(based, t - 1)
                act.activation(x3_pair[:, s, HI], ps_t[:, s, 0:D].rearrange("p (c t) -> p c t", c=DC), ACT.Copy).then_inc(x3_hi, 1)

            def exp(t, s):
                act.wait_ge(top_steps, 2 * t + 2)
                if later(t):
                    act.wait_ge(gate_steps, 4 * t - 4)
                act.activation(exps[:, s, :], ps_m[:, s, RANK:MIX], ACT.Exp, bias=neg_top[:, s:s + 1], scale=1.0 / WS,
                               accum_out=sums[:, s:s + 1]).then_inc(exp_made, 1)

            def gated_to_hi(t, s):
                act.wait_ge(gated_turned, t + 1)
                if later(t):
                    act.wait_ge(summed, t - 1)
                act.activation(gated_pair[:, s, HI, :], ps_g[:, s, :], ACT.Copy).then_inc(gated_hi, 1)

            skewed(act, TILES, (0, add_bias), (1, root), (3, gated_to_hi), (2, turned_hi), (2, exp))

        @block.vector
        def _(dve):
            dve.wait_ge(prep_a, 5)
            dve.scalar_tensor_tensor(base_pair[:, LO], base_raw[:, :, :], WS, base_pair[:, HI], ALU.mult, ALU.subtract).then_inc(prep_v, 1)
            dve.scalar_tensor_tensor(mix_pair[:, LO], mix_raw[:, :, :], WS, mix_pair[:, HI], ALU.mult, ALU.subtract).then_inc(prep_v, 1)
            dve.scalar_tensor_tensor(lora_pair[:, LO, :], lora_raw[:, :], 2.0 * WS, lora_pair[:, HI, :], ALU.mult, ALU.subtract).then_inc(prep_v, 1)
            dve.scalar_tensor_tensor(b_rows[32:33, :], b_raw[32:33, :], WS, b_hi[32:33, :], ALU.mult, ALU.subtract).then_inc(prep_v, 1)

            def add_x(t, s):
                dve.wait_ge(turned_back, t + 1)
                h = residual[:, bass.ds(t, 1), :]
                dve.tensor_tensor(h, h, ps_x[:, s:s + 1, 0:D], ALU.add).then_inc(h_steps, 1)
                wait_apart(dve, h_steps, 3 * t + 1, passed)
                dve.bn_stats(stats[:, s, :], h).then_inc(h_steps, 1)
                wait_apart(dve, h_steps, 3 * t + 2, passed)
                dve.bn_aggr(mean_var[:, s, :], stats[:, s, :]).then_inc(h_steps, 1)

            def norm(t, s):
                dve.wait_ge(std_made, t + 1)
                dve.reciprocal(rstd[:, s:s + 1], std[:, s:s + 1]).then_inc(rstd_made, 1)
                dve.wait_ge(rstd_made, t + 1)
                if later(t):
                    dve.wait_ge(turned, t - 1)
                dve.tensor_scalar(x3[:, s:s + 1, :], residual[:, bass.ds(t, 1), :], mean_var[:, s, 0:1], rstd[:, s:s + 1],
                                  ALU.subtract, ALU.mult).then_inc(x3_made, 1)

            def turned_lo(t, s):
                dve.wait_ge(x3_hi, t + 1)
                dve.tensor_tensor(x3_pair[:, s, LO], ps_t[:, s, 0:D].rearrange("p (c t) -> p c t", c=DC), x3_pair[:, s, HI],
                                  ALU.subtract).then_inc(x3_split, 1)

            def highest(t, s):
                dve.wait_ge(mixed, t + 1)
                dve.tensor_reduce(top[:, s:s + 1], ps_m[:, s, RANK:MIX], AX.X, ALU.max).then_inc(top_steps, 1)
                dve.wait_ge(top_steps, 2 * t + 1)
                dve.tensor_scalar(neg_top[:, s:s + 1], top[:, s:s + 1], -1.0 / WS, None, ALU.mult).then_inc(top_steps, 1)

            def gate(t, s):
                dve.wait_ge(exp_made, t + 1)
                dve.reciprocal(inv[:, s:s + 1], sums[:, s:s + 1]).then_inc(gate_steps, 1)
                dve.tensor_scalar(mid[:, s, :], ps_m[:, s, 0:RANK], 1.0 / WS, None, ALU.mult).then_inc(gate_steps, 1)
                dve.wait_ge(gate_steps, 4 * t + 1)
                dve.tensor_scalar(gates[:, s, :], exps[:, s, :], inv[:, s:s + 1], None, ALU.mult).then_inc(gate_steps, 1)
                dve.wait_ge(gate_steps, 4 * t + 3)
                if later(t):
                    dve.wait_ge(gated_turned, t - 1)
                dve.tensor_tensor(gated[:, s, 0:GATED * RANK].rearrange("p (e r) -> p e r", r=RANK),
                                  gates[:, s, :, None].to_broadcast([P, GATED, RANK]),
                                  mid[:, s, None, :].to_broadcast([P, GATED, RANK]), ALU.mult).then_inc(gate_steps, 1)

            def gated_to_lo(t, s):
                dve.wait_ge(gated_hi, t + 1)
                dve.tensor_tensor(gated_pair[:, s, LO, :], ps_g[:, s, :], gated_pair[:, s, HI, :], ALU.subtract).then_inc(gated_split, 1)

            def finish(t, s):
                dve.wait_ge(summed, t + 1)
                if later(t):
                    dve.wait_ge(stored[s], 8 * t - 8 * s)
                dve.scalar_tensor_tensor(out_tile[:, s:s + 1, :], ps_b[:, s:s + 1, 0:D], 1.0 / WS, residual[:, bass.ds(t, 1), :],
                                         ALU.mult, ALU.add).then_inc(out_made, 1)

            skewed(dve, TILES, (3, gate), (0, add_x), (1, norm), (2, turned_lo), (2, highest), (3, gated_to_lo), (4, finish))

        @block.tensor
        def _(pe):
            pe.wait_ge(prep_g, 8)
            pe.wait_ge(prep_v, 4)

            def turn_back(t, s):
                pe.wait_ge(xb_made, t + 1)
                if later(t):
                    pe.wait_ge(h_steps, 3 * t - 5)
                for c in range(DC):
                    mm = pe.transpose(ps_x[:, s, c * P:(c + 1) * P], xb[:, s, c, :], ident[:, :])
                mm.then_inc(turned_back, 1)

            def turn(t, s):
                pe.wait_ge(x3_made, t + 1)
                if later(t):
                    pe.wait_ge(x3_split, t - 1)
                for c in range(DC):
                    mm = pe.transpose(ps_t[:, s, c * P:(c + 1) * P], x3[:, s, c * P:(c + 1) * P], ident[:, :])
                mm.then_inc(turned, 1)

            def mix(t, s):
                pe.wait_ge(x3_split, t + 1)
                if later(t):
                    pe.wait_ge(gate_steps, 4 * t - 4)
                pe.matmul(ps_m[:, s, :], ones[:, :], b_rows[:, D:D + MIX], start=True, stop=False)
                split_matmuls(pe, ps_m[:, s, :], lambda a, c: x3_pair[:, s, a, c, :], lambda b, c: mix_pair[:, b, c, :], DC,
                              first_start=False).then_inc(mixed, 1)

            def base(t, s):
                if later(t):
                    pe.wait_ge(out_made, t - 1)
                pe.matmul(ps_b[:, s, 0:D], ones[:, :], b_rows[:, 0:D], start=True, stop=False, skip_group_check=True)
                for n, (c, a, b) in enumerate((c, a, b) for c in range(DC) for a, b in ((HI, HI), (HI, LO), (LO, HI))):
                    mm = pe.matmul(ps_b[:, s, 0:D], x3_pair[:, s, a, c, :], base_pair[:, b, c, :], start=False, stop=False,
                                   skip_group_check=True)
                mm.then_inc(based, 1)

            def turn_gated(t, s):
                pe.wait_ge(gate_steps, 4 * t + 4)
                if later(t):
                    pe.wait_ge(gated_split, t - 1)
                pe.transpose(ps_g[:, s, :], gated[:, s, :], ident[:, :]).then_inc(gated_turned, 1)

            def add_lora(t, s):
                pe.wait_ge(gated_split, t + 1)
                split_matmuls(pe, ps_b[:, s, 0:D], lambda a, _: gated_pair[:, s, a, :], lambda b, _: lora_pair[:, b, :], 1,
                              first_start=False, check=False).then_inc(summed, 1)

            skewed(pe, TILES, (4, add_lora), (3, turn_gated), (0, turn_back), (1, turn), (2, mix), (3, base))


def vit_tower(nc, d):
    keep = {
        "queue": nc.dram_tensor("queue", (QUEUE_TILES * ROWS, D), F32, kind="Internal").ap(),
        "answers": nc.dram_tensor("answers", (QUEUE_TILES * ROWS, D), F32, kind="Internal").ap(),
    }

    def hold(ctx, name, shape, dt=F32):
        keep[name] = ctx.enter_context(nc.sbuf_tensor(name, shape, dt))

    with ExitStack() as whole:
        hold(whole, "residual", [P, TILES, D])
        hold(whole, "chan_a", [P, 2, DC, NPAD], F16)
        hold(whole, "weights", [P, TOP, TILES])
        hold(whole, "places", [P, TOP, TILES], I32)
        hold(whole, "bounds", [P, 2, EXPERTS], I32)
        hold(whole, "bias_sum", [P, LAYERS + 1, DC])
        embed_and_norm(nc, d, keep)
        with ExitStack() as early:
            hold(early, "chan_b", [P, 2, DC, NPAD], F16)
            channel_attention(nc, d, keep)
            hold(early, "rows", [P, TILES, D])
            project_and_route(nc, d, keep)
        experts(nc, d, keep)
        hold(whole, "state", [P, DC, NPAD])
        gather_and_norm(nc, d, keep)
        linear_attention_layers(nc, d, keep)
        final_block(nc, d, keep)




def lay_out(x, L0_tok_W, L0_tok_b, L0_attn_norm_w, L0_attn_norm_b, L0_attn_qkv_w, L0_attn_qkv_b, L0_attn_proj_w,
            L0_attn_proj_b, L0_ffn_W_gate, L0_ffn_W_in, L0_ffn_b_in, L0_ffn_W_out, L0_ffn_b_out, L1_attn_Wqkv,
            L1_attn_bqkv, L1_attn_Wproj, L1_attn_bproj, L1_ffn_base_w, L1_ffn_base_b, L1_ffn_lora_A, L1_ffn_lora_B,
            L1_ffn_router_w, L1_ffn_router_b):
    def rows(w):
        return w.reshape(-1, P, w.shape[-1]).transpose(1, 0, 2)

    patches = x.reshape(IMAGES, CHANS, SIDE, PATCH, SIDE, PATCH).transpose(0, 2, 4, 1, 3, 5).reshape(N, FEAT)
    padded = np.zeros((NPAD, FEAT), x.dtype)
    padded[:N] = patches
    return {
        "patches": padded.reshape(TILES, P, FC, P).transpose(0, 3, 2, 1).reshape(TILES, P, FC * P),
        "tok_w": rows(L0_tok_W.T), "tok_b": L0_tok_b,
        "norm_w": L0_attn_norm_w, "norm_b": L0_attn_norm_b,
        "qkv0_w": rows(L0_attn_qkv_w.T), "qkv0_b": L0_attn_qkv_b.reshape(1, -1),
        "qkv0_bcol": L0_attn_qkv_b.reshape(-1, P).T,
        "proj0_w": rows(L0_attn_proj_w.T), "proj0_b": L0_attn_proj_b.reshape(1, -1),
        "gate_w": rows(L0_ffn_W_gate),
        "in_w": np.stack([rows(w) for w in L0_ffn_W_in]), "in_b": L0_ffn_b_in.reshape(-1, 8, P).transpose(2, 0, 1),
        "out_w": np.stack([rows(w) for w in L0_ffn_W_out]), "out_b": L0_ffn_b_out.reshape(1, -1),
        "qkv1_w": np.stack([rows(w.T) for w in L1_attn_Wqkv]), "qkv1_b": L1_attn_bqkv,
        "q1_bcol": L1_attn_bqkv[:, :D].reshape(-1, DC, P).transpose(2, 0, 1),
        "proj1_w": np.stack([rows(w.T) for w in L1_attn_Wproj]),
        "proj1_bcol": L1_attn_bproj.reshape(-1, DC, P).transpose(2, 0, 1),
        "base_w": rows(L1_ffn_base_w.T), "base_b": L1_ffn_base_b.reshape(1, -1),
        "lora_a": rows(L1_ffn_lora_A), "lora_b": L1_ffn_lora_B.reshape(-1, D),
        "router_w": rows(L1_ffn_router_w.T), "router_b": L1_ffn_router_b.reshape(1, -1),
    }


def kernel(**inputs):
    import concourse.bacc as bacc
    from concourse.bass_utils import run_bass_kernel_spmd

    nc = bacc.Bacc("TRN2", target_bir_lowering=False, num_devices=1)
    arrays, d = {}, {}
    for name, a in lay_out(**{k: np.asarray(v) for k, v in inputs.items()}).items():
        a = np.ascontiguousarray(a)
        arrays[f"in_{name}_dram"] = a
        d[name] = nc.dram_tensor(f"in_{name}_dram", a.shape, mybir.dt.from_np(a.dtype), kind="ExternalInput").ap()
    d["out"] = nc.dram_tensor("out_dram", (N, D), F32, kind="ExternalOutput").ap()
    vit_tower(nc, d)
    r = run_bass_kernel_spmd(nc, [arrays], core_ids=[0])
    return r.results[0]["out_dram"].reshape(IMAGES, TOK, D)
```

```python
from contextlib import ExitStack

import numpy as np

import concourse.bass as bass
from concourse import mybir

F32 = mybir.dt.float32
F16 = mybir.dt.float16
I32 = mybir.dt.int32
ACT = mybir.ActivationFunctionType
ALU = mybir.AluOpType
AX = mybir.AxisListType

P = 128
IMAGES, SIDE, PATCH, CHANS = 64, 7, 16, 3
TOK = SIDE * SIDE
N = IMAGES * TOK
TILES = -(-N // P)
NPAD = TILES * P
FEAT = CHANS * PATCH * PATCH
FC = FEAT // P
D = 256
DC = D // P
PAIRS = IMAGES // 2
PT = 2 * TOK
EPS = 1e-5
WS = 256.0
HI, LO = 0, 1
EXPERTS, TOP, HIDDEN = 8, 2, 1024
MC = HIDDEN // P
ROWS = 2 * P
LEAST_TILES = 2
EXPERT_TILES = (TOP * N + EXPERTS * LEAST_TILES * ROWS) // ROWS
MOST_OF_ONE = -(-N // ROWS)
QUEUE_TILES = EXPERT_TILES + MOST_OF_ONE + 1
SURE_TILES = TOP * N // ROWS
ZERO_ROWS = 4
ZERO_PART = P * ZERO_ROWS


class Prepared:
    pass


def in_loop(eng, first, last, step):
    if first < last and first % 2:
        step(first, 1)
        first += 1
    rounds = (last - first) // 2
    if rounds >= 2:
        with eng.Fori(0, rounds) as j:
            step(first + 2 * j, 0)
            step(first + 2 * j + 1, 1)
        first += 2 * rounds
    for i in range(first, last):
        step(i, i % 2)


def skewed(eng, n, *stages):
    deepest = max(lag for lag, _ in stages)

    def step(i, parity):
        for lag, f in stages:
            if not isinstance(i, int) or 0 <= i - lag < n:
                f(i - lag, (parity - lag) % 2)

    peeled = deepest + SLOTS
    for i in range(peeled):
        step(i, i % 2)
    in_loop(eng, peeled, n, step)
    for i in range(n, n + deepest):
        step(i, i % 2)


def wait_apart(eng, sem, value, passed):
    eng.wait_ge(sem, value)
    eng.sem_inc(passed, 1)


SLOTS = 2


def free(i):
    return i + 1


def made(i):
    return i + 1 + SLOTS


def landed(i, parity):
    return 8 * i + 16 - 8 * parity


def split_matmuls(pe, out, left, right, chunks, first_start=True, check=True):
    terms = [(c, a, b) for c in range(chunks) for a, b in ((HI, HI), (HI, LO), (LO, HI))]
    for n, (c, a, b) in enumerate(terms):
        mm = pe.matmul(out, left(a, c), right(b, c), start=first_start and n == 0, stop=n == len(terms) - 1,
                       skip_group_check=not check)
    return mm


def embed_and_norm(nc, d, keep):
    residual, normed_t = keep["residual"], keep["chan_a"]
    with ExitStack() as ctx:
        def sb(name, shape, dt=F32):
            return ctx.enter_context(nc.sbuf_tensor(name, shape, dt))

        def sem(name):
            return ctx.enter_context(nc.semaphore(name))

        patches = sb("patches", [P, 2, FC, P])
        patches_pair = sb("patches_pair", [P, 2, 2, FC, P], F16)
        w_raw = sb("tok_w_raw", [P, FC, D])
        w_pair = sb("tok_w_pair", [P, 2, FC, D], F16)
        tok_b = sb("tok_b_all", [P, D])
        norm_w = sb("norm_w_all", [P, D])
        norm_b = sb("norm_b_all", [P, D])
        ident = sb("ident_a", [P, P])
        eps = sb("eps_a", [P, 1])
        stats = sb("stats", [P, 2, 6])
        mean_var = sb("mean_var", [P, 2, 2])
        std = sb("std", [P, 2])
        rstd = sb("rstd", [P, 2])
        x0 = sb("x0", [P, 2, D])
        stats2 = sb("stats2", [P, 2, 6])
        mean_var2 = sb("mean_var2", [P, 2, 2])
        std2 = sb("std2", [P, 2])
        rstd2 = sb("rstd2", [P, 2])
        n0 = sb("n0", [P, 2, D])
        n1 = sb("n1", [P, 2, D])
        ps_embed = ctx.enter_context(nc.psum_tensor("ps_embed", [P, 2, 512], F32))
        ps_t = ctx.enter_context(nc.psum_tensor("ps_normed_t", [P, 2, 512], F32))

        consts_loaded, w_loaded = sem("consts_loaded"), sem("w_loaded")
        patches_loaded = [sem("patches_loaded0"), sem("patches_loaded1")]
        w_hi, w_split, ident_made = sem("w_hi"), sem("w_split"), sem("ident_made")
        patches_hi, patches_split = sem("patches_hi"), sem("patches_split")
        embedded, h_made, h_stats = sem("embedded"), sem("h_made"), sem("h_stats")
        std_made, rstd_made, x0_made, x0_stats = sem("std_made"), sem("rstd_made"), sem("x0_made"), sem("x0_stats")
        residual_made, std2_made, n_steps = sem("residual_made"), sem("std2_made"), sem("n_steps")
        transposed, t_hi, t_split, passed = sem("transposed"), sem("t_hi"), sem("t_split"), sem("a_passed")
        block = ctx.enter_context(nc.Block())

        @block.sync
        def _(sp):
            sp.dma_start(w_raw[:, :, :], d["tok_w"]).then_inc(w_loaded, 16)

            def load(t, s):
                sp.wait_ge(patches_split, free(t))
                sp.dma_start(patches[:, s:s + 1, :, :].rearrange("p a c t -> p (a c t)"),
                             d["patches"][bass.ds(t, 1)].rearrange("a p n -> (a p) n")).then_inc(patches_loaded[s], 16)

            in_loop(sp, 0, TILES, load)

        @block.scalar
        def _(act):
            act.dma_start(tok_b[:, :], d["tok_b"].partition_broadcast(P)).then_inc(consts_loaded, 16)
            act.dma_start(norm_w[:, :], d["norm_w"].partition_broadcast(P)).then_inc(consts_loaded, 16)
            act.dma_start(norm_b[:, :], d["norm_b"].partition_broadcast(P)).then_inc(consts_loaded, 16)
            act.wait_ge(w_loaded, 16)
            act.activation(w_pair[:, HI, :, :], w_raw[:, :, :], ACT.Copy, scale=WS).then_inc(w_hi, 1)

            def hi(t, s):
                act.wait_ge(patches_loaded[s], landed(t, s))
                act.wait_ge(embedded, free(t))
                act.activation(patches_pair[:, s, HI, :, :], patches[:, s, :, :], ACT.Copy).then_inc(patches_hi, 1)

            def root(t, s):
                act.wait_ge(h_stats, 2 * t + 2)
                act.activation(std[:, s:s + 1], mean_var[:, s, 1:2], ACT.Sqrt, bias=eps[:, 0:1]).then_inc(std_made, 1)

            def root2(t, s):
                act.wait_ge(x0_stats, 2 * t + 2)
                act.activation(std2[:, s:s + 1], mean_var2[:, s, 1:2], ACT.Sqrt, bias=eps[:, 0:1]).then_inc(std2_made, 1)

            def out_hi(t, s):
                act.wait_ge(transposed, made(t))
                act.activation(normed_t[:, HI, :, bass.ds(t * P, P)],
                               ps_t[:, s, 0:D].rearrange("p (c t) -> p c t", c=DC), ACT.Copy).then_inc(t_hi, 1)

            act.wait_ge(ident_made, 3)
            skewed(act, TILES, (7, out_hi), (0, hi), (2, root), (4, root2))

        @block.gpsimd
        def _(pool):
            pool.memset(ident[:, :], 0.0).then_inc(ident_made, 1)
            pool.wait_ge(ident_made, 1)
            pool.affine_select(out=ident[:, :], in_=ident[:, :], compare_op=ALU.not_equal, fill=1.0,
                               base=0, pattern=[[-1, P]], channel_multiplier=1).then_inc(ident_made, 1)
            pool.memset(eps[:, :], EPS).then_inc(ident_made, 1)
            pool.sem_inc(patches_split, SLOTS)

            def lo(t, s):
                pool.wait_ge(patches_hi, t + 1)
                pool.tensor_tensor(patches_pair[:, s, LO, :, :], patches[:, s, :, :], patches_pair[:, s, HI, :, :],
                                   ALU.subtract).then_inc(patches_split, 1)

            def add_x0(t, s):
                pool.wait_ge(x0_made, t + 1)
                row = residual[:, bass.ds(t, 1), :]
                pool.tensor_tensor(row, row, x0[:, s:s + 1, :], ALU.add).then_inc(residual_made, 1)

            skewed(pool, TILES, (4, add_x0), (0, lo))

        @block.vector
        def _(dve):
            dve.sem_inc(h_made, SLOTS)
            dve.sem_inc(t_split, SLOTS)
            dve.wait_ge(w_hi, 1)
            dve.scalar_tensor_tensor(w_pair[:, LO, :, :].rearrange("p c n -> p (c n)"), w_raw[:, :, :].rearrange("p c n -> p (c n)"), WS,
                                     w_pair[:, HI, :, :].rearrange("p c n -> p (c n)"), ALU.mult, ALU.subtract).then_inc(w_split, 1)
            dve.wait_ge(consts_loaded, 48)

            def h_and_stats(t, s):
                dve.wait_ge(embedded, made(t))
                dve.scalar_tensor_tensor(residual[:, bass.ds(t, 1), :], ps_embed[:, s:s + 1, 0:D], 1.0 / WS, tok_b[:, None, :],
                                         ALU.mult, ALU.add).then_inc(h_made, 1)
                wait_apart(dve, h_made, made(t), passed)
                dve.bn_stats(stats[:, s, :], residual[:, bass.ds(t, 1), :]).then_inc(h_stats, 1)
                wait_apart(dve, h_stats, 2 * t + 1, passed)
                dve.bn_aggr(mean_var[:, s, :], stats[:, s, :]).then_inc(h_stats, 1)

            def norm_and_stats(t, s):
                dve.wait_ge(std_made, t + 1)
                dve.reciprocal(rstd[:, s:s + 1], std[:, s:s + 1]).then_inc(rstd_made, 1)
                dve.wait_ge(rstd_made, t + 1)
                if not isinstance(t, int) or t >= 2:
                    dve.wait_ge(residual_made, t - 1)
                dve.tensor_scalar(x0[:, s:s + 1, :], residual[:, bass.ds(t, 1), :], mean_var[:, s, 0:1], rstd[:, s:s + 1],
                                  ALU.subtract, ALU.mult).then_inc(x0_made, 1)
                wait_apart(dve, x0_made, t + 1, passed)
                dve.bn_stats(stats2[:, s, :], x0[:, s, :]).then_inc(x0_stats, 1)
                wait_apart(dve, x0_stats, 2 * t + 1, passed)
                dve.bn_aggr(mean_var2[:, s, :], stats2[:, s, :]).then_inc(x0_stats, 1)

            def norm2(t, s):
                dve.wait_ge(std2_made, t + 1)
                dve.reciprocal(rstd2[:, s:s + 1], std2[:, s:s + 1]).then_inc(n_steps, 1)
                dve.wait_ge(n_steps, 4 * t + 1)
                dve.tensor_scalar(n0[:, s, :], x0[:, s, :], mean_var2[:, s, 0:1], rstd2[:, s:s + 1],
                                  ALU.subtract, ALU.mult).then_inc(n_steps, 1)
                dve.wait_ge(n_steps, 4 * t + 2)
                dve.tensor_tensor(n0[:, s, :], n0[:, s, :], norm_w[:, :], ALU.mult).then_inc(n_steps, 1)
                dve.wait_ge(n_steps, 4 * t + 3)
                dve.wait_ge(transposed, free(t))
                dve.tensor_tensor(n1[:, s, :], n0[:, s, :], norm_b[:, :], ALU.add).then_inc(n_steps, 1)

            def out_lo(t, s):
                dve.wait_ge(t_hi, t + 1)
                dve.tensor_tensor(normed_t[:, LO, :, bass.ds(t * P, P)],
                                  ps_t[:, s, 0:D].rearrange("p (c t) -> p c t", c=DC),
                                  normed_t[:, HI, :, bass.ds(t * P, P)], ALU.subtract).then_inc(t_split, 1)

            skewed(dve, TILES, (1, h_and_stats), (2, norm_and_stats), (3, norm2), (5, out_lo))

        @block.tensor
        def _(pe):
            pe.sem_inc(embedded, SLOTS)
            pe.sem_inc(transposed, SLOTS)
            pe.wait_ge(w_split, 1)
            pe.wait_ge(ident_made, 2)

            def embed(t, s):
                pe.wait_ge(patches_split, made(t))
                pe.wait_ge(h_made, free(t))
                split_matmuls(pe, ps_embed[:, s, 0:D], lambda a, c: patches_pair[:, s, a, c, :],
                              lambda b, c: w_pair[:, b, c, :], FC).then_inc(embedded, 1)

            def turn(t, s):
                pe.wait_ge(n_steps, 4 * t + 4)
                pe.wait_ge(t_split, free(t))
                for c in range(DC):
                    mm = pe.transpose(ps_t[:, s, c * P:(c + 1) * P], n1[:, s, c * P:(c + 1) * P], ident[:, :])
                mm.then_inc(transposed, 1)

            skewed(pe, TILES, (1, embed), (5, turn))


def channel_attention(nc, d, keep):
    normed_t, attended_t = keep["chan_a"], keep["chan_b"]
    scale = 1.0 / float(np.sqrt(TOK))
    with ExitStack() as ctx:
        def sb(name, shape, dt=F32):
            return ctx.enter_context(nc.sbuf_tensor(name, shape, dt))

        def psum(name, shape, dt=F32):
            return ctx.enter_context(nc.psum_tensor(name, shape, dt))

        def sem(name):
            return ctx.enter_context(nc.semaphore(name))

        w_raw = sb("qkv_w_raw", [P, DC, 3 * D])
        w_pair = sb("qkv_w_pair", [P, 2, DC, 3 * D], F16)
        bias_raw = sb("qk_b_raw", [33, 2 * D])
        bias_hi = sb("qk_b_hi", [33, 2 * D], F16)
        bias_rows = sb("qk_bias_rows", [P, 2 * D], F16)
        ones = sb("ones_b", [P, P], F16)
        v_b = sb("v_b", [P, 6])
        v_bs = sb("v_b_scaled", [P, DC])
        ident = sb("ident_b", [P, P])
        own = sb("own_image", [PT, 2])
        q_pair = sb("q_pair", [PT, 2, 2, 2, D], F16)
        k_pair = sb("k_pair", [PT, 2, 2, D], F16)
        v_pair = sb("v_pair", [P, 2, 2, DC, PT], F16)
        neg_max = sb("neg_max", [P, 2, DC])
        neg_scaled = sb("neg_scaled", [P, 2, DC])
        exps = sb("exps", [P, 2, DC, D])
        sums = sb("sums", [P, 2, DC])
        sums_s = sb("sums_scaled", [P, 2, DC])
        inv = sb("inv_sums", [P, 2, DC])
        et_pair = sb("exps_t_pair", [P, 2, 2, DC, D], F16)
        zeros = sb("zeros", [P, ZERO_ROWS * D])
        queue_rows, answer_rows = [keep[name].rearrange("(g p r) n -> g p (r n)", p=P, r=ZERO_ROWS) for name in ("queue", "answers")]
        zeros_made, cleared = sem("zeros_made"), sem("queue_cleared")
        ps_qk = psum("ps_qk", [P, 512])
        ps_v = psum("ps_v", [P, 512])
        ps_s = psum("ps_scores", [P, 2, DC, D])
        ps_e = psum("ps_exps_t", [P, 2, DC, D])
        ps_a = psum("ps_attended", [P, 2, 512])

        loaded, prep = sem("qkv_loaded"), sem("qkv_prep")
        w_hi, prep_v, prep_g = sem("qkv_w_hi"), sem("qkv_prep_v"), sem("qkv_prep_g")
        projected_qk, projected_v = sem("projected_qk"), sem("projected_v")
        qk_hi, qk_split, v_hi, v_split = sem("qk_hi"), sem("qk_split"), sem("v_hi"), sem("v_split")
        scored, max_steps, exp_steps = sem("scored"), sem("max_steps"), sem("exp_steps")
        turned, et_hi, et_split = sem("turned"), sem("et_hi"), sem("et_split")
        inv_steps, attended, a_hi, a_split = sem("inv_steps"), sem("attended"), sem("a_hi"), sem("a_split")
        block = ctx.enter_context(nc.Block())

        def images_of(f):
            return (lambda p, s: f(2 * p, 0)), (lambda p, s: f(2 * p + 1, 1))

        @block.sync
        def _(sp):
            sp.dma_start(w_raw[:, :, :], d["qkv0_w"]).then_inc(loaded, 16)
            sp.dma_start(bias_raw[0:1, :], d["qkv0_b"][:, 0:2 * D]).then_inc(loaded, 16)
            sp.dma_start(bias_raw[32:33, :], d["qkv0_b"][:, 0:2 * D]).then_inc(loaded, 16)
            sp.dma_start(v_b[:, :], d["qkv0_bcol"]).then_inc(loaded, 16)
            sp.wait_ge(zeros_made, 1)
            parts = 0
            for rows, first, last in ((queue_rows, 0, EXPERT_TILES + 1), (answer_rows, SURE_TILES, EXPERT_TILES)):
                for g in range(first * ROWS // ZERO_PART, -(-last * ROWS // ZERO_PART)):
                    sp.dma_start(rows[g], zeros[:, :]).then_inc(cleared, 16)
                    parts += 1
            sp.wait_ge(cleared, 16 * parts)

        @block.gpsimd
        def _(pool):
            pool.memset(ident[:, :], 0.0).then_inc(prep_g, 1)
            pool.memset(zeros[:, :], 0.0).then_inc(zeros_made, 1)
            pool.memset(own[:, :], 1.0 / WS).then_inc(prep_g, 1)
            pool.memset(ones[:, :], 1.0).then_inc(prep_g, 1)
            pool.wait_ge(prep_g, 2)
            pool.affine_select(out=ident[:, :], in_=ident[:, :], compare_op=ALU.not_equal, fill=1.0,
                               base=0, pattern=[[-1, P]], channel_multiplier=1).then_inc(prep_g, 1)
            pool.affine_select(out=own[:, 0:1], in_=own[:, 0:1], compare_op=ALU.is_ge, fill=0.0,
                               base=TOK - 1, pattern=[[0, 1]], channel_multiplier=-1).then_inc(prep_g, 1)
            pool.affine_select(out=own[:, 1:2], in_=own[:, 1:2], compare_op=ALU.is_ge, fill=0.0,
                               base=-TOK, pattern=[[0, 1]], channel_multiplier=1).then_inc(prep_g, 1)

        @block.scalar
        def _(act):
            act.wait_ge(loaded, 64)
            act.activation(w_pair[:, HI, :, :], w_raw[:, :, :], ACT.Copy, scale=WS).then_inc(w_hi, 1)
            act.wait_ge(prep_v, 1)
            act.activation(bias_rows[0:1, :], bias_raw[0:1, :], ACT.Copy, scale=WS).then_inc(w_hi, 1)
            act.activation(bias_hi[32:33, :], bias_raw[32:33, :], ACT.Copy, scale=WS).then_inc(w_hi, 1)
            act.activation(v_bs[:, :], v_b[:, 4:6], ACT.Copy, scale=WS).then_inc(w_hi, 1)
            act.wait_ge(w_hi, 4)
            act.wait_ge(prep_g, 6)

            def project_hi(p, s):
                act.wait_ge(projected_qk, p + 1)
                if not isinstance(p, int) or p >= 2:
                    act.wait_ge(scored, 2 * p - 2)
                for image in (0, 1):
                    act.activation(q_pair[:, s, HI, image, :], ps_qk[0:PT, 0:D], ACT.Copy, scale=own[:, image:image + 1])
                act.activation(k_pair[:, s, HI, :], ps_qk[0:PT, D:2 * D], ACT.Copy, scale=1.0 / WS).then_inc(qk_hi, 1)
                act.wait_ge(projected_v, p + 1)
                if not isinstance(p, int) or p >= 2:
                    act.wait_ge(attended, 2 * p - 2)
                for c in range(DC):
                    out = act.activation(v_pair[:, s, HI, c, :], ps_v[:, c * PT:(c + 1) * PT], ACT.Identity, bias=v_bs[:, c:c + 1])
                out.then_inc(v_hi, 1)

            def exp(n, s):
                act.wait_ge(max_steps, 2 * n + 2)
                if not isinstance(n, int) or n >= 2:
                    act.wait_ge(turned, n - 1)
                for c in range(DC):
                    act.activation(exps[:, s, c, :], ps_s[:, s, c, :], ACT.Exp, bias=neg_scaled[:, s, c:c + 1], scale=scale,
                                   accum_out=sums[:, s, c:c + 1]).then_inc(exp_steps, 1)

            def turned_hi(n, s):
                act.wait_ge(turned, n + 1)
                if not isinstance(n, int) or n >= 2:
                    act.wait_ge(attended, n - 1)
                act.activation(et_pair[:, s, HI, :, :], ps_e[:, s, :, :], ACT.Copy).then_inc(et_hi, 1)

            def attended_hi(n, s):
                act.wait_ge(attended, n + 1)
                act.wait_ge(inv_steps, 2 * n + 2)
                for c in range(DC):
                    out = act.activation(attended_t[:, HI, c, bass.ds(n * TOK, TOK)], ps_a[:, s, c * TOK:(c + 1) * TOK], ACT.Copy,
                                         scale=inv[:, s, c:c + 1])
                out.then_inc(a_hi, 1)

            exp0, exp1 = images_of(exp)
            turned_hi0, turned_hi1 = images_of(turned_hi)
            attended_hi0, attended_hi1 = images_of(attended_hi)
            skewed(act, PAIRS, (2, turned_hi0), (2, turned_hi1), (1, exp0), (2, attended_hi0), (1, exp1), (2, attended_hi1), (0, project_hi))

        @block.vector
        def _(dve):
            dve.memset(bias_rows[:, :], 0.0).then_inc(prep_v, 1)
            dve.wait_ge(w_hi, 4)
            dve.wait_ge(loaded, 64)
            dve.scalar_tensor_tensor(w_pair[:, LO, :, :].rearrange("p c n -> p (c n)"), w_raw[:, :, :].rearrange("p c n -> p (c n)"), WS,
                                     w_pair[:, HI, :, :].rearrange("p c n -> p (c n)"), ALU.mult, ALU.subtract).then_inc(prep_v, 1)
            dve.wait_ge(prep_v, 1)
            dve.scalar_tensor_tensor(bias_rows[32:33, :], bias_raw[32:33, :], WS, bias_hi[32:33, :],
                                     ALU.mult, ALU.subtract).then_inc(prep_v, 1)
            dve.wait_ge(prep_g, 6)

            def project_lo(p, s):
                dve.wait_ge(qk_hi, p + 1)
                for image in (0, 1):
                    dve.scalar_tensor_tensor(q_pair[:, s, LO, image, :], ps_qk[0:PT, 0:D], own[:, image:image + 1],
                                             q_pair[:, s, HI, image, :], ALU.mult, ALU.subtract)
                dve.scalar_tensor_tensor(k_pair[:, s, LO, :], ps_qk[0:PT, D:2 * D], 1.0 / WS, k_pair[:, s, HI, :],
                                         ALU.mult, ALU.subtract).then_inc(qk_split, 1)
                dve.wait_ge(v_hi, p + 1)
                for c in range(DC):
                    out = dve.scalar_tensor_tensor(v_pair[:, s, LO, c, :], ps_v[:, c * PT:(c + 1) * PT], v_bs[:, c:c + 1],
                                                   v_pair[:, s, HI, c, :], ALU.add, ALU.subtract)
                out.then_inc(v_split, 1)

            def row_max(n, s):
                dve.wait_ge(scored, n + 1)
                if not isinstance(n, int) or n >= 2:
                    dve.wait_ge(exp_steps, 2 * n - 2)
                dve.tensor_reduce(neg_max[:, s, :], ps_s[:, s, :, :], AX.X, ALU.max).then_inc(max_steps, 1)
                dve.wait_ge(max_steps, 2 * n + 1)
                dve.tensor_scalar(neg_scaled[:, s, :], neg_max[:, s, :], -scale, None, ALU.mult).then_inc(max_steps, 1)

            def turned_lo(n, s):
                dve.wait_ge(et_hi, n + 1)
                dve.tensor_tensor(et_pair[:, s, LO, :, :], ps_e[:, s, :, :], et_pair[:, s, HI, :, :],
                                  ALU.subtract).then_inc(et_split, 1)

            def inverse(n, s):
                dve.wait_ge(exp_steps, 2 * n + 2)
                if not isinstance(n, int) or n >= 2:
                    dve.wait_ge(a_hi, n - 1)
                dve.tensor_scalar(sums_s[:, s, :], sums[:, s, :], WS, None, ALU.mult).then_inc(inv_steps, 1)
                dve.wait_ge(inv_steps, 2 * n + 1)
                dve.reciprocal(inv[:, s, :], sums_s[:, s, :]).then_inc(inv_steps, 1)

            def attended_lo(n, s):
                dve.wait_ge(a_hi, n + 1)
                for c in range(DC):
                    out = dve.scalar_tensor_tensor(attended_t[:, LO, c, bass.ds(n * TOK, TOK)], ps_a[:, s, c * TOK:(c + 1) * TOK],
                                                   inv[:, s, c:c + 1], attended_t[:, HI, c, bass.ds(n * TOK, TOK)],
                                                   ALU.mult, ALU.subtract)
                out.then_inc(a_split, 1)

            row_max0, row_max1 = images_of(row_max)
            inverse0, inverse1 = images_of(inverse)
            turned_lo0, turned_lo1 = images_of(turned_lo)
            attended_lo0, attended_lo1 = images_of(attended_lo)
            skewed(dve, PAIRS, (2, turned_lo0), (1, row_max0), (2, turned_lo1), (1, row_max1), (2, attended_lo0), (1, inverse0), (2, attended_lo1), (1, inverse1), (0, project_lo))

        @block.tensor
        def _(pe):
            pe.wait_ge(prep_v, 3)
            pe.wait_ge(prep_g, 6)

            def project(p, s):
                if not (isinstance(p, int) and p == 0):
                    pe.wait_ge(qk_split, p)
                    pe.wait_ge(v_split, p)
                first = True
                for c in range(DC):
                    for a in (HI, LO):
                        x = normed_t[:, a, c, bass.ds(p * PT, PT)]
                        for b in ((HI, LO) if a == HI else (HI,)):
                            pe.matmul(ps_qk[0:PT, :], x, w_pair[:, b, c, 0:2 * D], start=first, stop=False)
                            for m in range(DC):
                                v = pe.matmul(ps_v[:, m * PT:(m + 1) * PT], w_pair[:, b, c, 2 * D + m * P:2 * D + (m + 1) * P], x,
                                              start=first and m == 0, stop=(c == DC - 1 and a == LO), skip_group_check=True)
                            first = False
                v.then_inc(projected_v, 1)
                pe.matmul(ps_qk[0:PT, :], ones[:, 0:PT], bias_rows[:, :], start=False, stop=True).then_inc(projected_qk, 1)

            def score(p, image, pair_slot):
                n, s = 2 * p + image, image
                if image == 0:
                    pe.wait_ge(qk_split, p + 1)
                if not isinstance(n, int) or n >= 2:
                    pe.wait_ge(exp_steps, 2 * n - 2)
                for m in range(DC):
                    mm = split_matmuls(pe, ps_s[:, s, m, :], lambda a, c: q_pair[:, pair_slot, a, image, m * P:(m + 1) * P],
                                       lambda b, c: k_pair[:, pair_slot, b, :], 1, first_start=(m == 0), check=False)
                mm.then_inc(scored, 1)

            def turn(n, s):
                pe.wait_ge(exp_steps, 2 * n + 2)
                if not isinstance(n, int) or n >= 2:
                    pe.wait_ge(et_split, n - 1)
                for c in range(DC):
                    for m in range(DC):
                        mm = pe.transpose(ps_e[:, s, c, m * P:(m + 1) * P], exps[:, s, m, c * P:(c + 1) * P], ident[:, :])
                mm.then_inc(turned, 1)

            def attend(p, image, pair_slot):
                n, s = 2 * p + image, image
                pe.wait_ge(et_split, n + 1)
                if image == 0:
                    pe.wait_ge(v_split, p + 1)
                if not isinstance(n, int) or n >= 2:
                    pe.wait_ge(a_split, n - 1)
                for m in range(DC):
                    mm = split_matmuls(pe, ps_a[:, s, m * TOK:(m + 1) * TOK],
                                       lambda a, c: et_pair[:, s, a, c, m * P:(m + 1) * P],
                                       lambda b, c: v_pair[:, pair_slot, b, c, image * TOK:(image + 1) * TOK], DC,
                                       first_start=(m == 0), check=False)
                mm.then_inc(attended, 1)

            def score0(p, s):
                score(p, 0, s)

            def score1(p, s):
                score(p, 1, s)

            def attend0(p, s):
                attend(p, 0, s)

            def attend1(p, s):
                attend(p, 1, s)

            turn0, turn1 = images_of(turn)
            skewed(pe, PAIRS, (1, score0), (1, score1), (2, attend0), (2, attend1), (0, project), (1, turn0), (1, turn1))


def project_and_route(nc, d, keep):
    residual, attended_t, x1 = keep["residual"], keep["chan_b"], keep["rows"]
    weights, places, bounds, queue = keep["weights"], keep["places"], keep["bounds"], keep["queue"]
    with ExitStack() as ctx:
        def sb(name, shape, dt=F32):
            return ctx.enter_context(nc.sbuf_tensor(name, shape, dt))

        def psum(name, shape, dt=F32):
            return ctx.enter_context(nc.psum_tensor(name, shape, dt))

        def sem(name):
            return ctx.enter_context(nc.semaphore(name))

        w_raw = sb("proj_w_raw", [P, DC, D])
        w_pair = sb("proj_w_pair", [P, 2, DC, D], F16)
        g_raw = sb("gate_w_raw", [P, DC, EXPERTS])
        g_pair = sb("gate_w_pair", [P, 2, DC, EXPERTS], F16)
        bias_raw = sb("proj_b_raw", [33, D])
        bias_hi = sb("proj_b_hi", [33, D], F16)
        bias_rows = sb("proj_bias_rows", [P, D], F16)
        ones = sb("ones_c", [P, P], F16)
        before = sb("before", [P, P], F16)
        ident = sb("ident_c", [P, P])
        eps = sb("eps_c", [P, 1])
        stats = sb("stats_c", [P, 2, 6])
        mean_var = sb("mean_var_c", [P, 2, 2])
        std = sb("std_c", [P, 2])
        rstd = sb("rstd_c", [P, 2])
        x1_tile = sb("x1_tile", [P, 2, D])
        xt_pair = sb("x1_t_pair", [P, 2, 2, DC, P], F16)
        logits = sb("logits", [P, 2, EXPERTS])
        best = sb("best", [P, 2, 8])
        best_at = sb("best_at", [P, 2, 8], mybir.dt.uint32)
        best_two = sb("best_two", [P, TOP, TILES])
        names_i = sb("expert_names_i", [P, EXPERTS], I32)
        names = sb("expert_names", [P, EXPERTS])
        limits_i = sb("tile_limits_i", [P, MOST_OF_ONE], I32)
        limits = sb("tile_limits", [P, MOST_OF_ONE])
        at_f = sb("best_at_f", [P, TOP, TILES])
        is_best = sb("is_best", [P, TOP, TILES, EXPERTS])
        chosen = sb("chosen", [P, TILES, EXPERTS], F16)
        diff = sb("logit_difference", [P, TILES])
        ratio = sb("exp_difference", [P, TILES])
        total = sb("exp_total", [P, TILES])
        over = sb("over_limit", [P, EXPERTS, MOST_OF_ONE])
        tiles_f = sb("tiles_of_expert", [P, EXPERTS])
        start_f = sb("first_tile_of_expert", [P, EXPERTS])
        place = sb("place", [P, TILES, EXPERTS])
        place_of = sb("place_of_choice", [P, TILES, EXPERTS])
        place_f = sb("place_f", [P, TOP, TILES])
        ps_p = psum("ps_proj", [P, 2, 512])
        ps_t = psum("ps_x1_t", [P, 2, 512])
        ps_g = psum("ps_gate", [P, 2, 512])
        ps_rank = psum("ps_rank", [P, 512])
        ps_r = ps_rank[:, 0:(TILES + 1) * EXPERTS].rearrange("p (t e) -> p t e", e=EXPERTS)

        loaded, cleared, prep_a, prep_v, prep_g = sem("c_loaded"), sem("c_cleared"), sem("c_prep_a"), sem("c_prep_v"), sem("c_prep_g")
        projected, h_steps, std_made, rstd_made, x1_made = sem("c_projected"), sem("c_h_steps"), sem("c_std"), sem("c_rstd"), sem("x1_made")
        x1_kept = sem("x1_kept")
        turned, t_hi, t_split, gated, picked = sem("c_turned"), sem("c_t_hi"), sem("c_t_split"), sem("gated"), sem("picked")
        passed = sem("c_passed")
        chain, ratio_made, ranked, scattered = sem("route_chain"), sem("ratio_made"), sem("ranked"), sem("scattered")
        CHOSEN = 4 + (N % P > 0)
        ROUTED = CHOSEN + 11 + EXPERTS + 3 * TOP
        block = ctx.enter_context(nc.Block())

        @block.sync
        def _(sp):
            sp.dma_start(w_raw[:, :, :], d["proj0_w"]).then_inc(loaded, 16)
            sp.dma_start(g_raw[:, :, :], d["gate_w"]).then_inc(loaded, 16)
            sp.dma_start(bias_raw[0:1, :], d["proj0_b"]).then_inc(loaded, 16)
            sp.dma_start(bias_raw[32:33, :], d["proj0_b"]).then_inc(loaded, 16)

        @block.gpsimd
        def _(pool):
            pool.memset(ident[:, :], 0.0).then_inc(prep_g, 1)
            pool.memset(before[:, :], 1.0).then_inc(prep_g, 1)
            pool.wait_ge(prep_g, 2)
            pool.affine_select(out=ident[:, :], in_=ident[:, :], compare_op=ALU.not_equal, fill=1.0,
                               base=0, pattern=[[-1, P]], channel_multiplier=1).then_inc(prep_g, 1)
            pool.affine_select(out=before[:, :], in_=before[:, :], compare_op=ALU.is_ge, fill=0.0,
                               base=-1, pattern=[[1, P]], channel_multiplier=-1).then_inc(prep_g, 1)
            pool.memset(eps[:, :], EPS).then_inc(prep_g, 1)
            pool.memset(ones[:, :], 1.0).then_inc(prep_g, 1)
            pool.iota(names_i[:, :], [[1, EXPERTS]], base=0, channel_multiplier=0).then_inc(prep_g, 1)
            pool.iota(limits_i[:, :], [[ROWS, MOST_OF_ONE]], base=0, channel_multiplier=0).then_inc(prep_g, 1)
            pool.wait_ge(prep_g, 8)
            pool.tensor_copy(names[:, :], names_i[:, :]).then_inc(prep_g, 1)
            pool.tensor_copy(limits[:, :], limits_i[:, :]).then_inc(prep_g, 1)

            def keep_x1(t, s):
                pool.wait_ge(x1_made, t + 1)
                pool.tensor_copy(x1[:, bass.ds(t, 1), :], x1_tile[:, s:s + 1, :]).then_inc(x1_kept, 1)

            in_loop(pool, 0, TILES, keep_x1)
            pool.wait_ge(chain, ROUTED)
            pool.wait_ge(x1_kept, TILES)
            for k in range(TOP):
                for t in range(TILES):
                    rows = min(P, N - t * P)
                    pool.indirect_dma_start(queue[:, :], bass.IndirectOffsetOnAxis(places[0:rows, k, t:t + 1], 0),
                                            x1[0:rows, t, :], None).then_inc(scattered, 16)
            pool.wait_ge(scattered, 16 * TOP * TILES)

        @block.scalar
        def _(act):
            act.wait_ge(loaded, 64)
            act.activation(w_pair[:, HI, :, :], w_raw[:, :, :], ACT.Copy, scale=WS).then_inc(prep_a, 1)
            act.activation(g_pair[:, HI, :, :], g_raw[:, :, :], ACT.Copy, scale=WS).then_inc(prep_a, 1)
            act.wait_ge(cleared, 2)
            act.activation(bias_rows[0:1, :], bias_raw[0:1, :], ACT.Copy, scale=WS).then_inc(prep_a, 1)
            act.activation(bias_hi[32:33, :], bias_raw[32:33, :], ACT.Copy, scale=WS).then_inc(prep_a, 1)
            act.wait_ge(prep_g, 10)

            def root(t, s):
                act.wait_ge(h_steps, 3 * t + 3)
                act.activation(std[:, s:s + 1], mean_var[:, s, 1:2], ACT.Sqrt, bias=eps[:, 0:1]).then_inc(std_made, 1)

            def t_hi_(t, s):
                act.wait_ge(turned, t + 1)
                act.wait_ge(gated, free(t))
                act.activation(xt_pair[:, s, HI, :, :], ps_t[:, s, 0:D].rearrange("p (c t) -> p c t", c=DC), ACT.Copy).then_inc(t_hi, 1)

            skewed(act, TILES, (0, root), (3, t_hi_))
            act.wait_ge(chain, 1)
            act.activation(ratio[:, :], diff[:, :], ACT.Exp).then_inc(ratio_made, 1)

        @block.vector
        def _(dve):
            dve.memset(bias_rows[:, :], 0.0).then_inc(cleared, 1)
            dve.memset(attended_t[:, :, :, N:NPAD], 0.0).then_inc(cleared, 1)
            dve.wait_ge(prep_a, 4)
            dve.wait_ge(cleared, 2)

            def flat(ap):
                return ap.rearrange("p c n -> p (c n)")

            dve.scalar_tensor_tensor(flat(w_pair[:, LO, :, :]), flat(w_raw[:, :, :]), WS, flat(w_pair[:, HI, :, :]),
                                     ALU.mult, ALU.subtract).then_inc(prep_v, 1)
            dve.scalar_tensor_tensor(flat(g_pair[:, LO, :, :]), flat(g_raw[:, :, :]), WS, flat(g_pair[:, HI, :, :]),
                                     ALU.mult, ALU.subtract).then_inc(prep_v, 1)
            dve.scalar_tensor_tensor(bias_rows[32:33, :], bias_raw[32:33, :], WS, bias_hi[32:33, :],
                                     ALU.mult, ALU.subtract).then_inc(prep_v, 1)
            dve.wait_ge(prep_g, 10)

            def h_and_stats(t, s):
                dve.wait_ge(projected, made(t))
                h = residual[:, bass.ds(t, 1), :]
                dve.scalar_tensor_tensor(h, ps_p[:, s:s + 1, 0:D], 1.0 / WS, h, ALU.mult, ALU.add).then_inc(h_steps, 1)
                wait_apart(dve, h_steps, 3 * t + 1, passed)
                dve.bn_stats(stats[:, s, :], h).then_inc(h_steps, 1)
                wait_apart(dve, h_steps, 3 * t + 2, passed)
                dve.bn_aggr(mean_var[:, s, :], stats[:, s, :]).then_inc(h_steps, 1)

            def norm(t, s):
                dve.wait_ge(std_made, t + 1)
                dve.reciprocal(rstd[:, s:s + 1], std[:, s:s + 1]).then_inc(rstd_made, 1)
                dve.wait_ge(rstd_made, t + 1)
                if not isinstance(t, int) or t >= 2:
                    dve.wait_ge(turned, t - 1)
                    dve.wait_ge(x1_kept, t - 1)
                dve.tensor_scalar(x1_tile[:, s:s + 1, :], residual[:, bass.ds(t, 1), :], mean_var[:, s, 0:1], rstd[:, s:s + 1],
                                  ALU.subtract, ALU.mult).then_inc(x1_made, 1)

            def t_lo(t, s):
                dve.wait_ge(t_hi, t + 1)
                dve.tensor_tensor(xt_pair[:, s, LO, :, :], ps_t[:, s, 0:D].rearrange("p (c t) -> p c t", c=DC),
                                  xt_pair[:, s, HI, :, :], ALU.subtract).then_inc(t_split, 1)

            def pick(t, s):
                dve.wait_ge(gated, made(t))
                dve.tensor_scalar(logits[:, s, :], ps_g[:, s, 0:EXPERTS], 1.0 / WS, None, ALU.mult).then_inc(picked, 1)
                wait_apart(dve, picked, 5 * t + 1, passed)
                dve.max(best[:, s, :], logits[:, s, :]).then_inc(picked, 1)
                wait_apart(dve, picked, 5 * t + 2, passed)
                dve.max_index(best_at[:, s, :], best[:, s, :], logits[:, s, :]).then_inc(picked, 1)
                dve.tensor_copy(best_two[:, :, bass.ds(t, 1)], best[:, s, 0:TOP, None]).then_inc(picked, 1)
                dve.wait_ge(picked, 5 * t + 3)
                dve.tensor_copy(at_f[:, :, bass.ds(t, 1)], best_at[:, s, 0:TOP, None]).then_inc(picked, 1)

            skewed(dve, TILES, (0, h_and_stats), (1, norm), (3, t_lo), (4, pick))

            steps = [0]

            def then(ins):
                steps[0] += 1
                ins.then_inc(chain, 1)
                dve.wait_ge(chain, steps[0])

            def wide(ap):
                return ap[:, :, None].to_broadcast([P, TILES, EXPERTS])

            dve.wait_ge(picked, 5 * TILES)
            then(dve.tensor_tensor(diff[:, :], best_two[:, 1, :], best_two[:, 0, :], ALU.subtract))
            for k in range(TOP):
                then(dve.tensor_tensor(is_best[:, k, :, :], wide(at_f[:, k, :]),
                                       names[:, None, :].to_broadcast([P, TILES, EXPERTS]), ALU.is_equal))
            then(dve.tensor_tensor(chosen[:, :, :], is_best[:, 0, :, :], is_best[:, 1, :, :], ALU.add))
            if N % P:
                then(dve.memset(chosen[N % P:P, TILES - 1, :], 0.0))
            assert steps[0] == CHOSEN
            dve.wait_ge(ratio_made, 1)
            then(dve.tensor_scalar(total[:, :], ratio[:, :], 1.0, None, ALU.add))
            then(dve.reciprocal(weights[:, 0, :], total[:, :]))
            then(dve.tensor_tensor(weights[:, 1, :], weights[:, 0, :], ratio[:, :], ALU.mult))
            dve.wait_ge(ranked, 1)
            counts = ps_r[:, TILES, :]
            then(dve.tensor_copy(start_f[:, :], counts))
            then(dve.tensor_tensor(over[:, :, :], start_f[:, :, None].to_broadcast([P, EXPERTS, MOST_OF_ONE]),
                                   limits[:, None, :].to_broadcast([P, EXPERTS, MOST_OF_ONE]), ALU.is_gt))
            then(dve.tensor_reduce(tiles_f[:, :], over[:, :, :], AX.X, ALU.add))
            then(dve.tensor_scalar(tiles_f[:, :], tiles_f[:, :], float(LEAST_TILES), None, ALU.max))
            then(dve.memset(start_f[:, 0:1], 0.0))
            for e in range(1, EXPERTS):
                then(dve.tensor_tensor(start_f[:, e:e + 1], start_f[:, e - 1:e], tiles_f[:, e - 1:e], ALU.add))
            then(dve.tensor_copy(bounds[:, 0, :], start_f[:, :]))
            then(dve.tensor_copy(bounds[:, 1, :], tiles_f[:, :]))
            then(dve.tensor_scalar(start_f[:, :], start_f[:, :], float(ROWS), None, ALU.mult))
            then(dve.tensor_tensor(place[:, :, :], ps_r[:, 0:TILES, :], start_f[:, None, :].to_broadcast([P, TILES, EXPERTS]), ALU.add))
            for k in range(TOP):
                then(dve.tensor_tensor(place_of[:, :, :], place[:, :, :], is_best[:, k, :, :], ALU.mult))
                then(dve.tensor_reduce(place_f[:, k, :], place_of[:, :, :], AX.X, ALU.add))
                then(dve.tensor_copy(places[:, k, :], place_f[:, k, :]))
            assert steps[0] == ROUTED, steps[0]

        @block.tensor
        def _(pe):
            pe.sem_inc(projected, SLOTS)
            pe.sem_inc(gated, SLOTS)
            pe.wait_ge(prep_v, 3)
            pe.wait_ge(cleared, 2)
            pe.wait_ge(prep_g, 10)

            def project(t, s):
                if not isinstance(t, int) or t >= 2:
                    pe.wait_ge(h_steps, 3 * t - 5)
                split = [(c, a) for c in range(DC) for a in (HI, LO)]
                for n, (c, a) in enumerate(split):
                    x = attended_t[:, a, c, bass.ds(t * P, P)]
                    for b in ((HI, LO) if a == HI else (HI,)):
                        pe.matmul(ps_p[:, s, 0:D], x, w_pair[:, b, c, :], start=(n == 0 and b == HI), stop=False)
                pe.matmul(ps_p[:, s, 0:D], ones[:, :], bias_rows[:, :], start=False, stop=True).then_inc(projected, 1)

            def turn(t, s):
                pe.wait_ge(x1_made, t + 1)
                if not isinstance(t, int) or t >= 2:
                    pe.wait_ge(t_split, t - 1)
                for c in range(DC):
                    mm = pe.transpose(ps_t[:, s, c * P:(c + 1) * P], x1_tile[:, s, c * P:(c + 1) * P], ident[:, :])
                mm.then_inc(turned, 1)

            def gate(t, s):
                pe.wait_ge(t_split, t + 1)
                if not isinstance(t, int) or t >= 2:
                    pe.wait_ge(picked, 5 * t - 9)
                split_matmuls(pe, ps_g[:, s, 0:EXPERTS], lambda a, c: xt_pair[:, s, a, c, :],
                              lambda b, c: g_pair[:, b, c, :], DC).then_inc(gated, 1)

            skewed(pe, TILES, (0, project), (2, turn), (3, gate))
            pe.wait_ge(chain, CHOSEN)
            pe.matmul(ps_r[:, 0:TILES, :], before[:, :], chosen[:, :, :], start=True, stop=False, skip_group_check=True)
            for t in range(TILES):
                mm = pe.matmul(ps_r[:, t + 1:TILES + 1, :], ones[:, :],
                               chosen[:, t:t + 1, :].to_broadcast([P, TILES - t, EXPERTS]),
                               start=False, stop=(t == TILES - 1), skip_group_check=True)
            mm.then_inc(ranked, 1)


def experts(nc, d, keep):
    bounds, queue, answers = keep["bounds"], keep["queue"], keep["answers"]
    WIDE = DC * HIDDEN
    PAIRED = MC // 2
    with ExitStack() as ctx:
        def sb(name, shape, dt=F32):
            return ctx.enter_context(nc.sbuf_tensor(name, shape, dt))

        def psum(name, shape, dt=F32):
            return ctx.enter_context(nc.psum_tensor(name, shape, dt))

        def sem(name):
            return ctx.enter_context(nc.semaphore(name))

        w_raw = sb("expert_w_raw", [P, 2, WIDE])
        w_pair = sb("expert_w_pair", [P, 2, 2, 2, WIDE], F16)
        in_b = sb("in_b", [P, EXPERTS, MC])
        out_b_raw = sb("out_b_raw", [33, EXPERTS * D])
        out_b_hi = sb("out_b_hi", [33, EXPERTS * D], F16)
        out_b_rows = sb("out_b_rows", [P, EXPERTS, D], F16)
        ones = sb("ones_d", [P, P], F16)
        ident = sb("ident_d", [P, P])
        x_tile = sb("x_tile", [P, 2, D])
        xt_pair = sb("x_t_pair", [P, 2, DC, ROWS], F16)
        hidden = sb("hidden", [P, 2, 2, ROWS])
        hidden_pair = sb("hidden_pair", [P, 2, MC, ROWS], F16)
        y_tile = sb("y_tile", [P, 2, D])
        ps_t = psum("ps_x_t", [P, DC, ROWS])
        ps_h = psum("ps_hidden", [P, PAIRED, 2, ROWS])
        ps_y = psum("ps_y", [P, 2, D])

        loaded, prep_g, prep_a, prep_v = sem("e_loaded"), sem("e_prep_g"), sem("e_prep_a"), sem("e_prep_v")
        w_loaded, w_hi, w_split = sem("expert_w_loaded"), sem("expert_w_hi"), sem("expert_w_split")
        x_loaded, turned, x_hi, x_split = sem("x_loaded"), sem("e_turned"), sem("x_hi"), sem("x_split")
        hidden_summed, gelu_made, hidden_hi, hidden_split = sem("hidden_summed"), sem("gelu_made"), sem("hidden_hi"), sem("hidden_split")
        hidden_used, y_made, y_stored, passed = sem("hidden_used"), sem("y_made"), sem("y_stored"), sem("e_passed")
        PART = 2 * WIDE // PAIRED
        queue_tiles = queue.rearrange("(g h p) n -> g p h n", h=2, p=P)
        answer_tiles = answers.rearrange("(g h p) n -> g p h n", h=2, p=P)
        block = ctx.enter_context(nc.Block())

        def start_of(eng, e):
            return eng.value_load(bounds[0:1, 0, bass.ds(e, 1)], min_val=0, max_val=EXPERT_TILES - 1)

        def tiles_of(eng, e):
            return eng.value_load(bounds[0:1, 1, bass.ds(e, 1)], min_val=LEAST_TILES, max_val=MOST_OF_ONE)

        def all_tiles(eng, tile):
            def expert(e, s):
                start, count = start_of(eng, e), tiles_of(eng, e)
                tile(start, e, s, not (isinstance(e, int) and e == EXPERTS - 1))
                with eng.Fori(1, count) as i:
                    g = eng.snap(start + i, min_val=0, max_val=EXPERT_TILES - 1)
                    tile(g, e, s, False)

            return expert

        def all_experts(eng, expert):
            in_loop(eng, 0, EXPERTS - 1, expert)
            expert(EXPERTS - 1, (EXPERTS - 1) % 2)

        def part(s, half, k):
            return w_pair[:, s, half, :, :].rearrange("p a n -> p (a n)")[:, k * PART:(k + 1) * PART]

        def raw_part(k):
            return w_raw[:, :, :].rearrange("p a n -> p (a n)")[:, k * PART:(k + 1) * PART]

        @block.sync
        def _(sp):
            sp.dma_start(in_b[:, :, :], d["in_b"]).then_inc(loaded, 16)
            sp.dma_start(out_b_raw[0:1, :], d["out_b"]).then_inc(loaded, 16)
            sp.dma_start(out_b_raw[32:33, :], d["out_b"]).then_inc(loaded, 16)

            def load_weights(e):
                if not isinstance(e, int) or e >= 1:
                    sp.wait_ge(w_split, PAIRED * e)
                for which, w in enumerate(("in_w", "out_w")):
                    sp.dma_start(w_raw[:, which:which + 1, :].rearrange("p a n -> p (a n)"),
                                 d[w][bass.ds(e, 1)].rearrange("a p c n -> (a p) (c n)")).then_inc(w_loaded, 16)

            def load_x(g):
                sp.dma_start(x_tile[:, :, :], queue_tiles[bass.ds(g, 1)].rearrange("a p h n -> (a p) h n")).then_inc(x_loaded, 16)

            load_x(0)
            load_weights(0)
            load_weights(1)

            def tile(g, e, s, ahead):
                sp.wait_ge(turned, g + 1)
                load_x(g + 1)
                if ahead and not (isinstance(e, int) and e + 2 >= EXPERTS):
                    load_weights(e + 2)
                sp.wait_ge(y_made, g + 2)
                sp.dma_start(answer_tiles[bass.ds(g, 1)].rearrange("a p h n -> (a p) h n"), y_tile[:, :, :]).then_inc(y_stored, 16)

            expert = all_tiles(sp, tile)
            in_loop(sp, 0, EXPERTS - 2, expert)
            expert(EXPERTS - 2, 0)
            expert(EXPERTS - 1, 1)
            wait_apart(sp, y_stored, 16 * (start_of(sp, EXPERTS - 1) + tiles_of(sp, EXPERTS - 1)) + 16, passed)

        @block.gpsimd
        def _(pool):
            pool.memset(ident[:, :], 0.0).then_inc(prep_g, 1)
            pool.wait_ge(prep_g, 1)
            pool.affine_select(out=ident[:, :], in_=ident[:, :], compare_op=ALU.not_equal, fill=1.0,
                               base=0, pattern=[[-1, P]], channel_multiplier=1).then_inc(prep_g, 1)
            pool.memset(ones[:, :], 1.0).then_inc(prep_g, 1)

        @block.scalar
        def _(act):
            act.sem_inc(gelu_made, PAIRED)
            act.sem_inc(y_made, 1)
            act.sem_inc(y_stored, 16)
            act.wait_ge(loaded, 48)
            act.wait_ge(prep_v, 1)
            act.activation(out_b_rows[0:1, :, :].rearrange("p e n -> p (e n)"), out_b_raw[0:1, :], ACT.Copy, scale=WS).then_inc(prep_a, 1)
            act.activation(out_b_hi[32:33, :], out_b_raw[32:33, :], ACT.Copy, scale=WS).then_inc(prep_a, 1)

            def part_hi(e, s, k):
                act.wait_ge(w_loaded, 32 * e + 32)
                act.activation(part(s, HI, k), raw_part(k), ACT.Copy, scale=WS).then_inc(w_hi, 1)

            def x_hi_(g):
                act.wait_ge(turned, g + 1)
                act.activation(xt_pair[:, HI, :, :], ps_t[:, :, :], ACT.Copy).then_inc(x_hi, 1)

            for k in range(PAIRED):
                part_hi(0, 0, k)
            x_hi_(0)

            def tile(g, e, s, ahead):
                for q in range(PAIRED):
                    act.wait_ge(hidden_split, PAIRED * g + q + 1)
                    wait_apart(act, hidden_summed, PAIRED * g + q + 1, passed)
                    for m in range(2):
                        out = act.activation(hidden[:, q % 2, m, :], ps_h[:, q, m, :], ACT.Gelu, scale=1.0 / WS,
                                             bias=in_b[:, bass.ds(e, 1), 2 * q + m:2 * q + m + 1].rearrange("p a b -> p (a b)"))
                    out.then_inc(gelu_made, 1)
                    if ahead:
                        part_hi(e + 1, 1 - s, q)
                x_hi_(g + 1)
                act.wait_ge(hidden_used, PAIRED * (g + 1) + PAIRED)
                act.wait_ge(y_stored, 16 * g + 16)
                act.activation(y_tile[:, :, :], ps_y[:, :, :], ACT.Copy, scale=1.0 / WS).then_inc(y_made, 1)

            all_experts(act, all_tiles(act, tile))

        @block.vector
        def _(dve):
            dve.sem_inc(hidden_split, SLOTS)
            dve.memset(out_b_rows[:, :, :], 0.0).then_inc(prep_v, 1)
            dve.wait_ge(prep_a, 2)
            dve.wait_ge(prep_v, 1)
            dve.scalar_tensor_tensor(out_b_rows[32:33, :, :].rearrange("p e n -> p (e n)"), out_b_raw[32:33, :], WS, out_b_hi[32:33, :],
                                     ALU.mult, ALU.subtract).then_inc(prep_v, 1)

            def x_lo(g):
                dve.wait_ge(x_hi, g + 1)
                dve.tensor_tensor(xt_pair[:, LO, :, :], ps_t[:, :, :], xt_pair[:, HI, :, :], ALU.subtract).then_inc(x_split, 1)

            def part_lo(e, s, k):
                dve.wait_ge(w_hi, PAIRED * e + k + 1)
                dve.scalar_tensor_tensor(part(s, LO, k), raw_part(k), WS, part(s, HI, k), ALU.mult, ALU.subtract).then_inc(w_split, 1)

            for k in range(PAIRED):
                part_lo(0, 0, k)
            x_lo(0)

            def tile(g, e, s, ahead):
                for q in range(PAIRED):
                    dve.wait_ge(gelu_made, PAIRED * g + q + 1 + PAIRED)
                    dve.wait_ge(hidden_used, PAIRED * g + q + 1)
                    dve.tensor_copy(hidden_pair[:, HI, 2 * q:2 * q + 2, :], hidden[:, q % 2, :, :]).then_inc(hidden_hi, 1)
                    dve.wait_ge(hidden_hi, PAIRED * g + q + 1)
                    dve.tensor_tensor(hidden_pair[:, LO, 2 * q:2 * q + 2, :], hidden[:, q % 2, :, :], hidden_pair[:, HI, 2 * q:2 * q + 2, :],
                                      ALU.subtract).then_inc(hidden_split, 1)
                    if ahead:
                        part_lo(e + 1, 1 - s, q)
                x_lo(g + 1)

            all_experts(dve, all_tiles(dve, tile))

        @block.tensor
        def _(pe):
            pe.sem_inc(hidden_used, PAIRED)
            pe.wait_ge(prep_g, 3)
            pe.wait_ge(prep_v, 2)

            def turn(g):
                pe.wait_ge(x_loaded, 16 * g + 16)
                if not isinstance(g, int) or g >= 1:
                    pe.wait_ge(x_split, g)
                for c in range(DC):
                    for h in range(2):
                        mm = pe.transpose(ps_t[:, c, h * P:(h + 1) * P], x_tile[:, h, c * P:(c + 1) * P], ident[:, :])
                mm.then_inc(turned, 1)

            turn(0)

            def tile(g, e, s, ahead):
                w_in = w_pair[:, s, :, 0, :].rearrange("p a (c m) -> p a c m", c=DC)
                w_out = w_pair[:, s, :, 1, :].rearrange("p a (m c) -> p a m c", m=MC)

                def first_layer(q):
                    pe.wait_ge(gelu_made, PAIRED * g + q + 1)
                    for m in range(2):
                        mm = split_matmuls(pe, ps_h[:, q, m, :], lambda a, c: w_in[:, a, c, (2 * q + m) * P:(2 * q + m + 1) * P],
                                           lambda b, c: xt_pair[:, b, c, :], DC, first_start=(m == 0), check=False)
                    mm.then_inc(hidden_summed, 1)

                def second_layer(q):
                    pe.wait_ge(hidden_split, PAIRED * g + q + 1 + SLOTS)
                    if q == 0:
                        pe.wait_ge(y_made, g + 1)
                    for h in range(2):
                        if q == 0:
                            pe.matmul(ps_y[:, h, :], ones[:, :], out_b_rows[:, bass.ds(e, 1), :], start=(h == 0), stop=False, skip_group_check=True)
                        for m in (2 * q, 2 * q + 1):
                            for a, b in ((HI, HI), (HI, LO), (LO, HI)):
                                mm = pe.matmul(ps_y[:, h, :], hidden_pair[:, a, m, h * P:(h + 1) * P], w_out[:, b, m, :],
                                               start=False, stop=(m == MC - 1 and a == LO), skip_group_check=True)
                    mm.then_inc(hidden_used, 1)

                pe.wait_ge(x_split, g + 1)
                first_layer(0)
                first_layer(1)
                first_layer(2)
                second_layer(0)
                first_layer(3)
                turn(g + 1)
                second_layer(1)
                second_layer(2)
                second_layer(3)

            body = all_tiles(pe, tile)

            def expert(e, s):
                pe.wait_ge(w_split, PAIRED * e + PAIRED)
                body(e, s)

            all_experts(pe, expert)


def gather_and_norm(nc, d, keep, ahead):
    residual, weights, places, answers = keep["residual"], keep["weights"], keep["places"], keep["answers"]
    state, pair = keep["state"], keep["chan_a"]
    with ExitStack() as ctx:
        def sb(name, shape, dt=F32):
            return ctx.enter_context(nc.sbuf_tensor(name, shape, dt))

        def sem(name):
            return ctx.enter_context(nc.semaphore(name))

        ident = sb("ident_f", [P, P])
        eps = sb("eps_f", [P, 1])
        rows_of = sb("answer_rows", [P, 2, TOP, D])
        stats = sb("stats_f", [P, 2, 6])
        mean_var = sb("mean_var_f", [P, 2, 2])
        std = sb("std_f", [P, 2])
        rstd = sb("rstd_f", [P, 2])
        x2 = sb("x2_tile", [P, 2, D])
        ps_t = ctx.enter_context(nc.psum_tensor("ps_x2_t", [P, 2, 512], F32))

        prep_g, passed = sem("f_prep_g"), sem("f_passed")
        gathered = [sem("gathered0"), sem("gathered1")]
        h_steps, std_made, rstd_made, x2_made = sem("f_h_steps"), sem("f_std"), sem("f_rstd"), sem("x2_made")
        turned, state_made, t_hi, t_split = sem("f_turned"), sem("state_made"), sem("f_t_hi"), sem("f_t_split")
        block = ctx.enter_context(nc.Block())

        @block.sync
        def _(sp):
            ahead.sync(sp)

        @block.gpsimd
        def _(pool):
            pool.memset(ident[:, :], 0.0).then_inc(prep_g, 1)
            pool.wait_ge(prep_g, 1)
            pool.affine_select(out=ident[:, :], in_=ident[:, :], compare_op=ALU.not_equal, fill=1.0,
                               base=0, pattern=[[-1, P]], channel_multiplier=1).then_inc(prep_g, 1)
            pool.memset(eps[:, :], EPS).then_inc(prep_g, 1)
            for t in range(TILES):
                rows = min(P, N - t * P)
                if t >= 2:
                    pool.wait_ge(h_steps, 4 * t - 6)
                for k in range(TOP):
                    pool.indirect_dma_start(rows_of[0:rows, t % 2, k, :], None, answers[0:EXPERT_TILES * ROWS, :],
                                            bass.IndirectOffsetOnAxis(places[0:rows, k, t:t + 1], 0)).then_inc(gathered[t % 2], 16)
            ahead.gpsimd(pool)

        @block.scalar
        def _(act):
            act.wait_ge(prep_g, 3)

            def root(t, s):
                act.wait_ge(h_steps, 4 * t + 4)
                act.activation(std[:, s:s + 1], mean_var[:, s, 1:2], ACT.Sqrt, bias=eps[:, 0:1]).then_inc(std_made, 1)

            def out_hi(t, s):
                act.wait_ge(turned, t + 1)
                turned_rows = ps_t[:, s, 0:D].rearrange("p (c t) -> p c t", c=DC)
                act.activation(state[:, :, bass.ds(t * P, P)], turned_rows, ACT.Copy).then_inc(state_made, 1)
                act.activation(pair[:, HI, :, bass.ds(t * P, P)], turned_rows, ACT.Copy).then_inc(t_hi, 1)

            skewed(act, TILES, (3, out_hi), (0, root))
            ahead.scalar(act)

        @block.vector
        def _(dve):
            def add_answers(t, s):
                rows = P if not isinstance(t, int) else min(P, N - t * P)
                dve.wait_ge(gathered[s], 16 * t + 32 - 16 * s)
                h = residual[0:rows, bass.ds(t, 1), :]
                for k in range(TOP):
                    dve.scalar_tensor_tensor(h, rows_of[0:rows, s, k:k + 1, :], weights[0:rows, k, bass.ds(t, 1)], h,
                                             ALU.mult, ALU.add).then_inc(h_steps, 1)
                    wait_apart(dve, h_steps, 4 * t + k + 1, passed)
                dve.bn_stats(stats[:, s, :], residual[:, bass.ds(t, 1), :]).then_inc(h_steps, 1)
                wait_apart(dve, h_steps, 4 * t + 3, passed)
                dve.bn_aggr(mean_var[:, s, :], stats[:, s, :]).then_inc(h_steps, 1)

            def norm(t, s):
                dve.wait_ge(std_made, t + 1)
                dve.reciprocal(rstd[:, s:s + 1], std[:, s:s + 1]).then_inc(rstd_made, 1)
                dve.wait_ge(rstd_made, t + 1)
                if not isinstance(t, int) or t >= 2:
                    dve.wait_ge(turned, t - 1)
                dve.tensor_scalar(x2[:, s:s + 1, :], residual[:, bass.ds(t, 1), :], mean_var[:, s, 0:1], rstd[:, s:s + 1],
                                  ALU.subtract, ALU.mult).then_inc(x2_made, 1)

            def out_lo(t, s):
                dve.wait_ge(t_hi, t + 1)
                dve.tensor_tensor(pair[:, LO, :, bass.ds(t * P, P)], ps_t[:, s, 0:D].rearrange("p (c t) -> p c t", c=DC),
                                  pair[:, HI, :, bass.ds(t * P, P)], ALU.subtract).then_inc(t_split, 1)

            skewed(dve, TILES, (0, add_answers), (1, norm), (3, out_lo))
            ahead.vector(dve)

        @block.tensor
        def _(pe):
            pe.wait_ge(prep_g, 2)

            def turn(t, s):
                pe.wait_ge(x2_made, t + 1)
                if not isinstance(t, int) or t >= 2:
                    pe.wait_ge(t_split, t - 1)
                for c in range(DC):
                    mm = pe.transpose(ps_t[:, s, c * P:(c + 1) * P], x2[:, s, c * P:(c + 1) * P], ident[:, :])
                mm.then_inc(turned, 1)

            skewed(pe, TILES, (4, turn))


LAYERS, HEADS = 12, 16
HD = D // HEADS
CHUNKS = 8
CT = N // CHUNKS
CP = PAIRS // CHUNKS
PIECES = CHUNKS
PIECE = (4 * D * DC) // PIECES


def layer_constants(nc, ctx, d, keep):
    def sb(name, shape, dt=F32):
        return ctx.enter_context(nc.sbuf_tensor(name, shape, dt))

    bias_sum = keep["bias_sum"]
    q_b_raw = sb("q_b_raw", [P, LAYERS, DC])
    proj_b = sb("proj_b", [P, LAYERS, DC])
    kv_b_hi = sb("kv_b_hi", [33, 2 * D], F16)
    c = Prepared()
    c.w_raw = sb("layer_w_raw", [P, PIECES, PIECE])
    c.w_pair = sb("layer_w_pair", [P, 2, 2, PIECES * PIECE], F16)
    c.kv_b_raw = sb("kv_b_raw", [33, 2 * D])
    c.kv_b_rows = sb("kv_b_rows", [P, 2, 2 * D], F16)
    c.q_b = sb("q_b", [P, LAYERS, DC])
    c.ones = sb("ones_g", [P, P], F16)
    c.own = sb("own_image_g", [PT, 2])
    c.mask = sb("head_mask", [P, 2, DC, P])

    def sem(name):
        return ctx.enter_context(nc.semaphore(name))

    c.loaded, c.prep_g, c.prep_v = sem("g_loaded"), sem("g_prep_g"), sem("g_prep_v")
    c.w_loaded, c.w_hi, c.w_split = sem("g_w_loaded"), sem("g_w_hi"), sem("g_w_split")
    c.b_loaded, c.b_hi, c.b_split = sem("g_b_loaded"), sem("g_b_hi"), sem("g_b_split")

    def load(sp, l):
        if not isinstance(l, int) or l >= 1:
            sp.wait_ge(c.w_split, PIECES * l)
            sp.wait_ge(c.b_split, l)
        sp.dma_start(c.w_raw[:, 0:6, :].rearrange("p a n -> p (a n)"),
                     d["qkv1_w"][bass.ds(l, 1)].rearrange("a p c n -> (a p) (c n)")).then_inc(c.w_loaded, 16)
        sp.dma_start(c.w_raw[:, 6:8, :].rearrange("p a n -> p (a n)"),
                     d["proj1_w"][bass.ds(l, 1)].rearrange("a p c n -> (a p) (c n)")).then_inc(c.w_loaded, 16)
        for row in (0, 32):
            sp.dma_start(c.kv_b_raw[row:row + 1, :], d["qkv1_b"][bass.ds(l, 1), D:3 * D]).then_inc(c.b_loaded, 16)

    def w_pieces(s, half, n):
        return c.w_pair[:, s, half, :].rearrange("p (a n) -> p a n", n=PIECE)[:, bass.ds(n, 1), :]

    def piece_hi(act, s, n):
        act.activation(w_pieces(s, HI, n), c.w_raw[:, bass.ds(n, 1), :], ACT.Copy, scale=WS).then_inc(c.w_hi, 1)

    def biases_hi(act, l, s):
        act.wait_ge(c.b_loaded, 32 * l + 32)
        act.activation(c.kv_b_rows[0:1, s, :], c.kv_b_raw[0:1, :], ACT.Copy, scale=WS)
        act.activation(kv_b_hi[32:33, :], c.kv_b_raw[32:33, :], ACT.Copy, scale=WS).then_inc(c.b_hi, 1)

    def piece_lo(dve, count, s, n):
        dve.wait_ge(c.w_hi, count)
        dve.scalar_tensor_tensor(w_pieces(s, LO, n), c.w_raw[:, bass.ds(n, 1), :], WS, w_pieces(s, HI, n),
                                 ALU.mult, ALU.subtract).then_inc(c.w_split, 1)

    def biases_lo(dve, l, s):
        dve.wait_ge(c.b_hi, l + 1)
        dve.scalar_tensor_tensor(c.kv_b_rows[32:33, s, :], c.kv_b_raw[32:33, :], WS, kv_b_hi[32:33, :],
                                 ALU.mult, ALU.subtract).then_inc(c.b_split, 1)

    c.load, c.piece_hi, c.biases_hi, c.piece_lo, c.biases_lo = load, piece_hi, biases_hi, piece_lo, biases_lo

    def sync(sp):
        load(sp, 0)
        sp.dma_start(q_b_raw[:, :, :], d["q1_bcol"]).then_inc(c.loaded, 16)
        sp.dma_start(proj_b[:, :, :], d["proj1_bcol"]).then_inc(c.loaded, 16)

    def gpsimd(pool):
        pool.memset(c.own[:, :], 1.0 / WS)
        pool.memset(c.ones[:, :], 1.0)
        pool.memset(c.mask[:, :, :, :], float(HD) ** -0.5).then_inc(c.prep_g, 1)
        pool.wait_ge(c.prep_g, 1)
        pool.affine_select(out=c.own[:, 0:1], in_=c.own[:, 0:1], compare_op=ALU.is_ge, fill=0.0,
                           base=TOK - 1, pattern=[[0, 1]], channel_multiplier=-1)
        pool.affine_select(out=c.own[:, 1:2], in_=c.own[:, 1:2], compare_op=ALU.is_ge, fill=0.0,
                           base=-TOK, pattern=[[0, 1]], channel_multiplier=1)
        for n, m in enumerate(c.mask[:, i, k, :].rearrange("p (h j) -> p h j", j=HD) for i in range(2) for k in range(DC)):
            pool.affine_select(out=m, in_=m, compare_op=ALU.is_ge, fill=0.0, base=0,
                               pattern=[[-HD, P // HD], [0, HD]], channel_multiplier=1).then_inc(c.prep_g, 1)
            pool.wait_ge(c.prep_g, n + 2)
            pool.affine_select(out=m, in_=m, compare_op=ALU.is_ge, fill=0.0, base=HD - 1,
                               pattern=[[HD, P // HD], [0, HD]], channel_multiplier=-1)

    def scalar(act):
        act.wait_ge(c.loaded, 32)
        act.activation(c.q_b[:, :, :], q_b_raw[:, :, :], ACT.Copy, scale=WS)
        act.wait_ge(c.prep_v, 1)
        act.wait_ge(c.w_loaded, 32)
        for n in range(PIECES):
            piece_hi(act, 0, n)
        biases_hi(act, 0, 0)

    def vector(dve):
        dve.memset(c.kv_b_rows[:, :, :], 0.0).then_inc(c.prep_v, 1)
        dve.memset(bias_sum[:, 0:1, :], 0.0).then_inc(c.prep_v, 1)
        dve.wait_ge(c.loaded, 32)
        for l in range(LAYERS):
            dve.wait_ge(c.prep_v, 2 + l)
            dve.tensor_tensor(bias_sum[:, l + 1, :], bias_sum[:, l, :], proj_b[:, l, :], ALU.add).then_inc(c.prep_v, 1)
        for n in range(PIECES):
            piece_lo(dve, n + 1, 0, n)
        biases_lo(dve, 0, 0)

    c.sync, c.gpsimd, c.scalar, c.vector = sync, gpsimd, scalar, vector
    return c


def linear_attention_layers(nc, d, keep, c0, ahead):
    state, pair, bias_sum = keep["state"], keep["chan_a"], keep["bias_sum"]
    with ExitStack() as ctx:
        def sb(name, shape, dt=F32):
            return ctx.enter_context(nc.sbuf_tensor(name, shape, dt))

        def psum(name, shape, dt=F32):
            return ctx.enter_context(nc.psum_tensor(name, shape, dt))

        def sem(name):
            return ctx.enter_context(nc.semaphore(name))

        w_pair, kv_b_rows, q_b, ones, own, mask = c0.w_pair, c0.kv_b_rows, c0.q_b, c0.ones, c0.own, c0.mask
        w_loaded, w_split, b_split = c0.w_loaded, c0.w_split, c0.b_split
        k_pair = sb("k_pair_g", [PT, CP, 2, D], F16)
        v_pair = sb("v_pair_g", [PT, CP, 2, 2, D], F16)
        q_pair = sb("q_pair_g", [P, 2, 2, DC, CT], F16)
        outer = sb("outer", [P, CP, 2, DC, P])
        outer_pair = sb("outer_pair", [P, CP, 2, 2, DC, P], F16)
        y_pair = sb("y_pair", [P, 2, DC, CT], F16)
        ps_kv = psum("ps_kv", [P, 2, 512])
        ps_o = psum("ps_outer", [P, 2, 2, DC, P])
        ps_y = psum("ps_y_g", [P, DC, 512])
        ps_x = psum("ps_q_or_x", [P, DC, 512])

        kv_summed, q_summed, outer_summed, applied, x_summed = sem("kv_summed"), sem("q_summed"), sem("outer_summed"), sem("applied"), sem("x_summed")
        kv_hi, q_hi, outer_hi, y_hi, x_hi = sem("kv_hi"), sem("q_hi"), sem("outer_hi"), sem("y_hi"), sem("g_x_hi")
        kv_split, q_split, outer_masked, outer_split = sem("kv_split"), sem("q_split"), sem("outer_masked"), sem("outer_split")
        y_split, x_made, x_split, passed = sem("y_split"), sem("g_x_made"), sem("g_x_split"), sem("g_passed")
        block = ctx.enter_context(nc.Block())

        def all_steps(eng, step):
            def layer(l, s):
                for c in (0, 1):
                    step(CHUNKS * l + c, l, s, c, c)
                in_loop(eng, 2, CHUNKS, lambda c, parity: step(CHUNKS * l + c, l, s, c, parity))

            layer(0, 0)
            with eng.Fori(0, (LAYERS - 2) // 2) as j:
                layer(1 + 2 * j, 1)
                layer(2 + 2 * j, 0)
            layer(LAYERS - 1, 1)
            step(CHUNKS * LAYERS, LAYERS, 0, 0, 0)
            step(CHUNKS * LAYERS + 1, LAYERS, 0, 1, 1)

        def known(value, least):
            return not isinstance(value, int) or value >= least

        def has(g, l, c, back):
            if isinstance(l, int) and l == 0 and isinstance(c, int) and c < back:
                return None
            if isinstance(l, int) and l == LAYERS and c >= back:
                return None
            if isinstance(c, int) and c < back:
                return c - back + CHUNKS, 1
            return c - back, 0

        @block.sync
        def _(sp):
            ahead.sync(sp)
            in_loop(sp, 1, LAYERS, lambda l, s: c0.load(sp, l))

        @block.gpsimd
        def _(pool):
            ahead.gpsimd(pool)

            def step(g, l, s, c, parity):
                if has(g, l, c, 1) is None:
                    return
                for p in range(CP):
                    q = CP * (g - 1) + p
                    pool.wait_ge(outer_hi, q + 1)
                    pool.tensor_tensor(outer_pair[:, p, LO], outer[:, p], outer_pair[:, p, HI], ALU.subtract).then_inc(outer_split, 1)

            all_steps(pool, step)

        @block.scalar
        def _(act):
            def split_next_hi(l, s, c):
                act.wait_ge(w_loaded, 32 * l + 64)
                c0.piece_hi(act, 1 - s, c)
                if isinstance(c, int) and c == 1:
                    c0.biases_hi(act, l + 1, 1 - s)

            def step(g, l, s, c, parity):
                first = has(g, l, c, 0)
                older, oldest = has(g, l, c, 1), has(g, l, c, 2)

                def outer_to_hi(p):
                    if older:
                        q = CP * (g - 1) + p
                        act.wait_ge(outer_masked, q + 1)
                        if known(q, CP):
                            act.wait_ge(applied, q - CP + 1)
                        act.activation(outer_pair[:, p, HI], outer[:, p], ACT.Copy).then_inc(outer_hi, 1)

                def kv_to_hi(p):
                    if first:
                        act.wait_ge(kv_summed, CP * g + p + 1)
                        act.activation(k_pair[:, p, HI, :], ps_kv[0:PT, p % 2, 0:D], ACT.Copy, scale=1.0 / WS)
                        for i in range(2):
                            out = act.activation(v_pair[:, p, HI, i, :], ps_kv[0:PT, p % 2, D:2 * D], ACT.Copy, scale=own[:, i:i + 1])
                        out.then_inc(kv_hi, 1)

                def y_to_hi():
                    if oldest:
                        act.wait_ge(applied, CP * (g - 1))
                        if known(g, 3):
                            act.wait_ge(x_summed, g - 2)
                        act.activation(y_pair[:, HI], ps_y[:, :, 0:CT], ACT.Copy, scale=1.0 / WS).then_inc(y_hi, 1)

                def x_to_hi():
                    if oldest:
                        chunk, back = oldest
                        wait_apart(act, x_made, g - 1, passed)
                        for m in range(DC):
                            out = act.activation(pair[:, HI, m, bass.ds(chunk * CT, CT)], state[:, m, bass.ds(chunk * CT, CT)], ACT.Identity,
                                                 bias=bias_sum[:, bass.ds(l - back + 1, 1), m:m + 1].rearrange("p a b -> p (a b)"))
                        out.then_inc(x_hi, 1)

                def q_to_hi():
                    if first:
                        if known(g, 2):
                            act.wait_ge(applied, CP * (g - 1))
                        wait_apart(act, q_summed, g + 1, passed)
                        for m in range(DC):
                            out = act.activation(q_pair[:, parity, HI, m, :], ps_x[:, m, 0:CT], ACT.Identity,
                                                 bias=q_b[:, bass.ds(l, 1), m:m + 1].rearrange("p a b -> p (a b)"))
                        out.then_inc(q_hi, 1)

                kv_to_hi(0)
                outer_to_hi(0)
                y_to_hi()
                kv_to_hi(1)
                outer_to_hi(1)
                kv_to_hi(2)
                outer_to_hi(2)
                if first and not (isinstance(l, int) and l == LAYERS - 1):
                    split_next_hi(l, s, c)
                outer_to_hi(3)
                x_to_hi()
                kv_to_hi(3)
                q_to_hi()

            all_steps(act, step)
            ahead.scalar(act)

        @block.vector
        def _(dve):
            def step(g, l, s, c, parity):
                first = has(g, l, c, 0)
                older, oldest = has(g, l, c, 1), has(g, l, c, 2)

                def mask_outer(p):
                    if older:
                        q = CP * (g - 1) + p
                        dve.wait_ge(outer_summed, q + 1)
                        if known(q, CP):
                            dve.wait_ge(outer_split, q - CP + 1)
                        dve.tensor_tensor(outer[:, p], ps_o[:, p % 2], mask[:, :, :, :], ALU.mult).then_inc(outer_masked, 1)

                def kv_to_lo(p):
                    if first:
                        dve.wait_ge(kv_hi, CP * g + p + 1)
                        dve.scalar_tensor_tensor(k_pair[:, p, LO, :], ps_kv[0:PT, p % 2, 0:D], 1.0 / WS, k_pair[:, p, HI, :],
                                                 ALU.mult, ALU.subtract)
                        for i in range(2):
                            out = dve.scalar_tensor_tensor(v_pair[:, p, LO, i, :], ps_kv[0:PT, p % 2, D:2 * D], own[:, i:i + 1],
                                                           v_pair[:, p, HI, i, :], ALU.mult, ALU.subtract)
                        out.then_inc(kv_split, 1)

                def y_to_lo():
                    if oldest:
                        dve.wait_ge(y_hi, g - 1)
                        dve.scalar_tensor_tensor(y_pair[:, LO], ps_y[:, :, 0:CT], 1.0 / WS, y_pair[:, HI],
                                                 ALU.mult, ALU.subtract).then_inc(y_split, 1)

                def make_x():
                    if oldest:
                        chunk, back = oldest
                        dve.wait_ge(x_summed, g - 1)
                        x = state[:, :, bass.ds(chunk * CT, CT)]
                        dve.scalar_tensor_tensor(x, ps_x[:, :, 0:CT], 1.0 / WS, x, ALU.mult, ALU.add).then_inc(x_made, 1)

                def x_to_lo():
                    if oldest:
                        chunk, back = oldest
                        dve.wait_ge(x_hi, g - 1)
                        for m in range(DC):
                            out = dve.scalar_tensor_tensor(pair[:, LO, m, bass.ds(chunk * CT, CT)], state[:, m, bass.ds(chunk * CT, CT)],
                                                           bias_sum[:, bass.ds(l - back + 1, 1), m:m + 1].rearrange("p a b -> p (a b)"),
                                                           pair[:, HI, m, bass.ds(chunk * CT, CT)], ALU.add, ALU.subtract)
                        out.then_inc(x_split, 1)

                def q_to_lo():
                    if first:
                        dve.wait_ge(q_hi, g + 1)
                        for m in range(DC):
                            out = dve.scalar_tensor_tensor(q_pair[:, parity, LO, m, :], ps_x[:, m, 0:CT],
                                                           q_b[:, bass.ds(l, 1), m:m + 1].rearrange("p a b -> p (a b)"),
                                                           q_pair[:, parity, HI, m, :], ALU.add, ALU.subtract)
                        out.then_inc(q_split, 1)

                mask_outer(0)
                kv_to_lo(0)
                mask_outer(1)
                y_to_lo()
                kv_to_lo(1)
                mask_outer(2)
                kv_to_lo(2)
                mask_outer(3)
                make_x()
                x_to_lo()
                kv_to_lo(3)
                if first and not (isinstance(l, int) and l == LAYERS - 1):
                    c0.piece_lo(dve, PIECES * (l + 1) + c + 1, 1 - s, c)
                    if isinstance(c, int) and c == 1:
                        c0.biases_lo(dve, l + 1, 1 - s)
                q_to_lo()

            all_steps(dve, step)
            ahead.vector(dve)

        @block.tensor
        def _(pe):
            def step(g, l, s, c, parity):
                first = has(g, l, c, 0)
                older, oldest = has(g, l, c, 1), has(g, l, c, 2)
                w_qkv = w_pair[:, s, :, 0:6 * PIECE].rearrange("p a (c n) -> p a c n", c=DC)

                def outer_products(p):
                    q = CP * (g - 1) + p
                    pe.wait_ge(kv_split, q + 1)
                    if known(q, 2):
                        pe.wait_ge(outer_masked, q - 1)
                    for m in range(DC):
                        mm = split_matmuls(pe, ps_o[:, p % 2, :, m, :], lambda a, _: k_pair[:, p, a, m * P:(m + 1) * P],
                                           lambda b, _: v_pair[:, p, b, :, m * P:(m + 1) * P], 1,
                                           first_start=(m == 0), check=False)
                    mm.then_inc(outer_summed, 1)

                def keys_and_values(p):
                    if known(CP * g + p, 2):
                        pe.wait_ge(kv_split, CP * g + p - 1)
                    pe.matmul(ps_kv[0:PT, p % 2, :], ones[:, 0:PT], kv_b_rows[:, s, :], start=True, stop=False)
                    for n, (m, a, b) in enumerate((m, a, b) for m in range(DC) for a, b in ((HI, HI), (HI, LO), (LO, HI))):
                        mm = pe.matmul(ps_kv[0:PT, p % 2, :], pair[:, a, m, bass.ds(c * CT + p * PT, PT)], w_qkv[:, b, m, D:3 * D],
                                       start=False, stop=(n == 3 * DC - 1))
                    mm.then_inc(kv_summed, 1)

                def queries():
                    if known(g, 2):
                        pe.wait_ge(x_made, g - 1)
                    for m in range(DC):
                        mm = split_matmuls(pe, ps_x[:, m, 0:CT], lambda a, k: w_qkv[:, a, k, m * P:(m + 1) * P],
                                           lambda b, k: pair[:, b, k, bass.ds(c * CT, CT)], DC)
                    mm.then_inc(q_summed, 1)

                def apply(p, back):
                    pe.wait_ge(outer_split, CP * (g - back) + p + 1)
                    if p == 0:
                        pe.wait_ge(q_split, g)
                        if known(g, 2):
                            pe.wait_ge(y_split, g - 1)
                    for i in range(2):
                        cols = slice((2 * p + i) * TOK, (2 * p + i + 1) * TOK)
                        for m in range(DC):
                            mm = split_matmuls(pe, ps_y[:, m, cols], lambda a, _: outer_pair[:, p, a, i, m, :],
                                               lambda b, _: q_pair[:, (parity - back) % 2, b, m, cols], 1,
                                               first_start=(p == 0 and i == 0), check=False)
                    mm.then_inc(applied, 1)

                def project():
                    chunk, back = oldest
                    slot = s if back == 0 else 1 - s
                    w_proj = w_pair[:, slot, :, 6 * PIECE:8 * PIECE].rearrange("p a (c n) -> p a c n", c=DC)
                    pe.wait_ge(w_split, PIECES * (l - back + 1))
                    pe.wait_ge(y_split, g - 1)
                    pe.wait_ge(q_split, g if older else g - 1)
                    for m in range(DC):
                        mm = split_matmuls(pe, ps_x[:, m, 0:CT], lambda a, k: w_proj[:, a, k, m * P:(m + 1) * P],
                                           lambda b, k: y_pair[:, b, k, :], DC)
                    mm.then_inc(x_summed, 1)

                if first:
                    if isinstance(c, int) and c == 0:
                        pe.wait_ge(w_split, PIECES * l + 6)
                        pe.wait_ge(b_split, l + 1)
                    if not (isinstance(l, int) and l == 0):
                        pe.wait_ge(x_split, g - CHUNKS + 1)
                for p in range(CP):
                    if older:
                        outer_products(p)
                    if p == 3 and oldest:
                        project()
                    if p == 1 and oldest:
                        apply(3, 2)
                    if first:
                        keys_and_values(p)
                    if p == 0 and oldest:
                        apply(2, 2)
                    if p >= 2 and older:
                        apply(p - 2, 1)
                if first:
                    queries()

            all_steps(pe, step)


GATED = 8
RANK = 8


MIX = RANK + GATED


def final_constants(nc, ctx, d):
    def sb(name, shape, dt=F32):
        return ctx.enter_context(nc.sbuf_tensor(name, shape, dt))

    base_raw = sb("base_raw", [P, DC, D])
    mix_raw = sb("mix_raw", [P, DC, MIX])
    lora_raw = sb("lora_raw", [P, D])
    b_raw = sb("final_b_raw", [33, D + MIX])
    b_hi = sb("final_b_hi", [33, D + MIX], F16)
    c = Prepared()
    c.base_pair = sb("base_pair", [P, 2, DC, D], F16)
    c.mix_pair = sb("mix_pair", [P, 2, DC, MIX], F16)
    c.lora_pair = sb("lora_pair", [P, 2, D], F16)
    c.b_rows = sb("final_b_rows", [P, D + MIX], F16)
    c.ones = sb("ones_h", [P, P], F16)
    c.ident = sb("ident_h", [P, P])
    c.power = sb("power_h", [P, 1])
    c.gated = sb("gated", [P, 2, P])
    loaded, prep_g, prep_a, prep_v = [ctx.enter_context(nc.semaphore(name)) for name in ("h_loaded", "h_prep_g", "h_prep_a", "h_prep_v")]

    def sync(sp):
        sp.wait_ge(prep_g, 2)
        sp.dma_start(base_raw[:, :, :], d["base_w"]).then_inc(loaded, 16)
        sp.dma_start(mix_raw[:, :, 0:RANK], d["lora_a"]).then_inc(loaded, 16)
        sp.dma_start(mix_raw[:, :, RANK:MIX], d["router_w"]).then_inc(loaded, 16)
        sp.dma_start(lora_raw[0:GATED * RANK, :], d["lora_b"]).then_inc(loaded, 16)
        for row in (0, 32):
            sp.dma_start(b_raw[row:row + 1, 0:D], d["base_b"]).then_inc(loaded, 16)
            sp.dma_start(b_raw[row:row + 1, D + RANK:D + MIX], d["router_b"]).then_inc(loaded, 16)

    def gpsimd(pool):
        pool.memset(lora_raw[:, :], 0.0).then_inc(prep_g, 1)
        pool.memset(b_raw[:, :], 0.0).then_inc(prep_g, 1)
        pool.memset(c.ident[:, :], 0.0).then_inc(prep_g, 1)
        pool.wait_ge(prep_g, 3)
        pool.affine_select(out=c.ident[:, :], in_=c.ident[:, :], compare_op=ALU.not_equal, fill=1.0,
                           base=0, pattern=[[-1, P]], channel_multiplier=1)
        pool.memset(c.power[:, :], -0.5)
        pool.memset(c.ones[:, :], 1.0)
        pool.memset(c.gated[:, :, :], 0.0)
        pool.memset(c.b_rows[:, :], 0.0).then_inc(prep_g, 1)

    def scalar(act):
        act.wait_ge(prep_g, 4)
        act.wait_ge(loaded, 128)
        act.activation(c.base_pair[:, HI], base_raw[:, :, :], ACT.Copy, scale=WS)
        act.activation(c.mix_pair[:, HI], mix_raw[:, :, :], ACT.Copy, scale=WS)
        act.activation(c.lora_pair[:, HI, :], lora_raw[:, :], ACT.Copy, scale=2.0 * WS)
        act.activation(c.b_rows[0:1, :], b_raw[0:1, :], ACT.Copy, scale=WS)
        act.activation(b_hi[32:33, :], b_raw[32:33, :], ACT.Copy, scale=WS).then_inc(prep_a, 1)

    def vector(dve):
        dve.wait_ge(prep_a, 1)
        dve.scalar_tensor_tensor(c.base_pair[:, LO], base_raw[:, :, :], WS, c.base_pair[:, HI], ALU.mult, ALU.subtract)
        dve.scalar_tensor_tensor(c.mix_pair[:, LO], mix_raw[:, :, :], WS, c.mix_pair[:, HI], ALU.mult, ALU.subtract)
        dve.scalar_tensor_tensor(c.lora_pair[:, LO, :], lora_raw[:, :], 2.0 * WS, c.lora_pair[:, HI, :], ALU.mult, ALU.subtract)
        dve.scalar_tensor_tensor(c.b_rows[32:33, :], b_raw[32:33, :], WS, b_hi[32:33, :], ALU.mult, ALU.subtract).then_inc(prep_v, 1)

    c.sync, c.gpsimd, c.scalar, c.vector = sync, gpsimd, scalar, vector
    return c


def final_block(nc, d, keep, c):
    residual, state, bias_sum = keep["residual"], keep["state"], keep["bias_sum"]
    with ExitStack() as ctx:
        def sb(name, shape, dt=F32):
            return ctx.enter_context(nc.sbuf_tensor(name, shape, dt))

        def psum(name, shape, dt=F32):
            return ctx.enter_context(nc.psum_tensor(name, shape, dt))

        def sem(name):
            return ctx.enter_context(nc.semaphore(name))

        base_pair, mix_pair, lora_pair, b_rows = c.base_pair, c.mix_pair, c.lora_pair, c.b_rows
        ones, ident, power, gated = c.ones, c.ident, c.power, c.gated
        xb = sb("x_with_bias", [P, 2, DC, P])
        stats = sb("stats_h", [P, 2, 6])
        mean_var = sb("mean_var_h", [P, 2, 2])
        var_eps = sb("var_eps_h", [P, 2])
        rstd = sb("rstd_h", [P, 2])
        x3 = sb("x3", [P, 2, D])
        x3_pair = sb("x3_pair", [P, 2, 2, DC, P], F16)
        top = sb("top_h", [P, 2])
        neg_top = sb("neg_top_h", [P, 2])
        exps = sb("exps_h", [P, 2, GATED])
        sums = sb("sums_h", [P, 2])
        inv = sb("inv_h", [P, 2])
        gates = sb("gates", [P, 2, GATED], mybir.dt.bfloat16)
        mid = sb("mid", [P, 2, RANK])
        gated_pair = sb("gated_pair", [P, 2, 2, P], F16)
        out_tile = sb("out_tile", [P, 2, D])
        ps_x = psum("ps_x_back", [P, 2, 512])
        ps_t = psum("ps_x3_t", [P, 2, 512])
        ps_m = psum("ps_mixed", [P, 2, MIX])
        ps_g = psum("ps_gated_t", [P, 2, P])
        ps_b = psum("ps_out", [P, 2, 512])

        xb_made, turned_back, h_steps = sem("xb_made"), sem("turned_back"), sem("h_h_steps")
        rstd_made, x3_made = sem("h_rstd"), sem("x3_made")
        turned, x3_hi, x3_split, mixed = sem("h_turned"), sem("x3_hi"), sem("x3_split"), sem("mixed")
        top_steps, exp_made, gate_steps = sem("top_steps"), sem("h_exp_made"), sem("gate_steps")
        gated_turned, gated_hi, gated_split = sem("gated_turned"), sem("gated_hi"), sem("gated_split")
        based, summed, out_made = sem("based"), sem("out_summed"), sem("out_made")
        passed = sem("h_passed")
        stored = [sem("stored0"), sem("stored1")]
        block = ctx.enter_context(nc.Block())

        def later(t):
            return not isinstance(t, int) or t >= 2

        @block.sync
        def _(sp):
            def store(t, s):
                rows = P if not isinstance(t, int) else min(P, N - t * P)
                sp.wait_ge(out_made, t + 1)
                sp.dma_start(d["out"][bass.ds(t * P, rows), :], out_tile[0:rows, s, :]).then_inc(stored[s], 16)

            in_loop(sp, 0, TILES - 1, store)
            store(TILES - 1, (TILES - 1) % 2)
            sp.wait_ge(stored[0], 16 * ((TILES + 1) // 2))
            sp.wait_ge(stored[1], 16 * (TILES // 2))

        @block.gpsimd
        def _(pool):
            def inverse_root(t, s):
                pool.wait_ge(h_steps, 4 * t + 4)
                if later(t):
                    pool.wait_ge(x3_made, t - 1)
                pool.tensor_tensor(rstd[:, s:s + 1], var_eps[:, s:s + 1], power[:, :], ALU.pow).then_inc(rstd_made, 1)

            skewed(pool, TILES, (1, inverse_root))

        @block.scalar
        def _(act):
            def add_bias(t, s):
                if later(t):
                    act.wait_ge(turned_back, t - 1)
                for m in range(DC):
                    out = act.activation(xb[:, s, m, :], state[:, m, bass.ds(t * P, P)], ACT.Identity,
                                         bias=bias_sum[:, LAYERS, m:m + 1])
                out.then_inc(xb_made, 1)

            def turned_hi(t, s):
                act.wait_ge(turned, t + 1)
                if later(t):
                    act.wait_ge(based, t - 1)
                act.activation(x3_pair[:, s, HI], ps_t[:, s, 0:D].rearrange("p (c t) -> p c t", c=DC), ACT.Copy).then_inc(x3_hi, 1)

            def exp(t, s):
                act.wait_ge(top_steps, 2 * t + 2)
                if later(t):
                    act.wait_ge(gate_steps, 4 * t - 4)
                act.activation(exps[:, s, :], ps_m[:, s, RANK:MIX], ACT.Exp, bias=neg_top[:, s:s + 1], scale=1.0 / WS,
                               accum_out=sums[:, s:s + 1]).then_inc(exp_made, 1)

            def gated_to_hi(t, s):
                act.wait_ge(gated_turned, t + 1)
                if later(t):
                    act.wait_ge(summed, t - 1)
                act.activation(gated_pair[:, s, HI, :], ps_g[:, s, :], ACT.Copy).then_inc(gated_hi, 1)

            skewed(act, TILES, (0, add_bias), (4, turned_hi), (5, gated_to_hi), (4, exp))

        @block.vector
        def _(dve):
            def add_x(t, s):
                dve.wait_ge(turned_back, t + 1)
                h = residual[:, bass.ds(t, 1), :]
                dve.tensor_tensor(h, h, ps_x[:, s:s + 1, 0:D], ALU.add).then_inc(h_steps, 1)
                wait_apart(dve, h_steps, 4 * t + 1, passed)
                dve.bn_stats(stats[:, s, :], h).then_inc(h_steps, 1)
                wait_apart(dve, h_steps, 4 * t + 2, passed)
                dve.bn_aggr(mean_var[:, s, :], stats[:, s, :]).then_inc(h_steps, 1)
                dve.wait_ge(h_steps, 4 * t + 3)
                if later(t):
                    dve.wait_ge(rstd_made, t - 1)
                dve.tensor_scalar(var_eps[:, s:s + 1], mean_var[:, s, 1:2], EPS, None, ALU.add).then_inc(h_steps, 1)

            def norm(t, s):
                dve.wait_ge(rstd_made, t + 1)
                if later(t):
                    dve.wait_ge(turned, t - 1)
                dve.tensor_scalar(x3[:, s:s + 1, :], residual[:, bass.ds(t, 1), :], mean_var[:, s, 0:1], rstd[:, s:s + 1],
                                  ALU.subtract, ALU.mult).then_inc(x3_made, 1)

            def turned_lo(t, s):
                dve.wait_ge(x3_hi, t + 1)
                dve.tensor_tensor(x3_pair[:, s, LO], ps_t[:, s, 0:D].rearrange("p (c t) -> p c t", c=DC), x3_pair[:, s, HI],
                                  ALU.subtract).then_inc(x3_split, 1)

            def highest(t, s):
                dve.wait_ge(mixed, t + 1)
                dve.tensor_reduce(top[:, s:s + 1], ps_m[:, s, RANK:MIX], AX.X, ALU.max).then_inc(top_steps, 1)
                dve.wait_ge(top_steps, 2 * t + 1)
                dve.tensor_scalar(neg_top[:, s:s + 1], top[:, s:s + 1], -1.0 / WS, None, ALU.mult).then_inc(top_steps, 1)

            def gate(t, s):
                dve.wait_ge(exp_made, t + 1)
                dve.reciprocal(inv[:, s:s + 1], sums[:, s:s + 1]).then_inc(gate_steps, 1)
                dve.tensor_scalar(mid[:, s, :], ps_m[:, s, 0:RANK], 1.0 / WS, None, ALU.mult).then_inc(gate_steps, 1)
                dve.wait_ge(gate_steps, 4 * t + 1)
                dve.tensor_scalar(gates[:, s, :], exps[:, s, :], inv[:, s:s + 1], None, ALU.mult).then_inc(gate_steps, 1)
                dve.wait_ge(gate_steps, 4 * t + 3)
                if later(t):
                    dve.wait_ge(gated_turned, t - 1)
                dve.tensor_tensor(gated[:, s, 0:GATED * RANK].rearrange("p (e r) -> p e r", r=RANK),
                                  gates[:, s, :, None].to_broadcast([P, GATED, RANK]),
                                  mid[:, s, None, :].to_broadcast([P, GATED, RANK]), ALU.mult).then_inc(gate_steps, 1)

            def gated_to_lo(t, s):
                dve.wait_ge(gated_hi, t + 1)
                dve.tensor_tensor(gated_pair[:, s, LO, :], ps_g[:, s, :], gated_pair[:, s, HI, :], ALU.subtract).then_inc(gated_split, 1)

            def finish(t, s):
                dve.wait_ge(summed, t + 1)
                if later(t):
                    dve.wait_ge(stored[s], 8 * t - 8 * s)
                dve.scalar_tensor_tensor(out_tile[:, s:s + 1, :], ps_b[:, s:s + 1, 0:D], 1.0 / WS, residual[:, bass.ds(t, 1), :],
                                         ALU.mult, ALU.add).then_inc(out_made, 1)

            skewed(dve, TILES, (5, gate), (3, norm), (4, turned_lo), (1, add_x), (4, highest), (5, gated_to_lo), (6, finish))

        @block.tensor
        def _(pe):
            def turn_back(t, s):
                pe.wait_ge(xb_made, t + 1)
                if later(t):
                    pe.wait_ge(h_steps, 4 * t - 7)
                for c in range(DC):
                    mm = pe.transpose(ps_x[:, s, c * P:(c + 1) * P], xb[:, s, c, :], ident[:, :])
                mm.then_inc(turned_back, 1)

            def turn(t, s):
                pe.wait_ge(x3_made, t + 1)
                if later(t):
                    pe.wait_ge(x3_split, t - 1)
                for c in range(DC):
                    mm = pe.transpose(ps_t[:, s, c * P:(c + 1) * P], x3[:, s, c * P:(c + 1) * P], ident[:, :])
                mm.then_inc(turned, 1)

            def mix(t, s):
                pe.wait_ge(x3_split, t + 1)
                if later(t):
                    pe.wait_ge(gate_steps, 4 * t - 4)
                pe.matmul(ps_m[:, s, :], ones[:, :], b_rows[:, D:D + MIX], start=True, stop=False)
                split_matmuls(pe, ps_m[:, s, :], lambda a, c: x3_pair[:, s, a, c, :], lambda b, c: mix_pair[:, b, c, :], DC,
                              first_start=False).then_inc(mixed, 1)

            def base(t, s):
                if later(t):
                    pe.wait_ge(out_made, t - 1)
                pe.matmul(ps_b[:, s, 0:D], ones[:, :], b_rows[:, 0:D], start=True, stop=False, skip_group_check=True)
                for n, (c, a, b) in enumerate((c, a, b) for c in range(DC) for a, b in ((HI, HI), (HI, LO), (LO, HI))):
                    mm = pe.matmul(ps_b[:, s, 0:D], x3_pair[:, s, a, c, :], base_pair[:, b, c, :], start=False, stop=False,
                                   skip_group_check=True)
                mm.then_inc(based, 1)

            def turn_gated(t, s):
                pe.wait_ge(gate_steps, 4 * t + 4)
                if later(t):
                    pe.wait_ge(gated_split, t - 1)
                pe.transpose(ps_g[:, s, :], gated[:, s, :], ident[:, :]).then_inc(gated_turned, 1)

            def add_lora(t, s):
                pe.wait_ge(gated_split, t + 1)
                split_matmuls(pe, ps_b[:, s, 0:D], lambda a, _: gated_pair[:, s, a, :], lambda b, _: lora_pair[:, b, :], 1,
                              first_start=False, check=False).then_inc(summed, 1)

            skewed(pe, TILES, (0, turn_back), (6, add_lora), (5, turn_gated), (3, turn), (4, mix), (5, base))


def vit_tower(nc, d):
    keep = {
        "queue": nc.dram_tensor("queue", (QUEUE_TILES * ROWS, D), F32, kind="Internal").ap(),
        "answers": nc.dram_tensor("answers", (QUEUE_TILES * ROWS, D), F32, kind="Internal").ap(),
    }

    def hold(ctx, name, shape, dt=F32):
        keep[name] = ctx.enter_context(nc.sbuf_tensor(name, shape, dt))

    with ExitStack() as whole:
        hold(whole, "residual", [P, TILES, D])
        hold(whole, "chan_a", [P, 2, DC, NPAD], F16)
        hold(whole, "weights", [P, TOP, TILES])
        hold(whole, "places", [P, TOP, TILES], I32)
        hold(whole, "bounds", [P, 2, EXPERTS], I32)
        hold(whole, "bias_sum", [P, LAYERS + 1, DC])
        embed_and_norm(nc, d, keep)
        with ExitStack() as early:
            hold(early, "chan_b", [P, 2, DC, NPAD], F16)
            channel_attention(nc, d, keep)
            hold(early, "rows", [P, TILES, D])
            project_and_route(nc, d, keep)
        experts(nc, d, keep)
        hold(whole, "state", [P, DC, NPAD])
        of_layers = layer_constants(nc, whole, d, keep)
        gather_and_norm(nc, d, keep, of_layers)
        of_final = final_constants(nc, whole, d)
        linear_attention_layers(nc, d, keep, of_layers, of_final)
        final_block(nc, d, keep, of_final)




def lay_out(x, L0_tok_W, L0_tok_b, L0_attn_norm_w, L0_attn_norm_b, L0_attn_qkv_w, L0_attn_qkv_b, L0_attn_proj_w,
            L0_attn_proj_b, L0_ffn_W_gate, L0_ffn_W_in, L0_ffn_b_in, L0_ffn_W_out, L0_ffn_b_out, L1_attn_Wqkv,
            L1_attn_bqkv, L1_attn_Wproj, L1_attn_bproj, L1_ffn_base_w, L1_ffn_base_b, L1_ffn_lora_A, L1_ffn_lora_B,
            L1_ffn_router_w, L1_ffn_router_b):
    def rows(w):
        return w.reshape(-1, P, w.shape[-1]).transpose(1, 0, 2)

    patches = x.reshape(IMAGES, CHANS, SIDE, PATCH, SIDE, PATCH).transpose(0, 2, 4, 1, 3, 5).reshape(N, FEAT)
    padded = np.zeros((NPAD, FEAT), x.dtype)
    padded[:N] = patches
    return {
        "patches": padded.reshape(TILES, P, FC, P).transpose(0, 3, 2, 1).reshape(TILES, P, FC * P),
        "tok_w": rows(L0_tok_W.T), "tok_b": L0_tok_b,
        "norm_w": L0_attn_norm_w, "norm_b": L0_attn_norm_b,
        "qkv0_w": rows(L0_attn_qkv_w.T), "qkv0_b": L0_attn_qkv_b.reshape(1, -1),
        "qkv0_bcol": L0_attn_qkv_b.reshape(-1, P).T,
        "proj0_w": rows(L0_attn_proj_w.T), "proj0_b": L0_attn_proj_b.reshape(1, -1),
        "gate_w": rows(L0_ffn_W_gate),
        "in_w": np.stack([rows(w) for w in L0_ffn_W_in]), "in_b": L0_ffn_b_in.reshape(-1, 8, P).transpose(2, 0, 1),
        "out_w": np.stack([rows(w) for w in L0_ffn_W_out]), "out_b": L0_ffn_b_out.reshape(1, -1),
        "qkv1_w": np.stack([rows(w.T) for w in L1_attn_Wqkv]), "qkv1_b": L1_attn_bqkv,
        "q1_bcol": L1_attn_bqkv[:, :D].reshape(-1, DC, P).transpose(2, 0, 1),
        "proj1_w": np.stack([rows(w.T) for w in L1_attn_Wproj]),
        "proj1_bcol": L1_attn_bproj.reshape(-1, DC, P).transpose(2, 0, 1),
        "base_w": rows(L1_ffn_base_w.T), "base_b": L1_ffn_base_b.reshape(1, -1),
        "lora_a": rows(L1_ffn_lora_A), "lora_b": L1_ffn_lora_B.reshape(-1, D),
        "router_w": rows(L1_ffn_router_w.T), "router_b": L1_ffn_router_b.reshape(1, -1),
    }


def kernel(**inputs):
    import concourse.bacc as bacc
    from concourse.bass_utils import run_bass_kernel_spmd

    nc = bacc.Bacc("TRN2", target_bir_lowering=False, num_devices=1)
    arrays, d = {}, {}
    for name, a in lay_out(**{k: np.asarray(v) for k, v in inputs.items()}).items():
        a = np.ascontiguousarray(a)
        arrays[f"in_{name}_dram"] = a
        d[name] = nc.dram_tensor(f"in_{name}_dram", a.shape, mybir.dt.from_np(a.dtype), kind="ExternalInput").ap()
    d["out"] = nc.dram_tensor("out_dram", (N, D), F32, kind="ExternalOutput").ap()
    vit_tower(nc, d)
    r = run_bass_kernel_spmd(nc, [arrays], core_ids=[0])
    return r.results[0]["out_dram"].reshape(IMAGES, TOK, D)
```

```python
from contextlib import ExitStack

import numpy as np

import concourse.bass as bass
from concourse import mybir

F32 = mybir.dt.float32
F16 = mybir.dt.float16
I32 = mybir.dt.int32
ACT = mybir.ActivationFunctionType
ALU = mybir.AluOpType
AX = mybir.AxisListType

P = 128
IMAGES, SIDE, PATCH, CHANS = 64, 7, 16, 3
TOK = SIDE * SIDE
N = IMAGES * TOK
TILES = -(-N // P)
NPAD = TILES * P
FEAT = CHANS * PATCH * PATCH
FC = FEAT // P
D = 256
DC = D // P
PAIRS = IMAGES // 2
PT = 2 * TOK
EPS = 1e-5
WS = 256.0
HI, LO = 0, 1
EXPERTS, TOP, HIDDEN = 8, 2, 1024
MC = HIDDEN // P
ROWS = 2 * P
LEAST_TILES = 2
EXPERT_TILES = (TOP * N + EXPERTS * LEAST_TILES * ROWS) // ROWS
MOST_OF_ONE = -(-N // ROWS)
QUEUE_TILES = EXPERT_TILES + MOST_OF_ONE + 1
SURE_TILES = TOP * N // ROWS
ZERO_ROWS = 4
ZERO_PART = P * ZERO_ROWS


class Prepared:
    pass


def in_loop(eng, first, last, step):
    if first < last and first % 2:
        step(first, 1)
        first += 1
    rounds = (last - first) // 2
    if rounds >= 2:
        with eng.Fori(0, rounds) as j:
            step(first + 2 * j, 0)
            step(first + 2 * j + 1, 1)
        first += 2 * rounds
    for i in range(first, last):
        step(i, i % 2)


def skewed(eng, n, *stages):
    deepest = max(lag for lag, _ in stages)

    def step(i, parity):
        for lag, f in stages:
            if not isinstance(i, int) or 0 <= i - lag < n:
                f(i - lag, (parity - lag) % 2)

    peeled = deepest + SLOTS
    for i in range(peeled):
        step(i, i % 2)
    in_loop(eng, peeled, n, step)
    for i in range(n, n + deepest):
        step(i, i % 2)


def later(i):
    return not isinstance(i, int) or i >= SLOTS


def wait_apart(eng, sem, value, passed):
    eng.wait_ge(sem, value)
    eng.sem_inc(passed, 1)


SLOTS = 2


def free(i):
    return i + 1


def made(i):
    return i + 1 + SLOTS


def landed(i, parity):
    return 8 * i + 16 - 8 * parity


def split_matmuls(pe, out, left, right, chunks, first_start=True, check=True):
    terms = [(c, a, b) for c in range(chunks) for a, b in ((HI, HI), (HI, LO), (LO, HI))]
    for n, (c, a, b) in enumerate(terms):
        mm = pe.matmul(out, left(a, c), right(b, c), start=first_start and n == 0, stop=n == len(terms) - 1,
                       skip_group_check=not check)
    return mm


def embed_and_norm(nc, d, keep):
    residual, normed_t = keep["residual"], keep["chan_a"]
    with ExitStack() as ctx:
        def sb(name, shape, dt=F32):
            return ctx.enter_context(nc.sbuf_tensor(name, shape, dt))

        def sem(name):
            return ctx.enter_context(nc.semaphore(name))

        patches = sb("patches", [P, 2, FC, P])
        patches_pair = sb("patches_pair", [P, 2, 2, FC, P], F16)
        w_raw = sb("tok_w_raw", [P, FC, D])
        w_pair = sb("tok_w_pair", [P, 2, FC, D], F16)
        tok_b = sb("tok_b_all", [P, D])
        norm_w = sb("norm_w_all", [P, D])
        norm_b = sb("norm_b_all", [P, D])
        ident = sb("ident_a", [P, P])
        eps = sb("eps_a", [P, 1])
        stats = sb("stats", [P, 2, 6])
        mean_var = sb("mean_var", [P, 2, 2])
        std = sb("std", [P, 2])
        rstd = sb("rstd", [P, 2])
        x0 = sb("x0", [P, 2, D])
        stats2 = sb("stats2", [P, 2, 6])
        mean_var2 = sb("mean_var2", [P, 2, 2])
        std2 = sb("std2", [P, 2])
        rstd2 = sb("rstd2", [P, 2])
        n0 = sb("n0", [P, 2, D])
        n1 = sb("n1", [P, 2, D])
        ps_embed = ctx.enter_context(nc.psum_tensor("ps_embed", [P, 2, 512], F32))
        ps_t = ctx.enter_context(nc.psum_tensor("ps_normed_t", [P, 2, 512], F32))

        passed = keep["passed"]
        consts_loaded, w_loaded = sem("consts_loaded"), sem("w_loaded")
        patches_loaded = [sem("patches_loaded0"), sem("patches_loaded1")]
        w_steps, ident_made = sem("w_steps"), sem("ident_made")
        patches_hi, patches_split = sem("patches_hi"), sem("patches_split")
        embedded, h_made, h_summed, h_known = sem("embedded"), sem("h_made"), sem("h_summed"), sem("h_known")
        std_made, rstd_made, x0_made = sem("std_made"), sem("rstd_made"), sem("x0_made")
        x0_summed, x0_known, residual_made = sem("x0_summed"), sem("x0_known"), sem("residual_made")
        std2_made, rstd2_made, n0_made, nw_made, n1_made = sem("std2_made"), sem("rstd2_made"), sem("n0_made"), sem("nw_made"), sem("n1_made")
        transposed, t_hi, t_split = sem("transposed"), sem("t_hi"), sem("t_split")
        block = ctx.enter_context(nc.Block())

        @block.sync
        def _(sp):
            sp.dma_start(w_raw[:, :, :], d["tok_w"]).then_inc(w_loaded, 16)

            def load(t, s):
                sp.wait_ge(patches_split, free(t))
                sp.dma_start(patches[:, s:s + 1, :, :].rearrange("p a c t -> p (a c t)"),
                             d["patches"][bass.ds(t, 1)].rearrange("a p n -> (a p) n")).then_inc(patches_loaded[s], 16)

            in_loop(sp, 0, TILES, load)

        @block.scalar
        def _(act):
            act.dma_start(tok_b[:, :], d["tok_b"].partition_broadcast(P)).then_inc(consts_loaded, 16)
            act.dma_start(norm_w[:, :], d["norm_w"].partition_broadcast(P)).then_inc(consts_loaded, 16)
            act.dma_start(norm_b[:, :], d["norm_b"].partition_broadcast(P)).then_inc(consts_loaded, 16)
            act.wait_ge(w_loaded, 16)
            act.activation(w_pair[:, HI, :, :], w_raw[:, :, :], ACT.Copy, scale=WS).then_inc(w_steps, 1)

            def hi(t, s):
                act.wait_ge(patches_loaded[s], landed(t, s))
                act.wait_ge(embedded, free(t))
                act.activation(patches_pair[:, s, HI, :, :], patches[:, s, :, :], ACT.Copy).then_inc(patches_hi, 1)

            def root(t, s):
                act.wait_ge(h_known, t + 1)
                act.activation(std[:, s:s + 1], mean_var[:, s, 1:2], ACT.Sqrt, bias=eps[:, 0:1]).then_inc(std_made, 1)

            def root2(t, s):
                act.wait_ge(x0_known, t + 1)
                act.activation(std2[:, s:s + 1], mean_var2[:, s, 1:2], ACT.Sqrt, bias=eps[:, 0:1]).then_inc(std2_made, 1)

            def out_hi(t, s):
                act.wait_ge(transposed, made(t))
                act.activation(normed_t[:, HI, :, bass.ds(t * P, P)],
                               ps_t[:, s, 0:D].rearrange("p (c t) -> p c t", c=DC), ACT.Copy).then_inc(t_hi, 1)

            act.wait_ge(ident_made, 3)
            skewed(act, TILES, (0, hi), (2, root), (5, out_hi), (3, root2))

        @block.gpsimd
        def _(pool):
            pool.memset(ident[:, :], 0.0).then_inc(ident_made, 1)
            pool.wait_ge(ident_made, 1)
            pool.affine_select(out=ident[:, :], in_=ident[:, :], compare_op=ALU.not_equal, fill=1.0,
                               base=0, pattern=[[-1, P]], channel_multiplier=1).then_inc(ident_made, 1)
            pool.memset(eps[:, :], EPS).then_inc(ident_made, 1)
            pool.sem_inc(patches_split, SLOTS)

            def lo(t, s):
                pool.wait_ge(patches_hi, t + 1)
                pool.tensor_tensor(patches_pair[:, s, LO, :, :], patches[:, s, :, :], patches_pair[:, s, HI, :, :],
                                   ALU.subtract).then_inc(patches_split, 1)

            def add_x0(t, s):
                pool.wait_ge(x0_made, t + 1)
                row = residual[:, bass.ds(t, 1), :]
                pool.tensor_tensor(row, row, x0[:, s:s + 1, :], ALU.add).then_inc(residual_made, 1)

            skewed(pool, TILES, (0, lo), (3, add_x0))

        @block.vector
        def _(dve):
            dve.sem_inc(h_made, SLOTS)
            dve.sem_inc(t_split, SLOTS)
            dve.wait_ge(w_steps, 1)
            dve.scalar_tensor_tensor(w_pair[:, LO, :, :].rearrange("p c n -> p (c n)"), w_raw[:, :, :].rearrange("p c n -> p (c n)"), WS,
                                     w_pair[:, HI, :, :].rearrange("p c n -> p (c n)"), ALU.mult, ALU.subtract).then_inc(w_steps, 1)
            dve.wait_ge(consts_loaded, 48)

            def make_h(t, s):
                dve.wait_ge(embedded, made(t))
                dve.scalar_tensor_tensor(residual[:, bass.ds(t, 1), :], ps_embed[:, s:s + 1, 0:D], 1.0 / WS, tok_b[:, None, :],
                                         ALU.mult, ALU.add).then_inc(h_made, 1)

            def h_stats(t, s):
                wait_apart(dve, h_made, made(t), passed)
                dve.bn_stats(stats[:, s, :], residual[:, bass.ds(t, 1), :]).then_inc(h_summed, 1)

            def h_mean_var(t, s):
                if later(t):
                    dve.wait_ge(x0_made, t - 1)
                wait_apart(dve, h_summed, t + 1, passed)
                dve.bn_aggr(mean_var[:, s, :], stats[:, s, :]).then_inc(h_known, 1)

            def invert(t, s):
                dve.wait_ge(std_made, t + 1)
                dve.reciprocal(rstd[:, s:s + 1], std[:, s:s + 1]).then_inc(rstd_made, 1)

            def norm(t, s):
                dve.wait_ge(rstd_made, t + 1)
                if later(t):
                    dve.wait_ge(residual_made, t - 1)
                    dve.wait_ge(n0_made, t - 1)
                dve.tensor_scalar(x0[:, s:s + 1, :], residual[:, bass.ds(t, 1), :], mean_var[:, s, 0:1], rstd[:, s:s + 1],
                                  ALU.subtract, ALU.mult).then_inc(x0_made, 1)

            def x0_stats(t, s):
                wait_apart(dve, x0_made, t + 1, passed)
                dve.bn_stats(stats2[:, s, :], x0[:, s, :]).then_inc(x0_summed, 1)

            def x0_mean_var(t, s):
                if later(t):
                    dve.wait_ge(n0_made, t - 1)
                wait_apart(dve, x0_summed, t + 1, passed)
                dve.bn_aggr(mean_var2[:, s, :], stats2[:, s, :]).then_inc(x0_known, 1)

            def invert2(t, s):
                dve.wait_ge(std2_made, t + 1)
                dve.reciprocal(rstd2[:, s:s + 1], std2[:, s:s + 1]).then_inc(rstd2_made, 1)

            def norm2(t, s):
                dve.wait_ge(rstd2_made, t + 1)
                if later(t):
                    dve.wait_ge(n1_made, t - 1)
                dve.tensor_scalar(n0[:, s, :], x0[:, s, :], mean_var2[:, s, 0:1], rstd2[:, s:s + 1],
                                  ALU.subtract, ALU.mult).then_inc(n0_made, 1)

            def times_w(t, s):
                dve.wait_ge(n0_made, t + 1)
                dve.tensor_tensor(n0[:, s, :], n0[:, s, :], norm_w[:, :], ALU.mult).then_inc(nw_made, 1)

            def plus_b(t, s):
                dve.wait_ge(nw_made, t + 1)
                dve.wait_ge(transposed, free(t))
                dve.tensor_tensor(n1[:, s, :], n0[:, s, :], norm_b[:, :], ALU.add).then_inc(n1_made, 1)

            def out_lo(t, s):
                dve.wait_ge(t_hi, t + 1)
                dve.tensor_tensor(normed_t[:, LO, :, bass.ds(t * P, P)],
                                  ps_t[:, s, 0:D].rearrange("p (c t) -> p c t", c=DC),
                                  normed_t[:, HI, :, bass.ds(t * P, P)], ALU.subtract).then_inc(t_split, 1)

            skewed(dve, TILES, (0, make_h), (1, invert), (2, invert2), (0, h_stats), (2, norm2), (1, norm), (5, out_lo),
                   (1, x0_stats), (0, h_mean_var), (2, times_w), (1, x0_mean_var), (2, plus_b))

        @block.tensor
        def _(pe):
            pe.sem_inc(embedded, SLOTS)
            pe.sem_inc(transposed, SLOTS)
            pe.wait_ge(w_steps, 2)
            pe.wait_ge(ident_made, 2)

            def embed(t, s):
                pe.wait_ge(patches_split, made(t))
                pe.wait_ge(h_made, free(t))
                split_matmuls(pe, ps_embed[:, s, 0:D], lambda a, c: patches_pair[:, s, a, c, :],
                              lambda b, c: w_pair[:, b, c, :], FC).then_inc(embedded, 1)

            def turn(t, s):
                pe.wait_ge(n1_made, t + 1)
                pe.wait_ge(t_split, free(t))
                for c in range(DC):
                    mm = pe.transpose(ps_t[:, s, c * P:(c + 1) * P], n1[:, s, c * P:(c + 1) * P], ident[:, :])
                mm.then_inc(transposed, 1)

            skewed(pe, TILES, (0, embed), (4, turn))


def channel_attention(nc, d, keep):
    normed_t, attended_t = keep["chan_a"], keep["chan_b"]
    scale = 1.0 / float(np.sqrt(TOK))
    with ExitStack() as ctx:
        def sb(name, shape, dt=F32):
            return ctx.enter_context(nc.sbuf_tensor(name, shape, dt))

        def psum(name, shape, dt=F32):
            return ctx.enter_context(nc.psum_tensor(name, shape, dt))

        def sem(name):
            return ctx.enter_context(nc.semaphore(name))

        w_raw = sb("qkv_w_raw", [P, DC, 3 * D])
        w_pair = sb("qkv_w_pair", [P, 2, DC, 3 * D], F16)
        bias_raw = sb("qk_b_raw", [33, 2 * D])
        bias_hi = sb("qk_b_hi", [33, 2 * D], F16)
        bias_rows = sb("qk_bias_rows", [P, 2 * D], F16)
        ones = sb("ones_b", [P, P], F16)
        v_b = sb("v_b", [P, 6])
        v_bs = sb("v_b_scaled", [P, DC])
        ident = sb("ident_b", [P, P])
        own = sb("own_image", [PT, 2])
        q_pair = sb("q_pair", [PT, 2, 2, 2, D], F16)
        k_pair = sb("k_pair", [PT, 2, 2, D], F16)
        v_pair = sb("v_pair", [P, 2, 2, DC, PT], F16)
        neg_max = sb("neg_max", [P, 2, DC])
        neg_scaled = sb("neg_scaled", [P, 2, DC])
        exps = sb("exps", [P, 2, DC, D])
        sums = sb("sums", [P, 2, DC])
        sums_s = sb("sums_scaled", [P, 2, DC])
        inv = sb("inv_sums", [P, 2, DC])
        et_pair = sb("exps_t_pair", [P, 2, 2, DC, D], F16)
        zeros = sb("zeros", [P, ZERO_ROWS * D])
        queue_rows, answer_rows = [keep[name].rearrange("(g p r) n -> g p (r n)", p=P, r=ZERO_ROWS) for name in ("queue", "answers")]
        cleared = sem("queue_cleared")
        ps_qk = psum("ps_qk", [P, 512])
        ps_v = psum("ps_v", [P, 512])
        ps_s = psum("ps_scores", [P, 2, DC, D])
        ps_e = psum("ps_exps_t", [P, 2, DC, D])
        ps_a = psum("ps_attended", [P, 2, 512])

        loaded, prep = sem("qkv_loaded"), sem("qkv_prep")
        w_hi, prep_v, prep_g = sem("qkv_w_hi"), sem("qkv_prep_v"), sem("qkv_prep_g")
        projected_qk, projected_v = sem("projected_qk"), sem("projected_v")
        qk_hi, qk_split, v_hi, v_split = sem("qk_hi"), sem("qk_split"), sem("v_hi"), sem("v_split")
        scored, max_steps, exp_steps = sem("scored"), sem("max_steps"), sem("exp_steps")
        turned, et_hi, et_split = sem("turned"), sem("et_hi"), sem("et_split")
        inv_steps, attended, a_hi, a_split = sem("inv_steps"), sem("attended"), sem("a_hi"), sem("a_split")
        block = ctx.enter_context(nc.Block())

        def images_of(f):
            return (lambda p, s: f(2 * p, 0)), (lambda p, s: f(2 * p + 1, 1))

        @block.sync
        def _(sp):
            sp.dma_start(w_raw[:, :, :], d["qkv0_w"]).then_inc(loaded, 16)
            sp.dma_start(bias_raw[0:1, :], d["qkv0_b"][:, 0:2 * D]).then_inc(loaded, 16)
            sp.dma_start(bias_raw[32:33, :], d["qkv0_b"][:, 0:2 * D]).then_inc(loaded, 16)
            sp.dma_start(v_b[:, :], d["qkv0_bcol"]).then_inc(loaded, 16)
            sp.wait_ge(prep_g, 7)
            parts = 0
            for rows, first, last in ((queue_rows, 0, EXPERT_TILES + 1), (answer_rows, SURE_TILES, EXPERT_TILES)):
                for g in range(first * ROWS // ZERO_PART, -(-last * ROWS // ZERO_PART)):
                    sp.dma_start(rows[g], zeros[:, :]).then_inc(cleared, 16)
                    parts += 1
            sp.wait_ge(cleared, 16 * parts)

        @block.gpsimd
        def _(pool):
            pool.memset(ident[:, :], 0.0).then_inc(prep_g, 1)
            pool.memset(own[:, :], 1.0 / WS).then_inc(prep_g, 1)
            pool.memset(ones[:, :], 1.0).then_inc(prep_g, 1)
            pool.wait_ge(prep_g, 2)
            pool.affine_select(out=ident[:, :], in_=ident[:, :], compare_op=ALU.not_equal, fill=1.0,
                               base=0, pattern=[[-1, P]], channel_multiplier=1).then_inc(prep_g, 1)
            pool.affine_select(out=own[:, 0:1], in_=own[:, 0:1], compare_op=ALU.is_ge, fill=0.0,
                               base=TOK - 1, pattern=[[0, 1]], channel_multiplier=-1).then_inc(prep_g, 1)
            pool.affine_select(out=own[:, 1:2], in_=own[:, 1:2], compare_op=ALU.is_ge, fill=0.0,
                               base=-TOK, pattern=[[0, 1]], channel_multiplier=1).then_inc(prep_g, 1)
            pool.memset(zeros[:, :], 0.0).then_inc(prep_g, 1)

        @block.scalar
        def _(act):
            act.wait_ge(loaded, 64)
            act.activation(w_pair[:, HI, :, :], w_raw[:, :, :], ACT.Copy, scale=WS).then_inc(w_hi, 1)
            act.wait_ge(prep_v, 1)
            act.activation(bias_rows[0:1, :], bias_raw[0:1, :], ACT.Copy, scale=WS).then_inc(w_hi, 1)
            act.activation(bias_hi[32:33, :], bias_raw[32:33, :], ACT.Copy, scale=WS).then_inc(w_hi, 1)
            act.activation(v_bs[:, :], v_b[:, 4:6], ACT.Copy, scale=WS).then_inc(w_hi, 1)
            act.wait_ge(w_hi, 4)
            act.wait_ge(prep_g, 6)

            def project_hi(p, s):
                act.wait_ge(projected_qk, p + 1)
                if not isinstance(p, int) or p >= 2:
                    act.wait_ge(scored, 2 * p - 2)
                for image in (0, 1):
                    act.activation(q_pair[:, s, HI, image, :], ps_qk[0:PT, 0:D], ACT.Copy, scale=own[:, image:image + 1])
                act.activation(k_pair[:, s, HI, :], ps_qk[0:PT, D:2 * D], ACT.Copy, scale=1.0 / WS).then_inc(qk_hi, 1)
                act.wait_ge(projected_v, p + 1)
                if not isinstance(p, int) or p >= 2:
                    act.wait_ge(attended, 2 * p - 2)
                for c in range(DC):
                    out = act.activation(v_pair[:, s, HI, c, :], ps_v[:, c * PT:(c + 1) * PT], ACT.Identity, bias=v_bs[:, c:c + 1])
                out.then_inc(v_hi, 1)

            def exp(n, s):
                act.wait_ge(max_steps, 2 * n + 2)
                if not isinstance(n, int) or n >= 2:
                    act.wait_ge(turned, n - 1)
                for c in range(DC):
                    act.activation(exps[:, s, c, :], ps_s[:, s, c, :], ACT.Exp, bias=neg_scaled[:, s, c:c + 1], scale=scale,
                                   accum_out=sums[:, s, c:c + 1]).then_inc(exp_steps, 1)

            def turned_hi(n, s):
                act.wait_ge(turned, n + 1)
                if not isinstance(n, int) or n >= 2:
                    act.wait_ge(attended, n - 1)
                act.activation(et_pair[:, s, HI, :, :], ps_e[:, s, :, :], ACT.Copy).then_inc(et_hi, 1)

            def attended_hi(n, s):
                act.wait_ge(attended, n + 1)
                act.wait_ge(inv_steps, 2 * n + 2)
                for c in range(DC):
                    out = act.activation(attended_t[:, HI, c, bass.ds(n * TOK, TOK)], ps_a[:, s, c * TOK:(c + 1) * TOK], ACT.Copy,
                                         scale=inv[:, s, c:c + 1])
                out.then_inc(a_hi, 1)

            exp0, exp1 = images_of(exp)
            turned_hi0, turned_hi1 = images_of(turned_hi)
            attended_hi0, attended_hi1 = images_of(attended_hi)
            skewed(act, PAIRS, (2, turned_hi0), (2, turned_hi1), (0, project_hi), (2, attended_hi0), (1, exp0),
                   (1, exp1), (2, attended_hi1))

        @block.vector
        def _(dve):
            dve.memset(bias_rows[:, :], 0.0).then_inc(prep_v, 1)
            dve.wait_ge(w_hi, 4)
            dve.wait_ge(loaded, 64)
            dve.scalar_tensor_tensor(w_pair[:, LO, :, :].rearrange("p c n -> p (c n)"), w_raw[:, :, :].rearrange("p c n -> p (c n)"), WS,
                                     w_pair[:, HI, :, :].rearrange("p c n -> p (c n)"), ALU.mult, ALU.subtract).then_inc(prep_v, 1)
            dve.wait_ge(prep_v, 1)
            dve.scalar_tensor_tensor(bias_rows[32:33, :], bias_raw[32:33, :], WS, bias_hi[32:33, :],
                                     ALU.mult, ALU.subtract).then_inc(prep_v, 1)
            dve.wait_ge(prep_g, 6)

            def project_lo(p, s):
                dve.wait_ge(qk_hi, p + 1)
                for image in (0, 1):
                    dve.scalar_tensor_tensor(q_pair[:, s, LO, image, :], ps_qk[0:PT, 0:D], own[:, image:image + 1],
                                             q_pair[:, s, HI, image, :], ALU.mult, ALU.subtract)
                dve.scalar_tensor_tensor(k_pair[:, s, LO, :], ps_qk[0:PT, D:2 * D], 1.0 / WS, k_pair[:, s, HI, :],
                                         ALU.mult, ALU.subtract).then_inc(qk_split, 1)
                dve.wait_ge(v_hi, p + 1)
                for c in range(DC):
                    out = dve.scalar_tensor_tensor(v_pair[:, s, LO, c, :], ps_v[:, c * PT:(c + 1) * PT], v_bs[:, c:c + 1],
                                                   v_pair[:, s, HI, c, :], ALU.add, ALU.subtract)
                out.then_inc(v_split, 1)

            def row_max(n, s):
                dve.wait_ge(scored, n + 1)
                if not isinstance(n, int) or n >= 2:
                    dve.wait_ge(exp_steps, 2 * n - 2)
                dve.tensor_reduce(neg_max[:, s, :], ps_s[:, s, :, :], AX.X, ALU.max).then_inc(max_steps, 1)
                dve.wait_ge(max_steps, 2 * n + 1)
                dve.tensor_scalar(neg_scaled[:, s, :], neg_max[:, s, :], -scale, None, ALU.mult).then_inc(max_steps, 1)

            def turned_lo(n, s):
                dve.wait_ge(et_hi, n + 1)
                dve.tensor_tensor(et_pair[:, s, LO, :, :], ps_e[:, s, :, :], et_pair[:, s, HI, :, :],
                                  ALU.subtract).then_inc(et_split, 1)

            def inverse(n, s):
                dve.wait_ge(exp_steps, 2 * n + 2)
                if not isinstance(n, int) or n >= 2:
                    dve.wait_ge(a_hi, n - 1)
                dve.tensor_scalar(sums_s[:, s, :], sums[:, s, :], WS, None, ALU.mult).then_inc(inv_steps, 1)
                dve.wait_ge(inv_steps, 2 * n + 1)
                dve.reciprocal(inv[:, s, :], sums_s[:, s, :]).then_inc(inv_steps, 1)

            def attended_lo(n, s):
                dve.wait_ge(a_hi, n + 1)
                for c in range(DC):
                    out = dve.scalar_tensor_tensor(attended_t[:, LO, c, bass.ds(n * TOK, TOK)], ps_a[:, s, c * TOK:(c + 1) * TOK],
                                                   inv[:, s, c:c + 1], attended_t[:, HI, c, bass.ds(n * TOK, TOK)],
                                                   ALU.mult, ALU.subtract)
                out.then_inc(a_split, 1)

            row_max0, row_max1 = images_of(row_max)
            inverse0, inverse1 = images_of(inverse)
            turned_lo0, turned_lo1 = images_of(turned_lo)
            attended_lo0, attended_lo1 = images_of(attended_lo)
            skewed(dve, PAIRS, (2, turned_lo0), (2, turned_lo1), (1, row_max0), (1, row_max1), (0, project_lo),
                   (2, attended_lo0), (2, attended_lo1), (1, inverse0), (1, inverse1))

        @block.tensor
        def _(pe):
            pe.wait_ge(prep_v, 3)
            pe.wait_ge(prep_g, 6)

            def project(p, s):
                if not (isinstance(p, int) and p == 0):
                    pe.wait_ge(qk_split, p)
                    pe.wait_ge(v_split, p)
                first = True
                for c in range(DC):
                    for a in (HI, LO):
                        x = normed_t[:, a, c, bass.ds(p * PT, PT)]
                        for b in ((HI, LO) if a == HI else (HI,)):
                            pe.matmul(ps_qk[0:PT, :], x, w_pair[:, b, c, 0:2 * D], start=first, stop=False)
                            for m in range(DC):
                                v = pe.matmul(ps_v[:, m * PT:(m + 1) * PT], w_pair[:, b, c, 2 * D + m * P:2 * D + (m + 1) * P], x,
                                              start=first and m == 0, stop=(c == DC - 1 and a == LO), skip_group_check=True)
                            first = False
                v.then_inc(projected_v, 1)
                pe.matmul(ps_qk[0:PT, :], ones[:, 0:PT], bias_rows[:, :], start=False, stop=True).then_inc(projected_qk, 1)

            def score(p, image, pair_slot):
                n, s = 2 * p + image, image
                if image == 0:
                    pe.wait_ge(qk_split, p + 1)
                if not isinstance(n, int) or n >= 2:
                    pe.wait_ge(exp_steps, 2 * n - 2)
                for m in range(DC):
                    mm = split_matmuls(pe, ps_s[:, s, m, :], lambda a, c: q_pair[:, pair_slot, a, image, m * P:(m + 1) * P],
                                       lambda b, c: k_pair[:, pair_slot, b, :], 1, first_start=(m == 0), check=False)
                mm.then_inc(scored, 1)

            def turn(n, s):
                pe.wait_ge(exp_steps, 2 * n + 2)
                if not isinstance(n, int) or n >= 2:
                    pe.wait_ge(et_split, n - 1)
                for c in range(DC):
                    for m in range(DC):
                        mm = pe.transpose(ps_e[:, s, c, m * P:(m + 1) * P], exps[:, s, m, c * P:(c + 1) * P], ident[:, :])
                mm.then_inc(turned, 1)

            def attend(p, image, pair_slot):
                n, s = 2 * p + image, image
                pe.wait_ge(et_split, n + 1)
                if image == 0:
                    pe.wait_ge(v_split, p + 1)
                if not isinstance(n, int) or n >= 2:
                    pe.wait_ge(a_split, n - 1)
                for m in range(DC):
                    mm = split_matmuls(pe, ps_a[:, s, m * TOK:(m + 1) * TOK],
                                       lambda a, c: et_pair[:, s, a, c, m * P:(m + 1) * P],
                                       lambda b, c: v_pair[:, pair_slot, b, c, image * TOK:(image + 1) * TOK], DC,
                                       first_start=(m == 0), check=False)
                mm.then_inc(attended, 1)

            def score0(p, s):
                score(p, 0, s)

            def score1(p, s):
                score(p, 1, s)

            def attend0(p, s):
                attend(p, 0, s)

            def attend1(p, s):
                attend(p, 1, s)

            turn0, turn1 = images_of(turn)
            skewed(pe, PAIRS, (0, project), (1, score0), (2, attend0), (2, attend1), (1, score1), (1, turn0), (1, turn1))


def project_and_route(nc, d, keep, ahead):
    residual, attended_t, x1 = keep["residual"], keep["chan_b"], keep["rows"]
    weights, places, bounds, queue = keep["weights"], keep["places"], keep["bounds"], keep["queue"]
    with ExitStack() as ctx:
        def sb(name, shape, dt=F32):
            return ctx.enter_context(nc.sbuf_tensor(name, shape, dt))

        def psum(name, shape, dt=F32):
            return ctx.enter_context(nc.psum_tensor(name, shape, dt))

        def sem(name):
            return ctx.enter_context(nc.semaphore(name))

        w_raw = sb("proj_w_raw", [P, DC, D])
        w_pair = sb("proj_w_pair", [P, 2, DC, D], F16)
        g_raw = sb("gate_w_raw", [P, DC, EXPERTS])
        g_pair = sb("gate_w_pair", [P, 2, DC, EXPERTS], F16)
        bias_raw = sb("proj_b_raw", [33, D])
        bias_hi = sb("proj_b_hi", [33, D], F16)
        bias_rows = sb("proj_bias_rows", [P, D], F16)
        ones = sb("ones_c", [P, P], F16)
        before = sb("before", [P, P], F16)
        ident = sb("ident_c", [P, P])
        eps = sb("eps_c", [P, 1])
        stats = sb("stats_c", [P, 2, 6])
        mean_var = sb("mean_var_c", [P, 2, 2])
        std = sb("std_c", [P, 2])
        rstd = sb("rstd_c", [P, 2])
        x1_tile = sb("x1_tile", [P, 2, D])
        xt_pair = sb("x1_t_pair", [P, 2, 2, DC, P], F16)
        logits = sb("logits", [P, 2, EXPERTS])
        best = sb("best", [P, 2, 8])
        best_at = sb("best_at", [P, 2, 8], mybir.dt.uint32)
        best_two = sb("best_two", [P, TOP, TILES])
        names_i = sb("expert_names_i", [P, EXPERTS], I32)
        names = sb("expert_names", [P, EXPERTS])
        limits_i = sb("tile_limits_i", [P, MOST_OF_ONE], I32)
        limits = sb("tile_limits", [P, MOST_OF_ONE])
        at_f = sb("best_at_f", [P, TOP, TILES])
        is_best = sb("is_best", [P, TOP, TILES, EXPERTS])
        chosen = sb("chosen", [P, TILES, EXPERTS], F16)
        diff = sb("logit_difference", [P, TILES])
        ratio = sb("exp_difference", [P, TILES])
        total = sb("exp_total", [P, TILES])
        over = sb("over_limit", [P, EXPERTS, MOST_OF_ONE])
        tiles_f = sb("tiles_of_expert", [P, EXPERTS])
        start_f = sb("first_tile_of_expert", [P, EXPERTS])
        place = sb("place", [P, TILES, EXPERTS])
        place_of = sb("place_of_choice", [P, TILES, EXPERTS])
        place_f = sb("place_f", [P, TOP, TILES])
        ps_p = psum("ps_proj", [P, 2, 512])
        ps_t = psum("ps_x1_t", [P, 2, 512])
        ps_g = psum("ps_gate", [P, 2, 512])
        ps_rank = psum("ps_rank", [P, 512])
        ps_r = ps_rank[:, 0:(TILES + 1) * EXPERTS].rearrange("p (t e) -> p t e", e=EXPERTS)

        loaded, prep_a, prep_v, prep_g = sem("c_loaded"), sem("c_prep_a"), sem("c_prep_v"), sem("c_prep_g")
        projected, std_made, rstd_made, x1_made = sem("c_projected"), sem("c_std"), sem("c_rstd"), sem("x1_made")
        x1_kept = sem("x1_kept")
        turned, t_hi, t_split, gated = sem("c_turned"), sem("c_t_hi"), sem("c_t_split"), sem("gated")
        h_made, h_summed, h_known = sem("c_h_made"), sem("c_h_summed"), sem("c_h_known")
        logits_made, best_found, best_named = sem("logits_made"), sem("best_found"), sem("best_named")
        values_kept, names_kept = sem("values_kept"), sem("names_kept")
        passed = keep["passed"]
        chain, ratio_made, ranked, scattered = sem("route_chain"), sem("ratio_made"), sem("ranked"), sem("scattered")
        CHOSEN = 4 + (N % P > 0)
        ROUTED = CHOSEN + 11 + EXPERTS + 3 * TOP
        block = ctx.enter_context(nc.Block())

        @block.sync
        def _(sp):
            sp.dma_start(w_raw[:, :, :], d["proj0_w"]).then_inc(loaded, 16)
            sp.dma_start(g_raw[:, :, :], d["gate_w"]).then_inc(loaded, 16)
            sp.dma_start(bias_raw[0:1, :], d["proj0_b"]).then_inc(loaded, 16)
            sp.dma_start(bias_raw[32:33, :], d["proj0_b"]).then_inc(loaded, 16)
            ahead.sync(sp)

        @block.gpsimd
        def _(pool):
            pool.memset(ident[:, :], 0.0).then_inc(prep_g, 1)
            pool.memset(before[:, :], 1.0).then_inc(prep_g, 1)
            pool.wait_ge(prep_g, 2)
            pool.affine_select(out=ident[:, :], in_=ident[:, :], compare_op=ALU.not_equal, fill=1.0,
                               base=0, pattern=[[-1, P]], channel_multiplier=1).then_inc(prep_g, 1)
            pool.affine_select(out=before[:, :], in_=before[:, :], compare_op=ALU.is_ge, fill=0.0,
                               base=-1, pattern=[[1, P]], channel_multiplier=-1).then_inc(prep_g, 1)
            pool.memset(eps[:, :], EPS).then_inc(prep_g, 1)
            pool.memset(ones[:, :], 1.0).then_inc(prep_g, 1)
            pool.iota(names_i[:, :], [[1, EXPERTS]], base=0, channel_multiplier=0).then_inc(prep_g, 1)
            pool.iota(limits_i[:, :], [[ROWS, MOST_OF_ONE]], base=0, channel_multiplier=0).then_inc(prep_g, 1)
            pool.wait_ge(prep_g, 8)
            pool.tensor_copy(names[:, :], names_i[:, :]).then_inc(prep_g, 1)
            pool.tensor_copy(limits[:, :], limits_i[:, :]).then_inc(prep_g, 1)

            def keep_x1(t, s):
                pool.wait_ge(x1_made, t + 1)
                pool.tensor_copy(x1[:, bass.ds(t, 1), :], x1_tile[:, s:s + 1, :]).then_inc(x1_kept, 1)

            in_loop(pool, 0, TILES, keep_x1)
            ahead.gpsimd(pool)
            pool.wait_ge(chain, ROUTED)
            pool.wait_ge(x1_kept, TILES)
            for k in range(TOP):
                for t in range(TILES):
                    rows = min(P, N - t * P)
                    pool.indirect_dma_start(queue[:, :], bass.IndirectOffsetOnAxis(places[0:rows, k, t:t + 1], 0),
                                            x1[0:rows, t, :], None).then_inc(scattered, 16)
            pool.wait_ge(scattered, 16 * TOP * TILES)

        @block.scalar
        def _(act):
            act.wait_ge(loaded, 64)
            act.activation(w_pair[:, HI, :, :], w_raw[:, :, :], ACT.Copy, scale=WS).then_inc(prep_a, 1)
            act.activation(g_pair[:, HI, :, :], g_raw[:, :, :], ACT.Copy, scale=WS).then_inc(prep_a, 1)
            act.wait_ge(prep_v, 2)
            act.activation(bias_rows[0:1, :], bias_raw[0:1, :], ACT.Copy, scale=WS).then_inc(prep_a, 1)
            act.activation(bias_hi[32:33, :], bias_raw[32:33, :], ACT.Copy, scale=WS).then_inc(prep_a, 1)
            act.wait_ge(prep_g, 10)

            def root(t, s):
                act.wait_ge(h_known, t + 1)
                act.activation(std[:, s:s + 1], mean_var[:, s, 1:2], ACT.Sqrt, bias=eps[:, 0:1]).then_inc(std_made, 1)

            def t_hi_(t, s):
                act.wait_ge(turned, t + 1)
                act.wait_ge(gated, free(t))
                act.activation(xt_pair[:, s, HI, :, :], ps_t[:, s, 0:D].rearrange("p (c t) -> p c t", c=DC), ACT.Copy).then_inc(t_hi, 1)

            skewed(act, TILES, (4, t_hi_), (1, root))
            act.wait_ge(chain, 1)
            act.activation(ratio[:, :], diff[:, :], ACT.Exp).then_inc(ratio_made, 1)
            ahead.scalar(act)

        @block.vector
        def _(dve):
            dve.memset(bias_rows[:, :], 0.0).then_inc(prep_v, 1)
            dve.memset(attended_t[:, :, :, N:NPAD], 0.0).then_inc(prep_v, 1)
            dve.wait_ge(prep_a, 4)
            dve.wait_ge(prep_v, 2)

            def flat(ap):
                return ap.rearrange("p c n -> p (c n)")

            dve.scalar_tensor_tensor(flat(w_pair[:, LO, :, :]), flat(w_raw[:, :, :]), WS, flat(w_pair[:, HI, :, :]),
                                     ALU.mult, ALU.subtract).then_inc(prep_v, 1)
            dve.scalar_tensor_tensor(flat(g_pair[:, LO, :, :]), flat(g_raw[:, :, :]), WS, flat(g_pair[:, HI, :, :]),
                                     ALU.mult, ALU.subtract).then_inc(prep_v, 1)
            dve.scalar_tensor_tensor(bias_rows[32:33, :], bias_raw[32:33, :], WS, bias_hi[32:33, :],
                                     ALU.mult, ALU.subtract).then_inc(prep_v, 1)
            dve.wait_ge(prep_g, 10)

            def make_h(t, s):
                dve.wait_ge(projected, made(t))
                h = residual[:, bass.ds(t, 1), :]
                dve.scalar_tensor_tensor(h, ps_p[:, s:s + 1, 0:D], 1.0 / WS, h, ALU.mult, ALU.add).then_inc(h_made, 1)

            def h_stats(t, s):
                wait_apart(dve, h_made, t + 1, passed)
                dve.bn_stats(stats[:, s, :], residual[:, bass.ds(t, 1), :]).then_inc(h_summed, 1)

            def h_mean_var(t, s):
                if later(t):
                    dve.wait_ge(x1_made, t - 1)
                wait_apart(dve, h_summed, t + 1, passed)
                dve.bn_aggr(mean_var[:, s, :], stats[:, s, :]).then_inc(h_known, 1)

            def invert(t, s):
                dve.wait_ge(std_made, t + 1)
                dve.reciprocal(rstd[:, s:s + 1], std[:, s:s + 1]).then_inc(rstd_made, 1)

            def norm(t, s):
                dve.wait_ge(rstd_made, t + 1)
                if later(t):
                    dve.wait_ge(turned, t - 1)
                    dve.wait_ge(x1_kept, t - 1)
                dve.tensor_scalar(x1_tile[:, s:s + 1, :], residual[:, bass.ds(t, 1), :], mean_var[:, s, 0:1], rstd[:, s:s + 1],
                                  ALU.subtract, ALU.mult).then_inc(x1_made, 1)

            def t_lo(t, s):
                dve.wait_ge(t_hi, t + 1)
                dve.tensor_tensor(xt_pair[:, s, LO, :, :], ps_t[:, s, 0:D].rearrange("p (c t) -> p c t", c=DC),
                                  xt_pair[:, s, HI, :, :], ALU.subtract).then_inc(t_split, 1)

            def logits_of(t, s):
                dve.wait_ge(gated, made(t))
                if later(t):
                    dve.wait_ge(best_found, t - 1)
                    dve.wait_ge(best_named, t - 1)
                dve.tensor_scalar(logits[:, s, :], ps_g[:, s, 0:EXPERTS], 1.0 / WS, None, ALU.mult).then_inc(logits_made, 1)

            def find_best(t, s):
                if later(t):
                    dve.wait_ge(values_kept, t - 1)
                wait_apart(dve, logits_made, t + 1, passed)
                dve.max(best[:, s, :], logits[:, s, :]).then_inc(best_found, 1)

            def name_best(t, s):
                if later(t):
                    dve.wait_ge(names_kept, t - 1)
                wait_apart(dve, best_found, t + 1, passed)
                dve.max_index(best_at[:, s, :], best[:, s, :], logits[:, s, :]).then_inc(best_named, 1)

            def keep_values(t, s):
                dve.wait_ge(best_named, t + 1)
                dve.tensor_copy(best_two[:, :, bass.ds(t, 1)], best[:, s, 0:TOP, None]).then_inc(values_kept, 1)

            def keep_names(t, s):
                dve.wait_ge(best_named, t + 1)
                dve.tensor_copy(at_f[:, :, bass.ds(t, 1)], best_at[:, s, 0:TOP, None]).then_inc(names_kept, 1)

            skewed(dve, TILES, (0, make_h), (2, invert), (7, keep_names), (6, logits_of), (0, h_stats), (7, keep_values),
                   (2, norm), (6, find_best), (4, t_lo), (0, h_mean_var), (6, name_best))

            steps = [0]

            def then(ins):
                steps[0] += 1
                ins.then_inc(chain, 1)
                dve.wait_ge(chain, steps[0])

            def wide(ap):
                return ap[:, :, None].to_broadcast([P, TILES, EXPERTS])

            dve.wait_ge(values_kept, TILES)
            dve.wait_ge(names_kept, TILES)
            then(dve.tensor_tensor(diff[:, :], best_two[:, 1, :], best_two[:, 0, :], ALU.subtract))
            for k in range(TOP):
                then(dve.tensor_tensor(is_best[:, k, :, :], wide(at_f[:, k, :]),
                                       names[:, None, :].to_broadcast([P, TILES, EXPERTS]), ALU.is_equal))
            then(dve.tensor_tensor(chosen[:, :, :], is_best[:, 0, :, :], is_best[:, 1, :, :], ALU.add))
            if N % P:
                then(dve.memset(chosen[N % P:P, TILES - 1, :], 0.0))
            assert steps[0] == CHOSEN
            dve.wait_ge(ratio_made, 1)
            then(dve.tensor_scalar(total[:, :], ratio[:, :], 1.0, None, ALU.add))
            then(dve.reciprocal(weights[:, 0, :], total[:, :]))
            then(dve.tensor_tensor(weights[:, 1, :], weights[:, 0, :], ratio[:, :], ALU.mult))
            dve.wait_ge(ranked, 1)
            counts = ps_r[:, TILES, :]
            then(dve.tensor_copy(start_f[:, :], counts))
            then(dve.tensor_tensor(over[:, :, :], start_f[:, :, None].to_broadcast([P, EXPERTS, MOST_OF_ONE]),
                                   limits[:, None, :].to_broadcast([P, EXPERTS, MOST_OF_ONE]), ALU.is_gt))
            then(dve.tensor_reduce(tiles_f[:, :], over[:, :, :], AX.X, ALU.add))
            then(dve.tensor_scalar(tiles_f[:, :], tiles_f[:, :], float(LEAST_TILES), None, ALU.max))
            then(dve.memset(start_f[:, 0:1], 0.0))
            for e in range(1, EXPERTS):
                then(dve.tensor_tensor(start_f[:, e:e + 1], start_f[:, e - 1:e], tiles_f[:, e - 1:e], ALU.add))
            then(dve.tensor_copy(bounds[:, 0, :], start_f[:, :]))
            then(dve.tensor_copy(bounds[:, 1, :], tiles_f[:, :]))
            then(dve.tensor_scalar(start_f[:, :], start_f[:, :], float(ROWS), None, ALU.mult))
            then(dve.tensor_tensor(place[:, :, :], ps_r[:, 0:TILES, :], start_f[:, None, :].to_broadcast([P, TILES, EXPERTS]), ALU.add))
            for k in range(TOP):
                then(dve.tensor_tensor(place_of[:, :, :], place[:, :, :], is_best[:, k, :, :], ALU.mult))
                then(dve.tensor_reduce(place_f[:, k, :], place_of[:, :, :], AX.X, ALU.add))
                then(dve.tensor_copy(places[:, k, :], place_f[:, k, :]))
            assert steps[0] == ROUTED, steps[0]
            ahead.vector(dve)

        @block.tensor
        def _(pe):
            pe.sem_inc(projected, SLOTS)
            pe.sem_inc(gated, SLOTS)
            pe.wait_ge(prep_v, 5)
            pe.wait_ge(prep_g, 10)

            def project(t, s):
                if not isinstance(t, int) or t >= 2:
                    pe.wait_ge(h_made, t - 1)
                split = [(c, a) for c in range(DC) for a in (HI, LO)]
                for n, (c, a) in enumerate(split):
                    x = attended_t[:, a, c, bass.ds(t * P, P)]
                    for b in ((HI, LO) if a == HI else (HI,)):
                        pe.matmul(ps_p[:, s, 0:D], x, w_pair[:, b, c, :], start=(n == 0 and b == HI), stop=False)
                pe.matmul(ps_p[:, s, 0:D], ones[:, :], bias_rows[:, :], start=False, stop=True).then_inc(projected, 1)

            def turn(t, s):
                pe.wait_ge(x1_made, t + 1)
                if not isinstance(t, int) or t >= 2:
                    pe.wait_ge(t_split, t - 1)
                for c in range(DC):
                    mm = pe.transpose(ps_t[:, s, c * P:(c + 1) * P], x1_tile[:, s, c * P:(c + 1) * P], ident[:, :])
                mm.then_inc(turned, 1)

            def gate(t, s):
                pe.wait_ge(t_split, t + 1)
                if not isinstance(t, int) or t >= 2:
                    pe.wait_ge(logits_made, t - 1)
                split_matmuls(pe, ps_g[:, s, 0:EXPERTS], lambda a, c: xt_pair[:, s, a, c, :],
                              lambda b, c: g_pair[:, b, c, :], DC).then_inc(gated, 1)

            skewed(pe, TILES, (0, project), (4, turn), (5, gate))
            pe.wait_ge(chain, CHOSEN)
            pe.matmul(ps_r[:, 0:TILES, :], before[:, :], chosen[:, :, :], start=True, stop=False, skip_group_check=True)
            for t in range(TILES):
                mm = pe.matmul(ps_r[:, t + 1:TILES + 1, :], ones[:, :],
                               chosen[:, t:t + 1, :].to_broadcast([P, TILES - t, EXPERTS]),
                               start=False, stop=(t == TILES - 1), skip_group_check=True)
            mm.then_inc(ranked, 1)


WIDE = DC * HIDDEN
PAIRED = MC // 2
PART = 2 * WIDE // PAIRED


def expert_constants(nc, ctx, d):
    def sb(name, shape, dt=F32):
        return ctx.enter_context(nc.sbuf_tensor(name, shape, dt))

    def sem(name):
        return ctx.enter_context(nc.semaphore(name))

    c = Prepared()
    w_raw = sb("expert_w_raw", [P, 2, WIDE])
    out_b_raw = sb("out_b_raw", [33, EXPERTS * D])
    out_b_hi = sb("out_b_hi", [33, EXPERTS * D], F16)
    c.w_pair = sb("expert_w_pair", [P, 2, 2, 2, WIDE], F16)
    c.in_b = sb("in_b", [P, EXPERTS, MC])
    c.out_b_rows = sb("out_b_rows", [P, EXPERTS, D], F16)
    c.ones = sb("ones_d", [P, P], F16)
    c.ident = sb("ident_d", [P, P])
    loaded, prep = sem("e_loaded"), sem("e_prep")
    w_loaded, w_hi, c.w_split = sem("expert_w_loaded"), sem("expert_w_hi"), sem("expert_w_split")

    def part(s, half, k):
        return c.w_pair[:, s, half, :, :].rearrange("p a n -> p (a n)")[:, k * PART:(k + 1) * PART]

    def raw_part(k):
        return w_raw[:, :, :].rearrange("p a n -> p (a n)")[:, k * PART:(k + 1) * PART]

    def load_weights(sp, e):
        if not isinstance(e, int) or e >= 1:
            sp.wait_ge(c.w_split, PAIRED * e)
        for which, w in enumerate(("in_w", "out_w")):
            sp.dma_start(w_raw[:, which:which + 1, :].rearrange("p a n -> p (a n)"),
                         d[w][bass.ds(e, 1)].rearrange("a p c n -> (a p) (c n)")).then_inc(w_loaded, 16)

    def part_hi(act, e, s, k):
        act.wait_ge(w_loaded, 32 * e + 32)
        act.activation(part(s, HI, k), raw_part(k), ACT.Copy, scale=WS).then_inc(w_hi, 1)

    def part_lo(dve, e, s, k):
        dve.wait_ge(w_hi, PAIRED * e + k + 1)
        dve.scalar_tensor_tensor(part(s, LO, k), raw_part(k), WS, part(s, HI, k), ALU.mult, ALU.subtract).then_inc(c.w_split, 1)

    def sync(sp):
        sp.dma_start(c.in_b[:, :, :], d["in_b"]).then_inc(loaded, 16)
        sp.dma_start(out_b_raw[0:1, :], d["out_b"]).then_inc(loaded, 16)
        sp.dma_start(out_b_raw[32:33, :], d["out_b"]).then_inc(loaded, 16)
        load_weights(sp, 0)

    def gpsimd(pool):
        pool.memset(c.ident[:, :], 0.0).then_inc(prep, 1)
        pool.wait_ge(prep, 1)
        pool.affine_select(out=c.ident[:, :], in_=c.ident[:, :], compare_op=ALU.not_equal, fill=1.0,
                           base=0, pattern=[[-1, P]], channel_multiplier=1)
        pool.memset(c.ones[:, :], 1.0)
        pool.memset(c.out_b_rows[:, :, :], 0.0).then_inc(prep, 1)

    def scalar(act):
        act.wait_ge(loaded, 48)
        act.wait_ge(prep, 2)
        act.activation(c.out_b_rows[0:1, :, :].rearrange("p e n -> p (e n)"), out_b_raw[0:1, :], ACT.Copy, scale=WS)
        act.activation(out_b_hi[32:33, :], out_b_raw[32:33, :], ACT.Copy, scale=WS).then_inc(prep, 1)
        for k in range(PAIRED):
            part_hi(act, 0, 0, k)

    def vector(dve):
        dve.wait_ge(prep, 3)
        dve.scalar_tensor_tensor(c.out_b_rows[32:33, :, :].rearrange("p e n -> p (e n)"), out_b_raw[32:33, :], WS, out_b_hi[32:33, :],
                                 ALU.mult, ALU.subtract)
        for k in range(PAIRED):
            part_lo(dve, 0, 0, k)

    c.load_weights, c.part_hi, c.part_lo = load_weights, part_hi, part_lo
    c.sync, c.gpsimd, c.scalar, c.vector = sync, gpsimd, scalar, vector
    return c


def experts(nc, d, keep, c0):
    bounds, queue, answers = keep["bounds"], keep["queue"], keep["answers"]
    with ExitStack() as ctx:
        def sb(name, shape, dt=F32):
            return ctx.enter_context(nc.sbuf_tensor(name, shape, dt))

        def psum(name, shape, dt=F32):
            return ctx.enter_context(nc.psum_tensor(name, shape, dt))

        def sem(name):
            return ctx.enter_context(nc.semaphore(name))

        w_pair, in_b, out_b_rows, ones, ident = c0.w_pair, c0.in_b, c0.out_b_rows, c0.ones, c0.ident
        w_split, load_weights, part_hi, part_lo = c0.w_split, c0.load_weights, c0.part_hi, c0.part_lo
        x_tile = sb("x_tile", [P, 2, D])
        xt_pair = sb("x_t_pair", [P, 2, DC, ROWS], F16)
        hidden = sb("hidden", [P, 2, 2, ROWS])
        hidden_pair = sb("hidden_pair", [P, 2, MC, ROWS], F16)
        y_tile = sb("y_tile", [P, 2, D])
        ps_t = psum("ps_x_t", [P, DC, ROWS])
        ps_h = psum("ps_hidden", [P, PAIRED, 2, ROWS])
        ps_y = psum("ps_y", [P, 2, D])

        x_loaded, turned, x_hi, x_split = sem("x_loaded"), sem("e_turned"), sem("x_hi"), sem("x_split")
        hidden_summed, gelu_made, hidden_hi, hidden_split = sem("hidden_summed"), sem("gelu_made"), sem("hidden_hi"), sem("hidden_split")
        hidden_used, y_made, y_stored, passed = sem("hidden_used"), sem("y_made"), sem("y_stored"), keep["passed"]
        queue_tiles = queue.rearrange("(g h p) n -> g p h n", h=2, p=P)
        answer_tiles = answers.rearrange("(g h p) n -> g p h n", h=2, p=P)
        block = ctx.enter_context(nc.Block())

        def start_of(eng, e):
            return eng.value_load(bounds[0:1, 0, bass.ds(e, 1)], min_val=0, max_val=EXPERT_TILES - 1)

        def tiles_of(eng, e):
            return eng.value_load(bounds[0:1, 1, bass.ds(e, 1)], min_val=LEAST_TILES, max_val=MOST_OF_ONE)

        def all_tiles(eng, tile):
            def expert(e, s):
                start, count = start_of(eng, e), tiles_of(eng, e)
                tile(start, e, s, not (isinstance(e, int) and e == EXPERTS - 1))
                with eng.Fori(1, count) as i:
                    g = eng.snap(start + i, min_val=0, max_val=EXPERT_TILES - 1)
                    tile(g, e, s, False)

            return expert

        def all_experts(eng, expert):
            in_loop(eng, 0, EXPERTS - 1, expert)
            expert(EXPERTS - 1, (EXPERTS - 1) % 2)

        @block.sync
        def _(sp):
            def load_x(g):
                sp.dma_start(x_tile[:, :, :], queue_tiles[bass.ds(g, 1)].rearrange("a p h n -> (a p) h n")).then_inc(x_loaded, 16)

            load_x(0)
            load_weights(sp, 1)

            def tile(g, e, s, ahead):
                sp.wait_ge(turned, g + 1)
                load_x(g + 1)
                if ahead and not (isinstance(e, int) and e + 2 >= EXPERTS):
                    load_weights(sp, e + 2)
                sp.wait_ge(y_made, g + 2)
                sp.dma_start(answer_tiles[bass.ds(g, 1)].rearrange("a p h n -> (a p) h n"), y_tile[:, :, :]).then_inc(y_stored, 16)

            expert = all_tiles(sp, tile)
            in_loop(sp, 0, EXPERTS - 2, expert)
            expert(EXPERTS - 2, 0)
            expert(EXPERTS - 1, 1)
            wait_apart(sp, y_stored, 16 * (start_of(sp, EXPERTS - 1) + tiles_of(sp, EXPERTS - 1)) + 16, passed)

        @block.scalar
        def _(act):
            act.sem_inc(gelu_made, PAIRED)
            act.sem_inc(y_made, 1)
            act.sem_inc(y_stored, 16)
            def x_hi_(g):
                act.wait_ge(turned, g + 1)
                act.activation(xt_pair[:, HI, :, :], ps_t[:, :, :], ACT.Copy).then_inc(x_hi, 1)

            x_hi_(0)

            def tile(g, e, s, ahead):
                for q in range(PAIRED):
                    act.wait_ge(hidden_split, PAIRED * g + q + 1)
                    wait_apart(act, hidden_summed, PAIRED * g + q + 1, passed)
                    for m in range(2):
                        out = act.activation(hidden[:, q % 2, m, :], ps_h[:, q, m, :], ACT.Gelu, scale=1.0 / WS,
                                             bias=in_b[:, bass.ds(e, 1), 2 * q + m:2 * q + m + 1].rearrange("p a b -> p (a b)"))
                    out.then_inc(gelu_made, 1)
                    if ahead:
                        part_hi(act, e + 1, 1 - s, q)
                x_hi_(g + 1)
                act.wait_ge(hidden_used, PAIRED * (g + 1) + PAIRED)
                act.wait_ge(y_stored, 16 * g + 16)
                act.activation(y_tile[:, :, :], ps_y[:, :, :], ACT.Copy, scale=1.0 / WS).then_inc(y_made, 1)

            all_experts(act, all_tiles(act, tile))

        @block.vector
        def _(dve):
            dve.sem_inc(hidden_split, SLOTS)
            def x_lo(g):
                dve.wait_ge(x_hi, g + 1)
                dve.tensor_tensor(xt_pair[:, LO, :, :], ps_t[:, :, :], xt_pair[:, HI, :, :], ALU.subtract).then_inc(x_split, 1)

            x_lo(0)

            def tile(g, e, s, ahead):
                for q in range(PAIRED):
                    dve.wait_ge(gelu_made, PAIRED * g + q + 1 + PAIRED)
                    dve.wait_ge(hidden_used, PAIRED * g + q + 1)
                    dve.tensor_copy(hidden_pair[:, HI, 2 * q:2 * q + 2, :], hidden[:, q % 2, :, :]).then_inc(hidden_hi, 1)
                    dve.wait_ge(hidden_hi, PAIRED * g + q + 1)
                    dve.tensor_tensor(hidden_pair[:, LO, 2 * q:2 * q + 2, :], hidden[:, q % 2, :, :], hidden_pair[:, HI, 2 * q:2 * q + 2, :],
                                      ALU.subtract).then_inc(hidden_split, 1)
                    if ahead:
                        part_lo(dve, e + 1, 1 - s, q)
                x_lo(g + 1)

            all_experts(dve, all_tiles(dve, tile))

        @block.tensor
        def _(pe):
            pe.sem_inc(hidden_used, PAIRED)

            def turn(g):
                pe.wait_ge(x_loaded, 16 * g + 16)
                if not isinstance(g, int) or g >= 1:
                    pe.wait_ge(x_split, g)
                for c in range(DC):
                    for h in range(2):
                        mm = pe.transpose(ps_t[:, c, h * P:(h + 1) * P], x_tile[:, h, c * P:(c + 1) * P], ident[:, :])
                mm.then_inc(turned, 1)

            turn(0)

            def tile(g, e, s, ahead):
                w_in = w_pair[:, s, :, 0, :].rearrange("p a (c m) -> p a c m", c=DC)
                w_out = w_pair[:, s, :, 1, :].rearrange("p a (m c) -> p a m c", m=MC)

                def first_layer(q):
                    pe.wait_ge(gelu_made, PAIRED * g + q + 1)
                    for m in range(2):
                        mm = split_matmuls(pe, ps_h[:, q, m, :], lambda a, c: w_in[:, a, c, (2 * q + m) * P:(2 * q + m + 1) * P],
                                           lambda b, c: xt_pair[:, b, c, :], DC, first_start=(m == 0), check=False)
                    mm.then_inc(hidden_summed, 1)

                def second_layer(q):
                    pe.wait_ge(hidden_split, PAIRED * g + q + 1 + SLOTS)
                    if q == 0:
                        pe.wait_ge(y_made, g + 1)
                    for h in range(2):
                        if q == 0:
                            pe.matmul(ps_y[:, h, :], ones[:, :], out_b_rows[:, bass.ds(e, 1), :], start=(h == 0), stop=False, skip_group_check=True)
                        for m in (2 * q, 2 * q + 1):
                            for a, b in ((HI, HI), (HI, LO), (LO, HI)):
                                mm = pe.matmul(ps_y[:, h, :], hidden_pair[:, a, m, h * P:(h + 1) * P], w_out[:, b, m, :],
                                               start=False, stop=(m == MC - 1 and a == LO), skip_group_check=True)
                    mm.then_inc(hidden_used, 1)

                pe.wait_ge(x_split, g + 1)
                first_layer(0)
                first_layer(1)
                first_layer(2)
                second_layer(0)
                first_layer(3)
                turn(g + 1)
                second_layer(1)
                second_layer(2)
                second_layer(3)

            body = all_tiles(pe, tile)

            def expert(e, s):
                pe.wait_ge(w_split, PAIRED * e + PAIRED)
                body(e, s)

            all_experts(pe, expert)


def gather_and_norm(nc, d, keep, ahead):
    residual, weights, places, answers = keep["residual"], keep["weights"], keep["places"], keep["answers"]
    state, pair = keep["state"], keep["chan_a"]
    with ExitStack() as ctx:
        def sb(name, shape, dt=F32):
            return ctx.enter_context(nc.sbuf_tensor(name, shape, dt))

        def sem(name):
            return ctx.enter_context(nc.semaphore(name))

        ident = sb("ident_f", [P, P])
        eps = sb("eps_f", [P, 1])
        rows_of = sb("answer_rows", [P, 2, TOP, D])
        stats = sb("stats_f", [P, 2, 6])
        mean_var = sb("mean_var_f", [P, 2, 2])
        std = sb("std_f", [P, 2])
        rstd = sb("rstd_f", [P, 2])
        x2 = sb("x2_tile", [P, 2, D])
        ps_t = ctx.enter_context(nc.psum_tensor("ps_x2_t", [P, 2, 512], F32))

        prep_g, passed = sem("f_prep_g"), keep["passed"]
        gathered = [sem("gathered0"), sem("gathered1")]
        h_steps, std_made, rstd_made, x2_made = sem("f_h_steps"), sem("f_std"), sem("f_rstd"), sem("x2_made")
        turned, state_made, t_hi, t_split = sem("f_turned"), sem("state_made"), sem("f_t_hi"), sem("f_t_split")
        block = ctx.enter_context(nc.Block())

        @block.sync
        def _(sp):
            ahead.sync(sp)

        @block.gpsimd
        def _(pool):
            pool.memset(ident[:, :], 0.0).then_inc(prep_g, 1)
            pool.wait_ge(prep_g, 1)
            pool.affine_select(out=ident[:, :], in_=ident[:, :], compare_op=ALU.not_equal, fill=1.0,
                               base=0, pattern=[[-1, P]], channel_multiplier=1).then_inc(prep_g, 1)
            pool.memset(eps[:, :], EPS).then_inc(prep_g, 1)
            for t in range(TILES):
                rows = min(P, N - t * P)
                if t >= 2:
                    pool.wait_ge(h_steps, 4 * t - 6)
                for k in range(TOP):
                    pool.indirect_dma_start(rows_of[0:rows, t % 2, k, :], None, answers[0:EXPERT_TILES * ROWS, :],
                                            bass.IndirectOffsetOnAxis(places[0:rows, k, t:t + 1], 0)).then_inc(gathered[t % 2], 16)
            ahead.gpsimd(pool)

        @block.scalar
        def _(act):
            act.wait_ge(prep_g, 3)

            def root(t, s):
                act.wait_ge(h_steps, 4 * t + 4)
                act.activation(std[:, s:s + 1], mean_var[:, s, 1:2], ACT.Sqrt, bias=eps[:, 0:1]).then_inc(std_made, 1)

            def out_hi(t, s):
                act.wait_ge(turned, t + 1)
                turned_rows = ps_t[:, s, 0:D].rearrange("p (c t) -> p c t", c=DC)
                act.activation(state[:, :, bass.ds(t * P, P)], turned_rows, ACT.Copy).then_inc(state_made, 1)
                act.activation(pair[:, HI, :, bass.ds(t * P, P)], turned_rows, ACT.Copy).then_inc(t_hi, 1)

            skewed(act, TILES, (3, out_hi), (0, root))
            ahead.scalar(act)

        @block.vector
        def _(dve):
            def add_answers(t, s):
                rows = P if not isinstance(t, int) else min(P, N - t * P)
                dve.wait_ge(gathered[s], 16 * t + 32 - 16 * s)
                h = residual[0:rows, bass.ds(t, 1), :]
                for k in range(TOP):
                    dve.scalar_tensor_tensor(h, rows_of[0:rows, s, k:k + 1, :], weights[0:rows, k, bass.ds(t, 1)], h,
                                             ALU.mult, ALU.add).then_inc(h_steps, 1)
                    wait_apart(dve, h_steps, 4 * t + k + 1, passed)
                dve.bn_stats(stats[:, s, :], residual[:, bass.ds(t, 1), :]).then_inc(h_steps, 1)
                wait_apart(dve, h_steps, 4 * t + 3, passed)
                dve.bn_aggr(mean_var[:, s, :], stats[:, s, :]).then_inc(h_steps, 1)

            def norm(t, s):
                dve.wait_ge(std_made, t + 1)
                dve.reciprocal(rstd[:, s:s + 1], std[:, s:s + 1]).then_inc(rstd_made, 1)
                dve.wait_ge(rstd_made, t + 1)
                if not isinstance(t, int) or t >= 2:
                    dve.wait_ge(turned, t - 1)
                dve.tensor_scalar(x2[:, s:s + 1, :], residual[:, bass.ds(t, 1), :], mean_var[:, s, 0:1], rstd[:, s:s + 1],
                                  ALU.subtract, ALU.mult).then_inc(x2_made, 1)

            def out_lo(t, s):
                dve.wait_ge(t_hi, t + 1)
                dve.tensor_tensor(pair[:, LO, :, bass.ds(t * P, P)], ps_t[:, s, 0:D].rearrange("p (c t) -> p c t", c=DC),
                                  pair[:, HI, :, bass.ds(t * P, P)], ALU.subtract).then_inc(t_split, 1)

            skewed(dve, TILES, (0, add_answers), (1, norm), (3, out_lo))
            ahead.vector(dve)

        @block.tensor
        def _(pe):
            pe.wait_ge(prep_g, 2)

            def turn(t, s):
                pe.wait_ge(x2_made, t + 1)
                if not isinstance(t, int) or t >= 2:
                    pe.wait_ge(t_split, t - 1)
                for c in range(DC):
                    mm = pe.transpose(ps_t[:, s, c * P:(c + 1) * P], x2[:, s, c * P:(c + 1) * P], ident[:, :])
                mm.then_inc(turned, 1)

            skewed(pe, TILES, (4, turn))


LAYERS, HEADS = 12, 16
HD = D // HEADS
CHUNKS = 8
CT = N // CHUNKS
CP = PAIRS // CHUNKS
PIECES = CHUNKS
PIECE = (4 * D * DC) // PIECES


def layer_constants(nc, ctx, d, keep):
    def sb(name, shape, dt=F32):
        return ctx.enter_context(nc.sbuf_tensor(name, shape, dt))

    bias_sum = keep["bias_sum"]
    q_b_raw = sb("q_b_raw", [P, LAYERS, DC])
    proj_b = sb("proj_b", [P, LAYERS, DC])
    kv_b_hi = sb("kv_b_hi", [33, 2 * D], F16)
    c = Prepared()
    c.w_raw = sb("layer_w_raw", [P, PIECES, PIECE])
    c.w_pair = sb("layer_w_pair", [P, 2, 2, PIECES * PIECE], F16)
    c.kv_b_raw = sb("kv_b_raw", [33, 2 * D])
    c.kv_b_rows = sb("kv_b_rows", [P, 2, 2 * D], F16)
    c.q_b = sb("q_b", [P, LAYERS, DC])
    c.ones = sb("ones_g", [P, P], F16)
    c.own = sb("own_image_g", [PT, 2])
    c.mask = sb("head_mask", [P, 2, DC, P])

    def sem(name):
        return ctx.enter_context(nc.semaphore(name))

    c.loaded, c.prep_g, c.prep_v = sem("g_loaded"), sem("g_prep_g"), sem("g_prep_v")
    c.w_loaded, c.w_hi, c.w_split = sem("g_w_loaded"), sem("g_w_hi"), sem("g_w_split")
    c.b_loaded, c.b_hi, c.b_split = sem("g_b_loaded"), sem("g_b_hi"), sem("g_b_split")

    def load(sp, l):
        if not isinstance(l, int) or l >= 1:
            sp.wait_ge(c.w_split, PIECES * l)
            sp.wait_ge(c.b_split, l)
        sp.dma_start(c.w_raw[:, 0:6, :].rearrange("p a n -> p (a n)"),
                     d["qkv1_w"][bass.ds(l, 1)].rearrange("a p c n -> (a p) (c n)")).then_inc(c.w_loaded, 16)
        sp.dma_start(c.w_raw[:, 6:8, :].rearrange("p a n -> p (a n)"),
                     d["proj1_w"][bass.ds(l, 1)].rearrange("a p c n -> (a p) (c n)")).then_inc(c.w_loaded, 16)
        for row in (0, 32):
            sp.dma_start(c.kv_b_raw[row:row + 1, :], d["qkv1_b"][bass.ds(l, 1), D:3 * D]).then_inc(c.b_loaded, 16)

    def w_pieces(s, half, n):
        return c.w_pair[:, s, half, :].rearrange("p (a n) -> p a n", n=PIECE)[:, bass.ds(n, 1), :]

    def piece_hi(act, s, n):
        act.activation(w_pieces(s, HI, n), c.w_raw[:, bass.ds(n, 1), :], ACT.Copy, scale=WS).then_inc(c.w_hi, 1)

    def biases_hi(act, l, s):
        act.wait_ge(c.b_loaded, 32 * l + 32)
        act.activation(c.kv_b_rows[0:1, s, :], c.kv_b_raw[0:1, :], ACT.Copy, scale=WS)
        act.activation(kv_b_hi[32:33, :], c.kv_b_raw[32:33, :], ACT.Copy, scale=WS).then_inc(c.b_hi, 1)

    def piece_lo(dve, count, s, n):
        dve.wait_ge(c.w_hi, count)
        dve.scalar_tensor_tensor(w_pieces(s, LO, n), c.w_raw[:, bass.ds(n, 1), :], WS, w_pieces(s, HI, n),
                                 ALU.mult, ALU.subtract).then_inc(c.w_split, 1)

    def biases_lo(dve, l, s):
        dve.wait_ge(c.b_hi, l + 1)
        dve.scalar_tensor_tensor(c.kv_b_rows[32:33, s, :], c.kv_b_raw[32:33, :], WS, kv_b_hi[32:33, :],
                                 ALU.mult, ALU.subtract).then_inc(c.b_split, 1)

    c.load, c.piece_hi, c.biases_hi, c.piece_lo, c.biases_lo = load, piece_hi, biases_hi, piece_lo, biases_lo

    def sync(sp):
        load(sp, 0)
        sp.dma_start(q_b_raw[:, :, :], d["q1_bcol"]).then_inc(c.loaded, 16)
        sp.dma_start(proj_b[:, :, :], d["proj1_bcol"]).then_inc(c.loaded, 16)

    def gpsimd(pool):
        pool.memset(c.own[:, :], 1.0 / WS)
        pool.memset(c.ones[:, :], 1.0)
        pool.memset(c.mask[:, :, :, :], float(HD) ** -0.5).then_inc(c.prep_g, 1)
        pool.wait_ge(c.prep_g, 1)
        pool.affine_select(out=c.own[:, 0:1], in_=c.own[:, 0:1], compare_op=ALU.is_ge, fill=0.0,
                           base=TOK - 1, pattern=[[0, 1]], channel_multiplier=-1)
        pool.affine_select(out=c.own[:, 1:2], in_=c.own[:, 1:2], compare_op=ALU.is_ge, fill=0.0,
                           base=-TOK, pattern=[[0, 1]], channel_multiplier=1)
        for n, m in enumerate(c.mask[:, i, k, :].rearrange("p (h j) -> p h j", j=HD) for i in range(2) for k in range(DC)):
            pool.affine_select(out=m, in_=m, compare_op=ALU.is_ge, fill=0.0, base=0,
                               pattern=[[-HD, P // HD], [0, HD]], channel_multiplier=1).then_inc(c.prep_g, 1)
            pool.wait_ge(c.prep_g, n + 2)
            pool.affine_select(out=m, in_=m, compare_op=ALU.is_ge, fill=0.0, base=HD - 1,
                               pattern=[[HD, P // HD], [0, HD]], channel_multiplier=-1)

    def scalar(act):
        act.wait_ge(c.loaded, 32)
        act.activation(c.q_b[:, :, :], q_b_raw[:, :, :], ACT.Copy, scale=WS)
        act.wait_ge(c.prep_v, 1)
        act.wait_ge(c.w_loaded, 32)
        for n in range(PIECES):
            piece_hi(act, 0, n)
        biases_hi(act, 0, 0)

    def vector(dve):
        dve.memset(c.kv_b_rows[:, :, :], 0.0).then_inc(c.prep_v, 1)
        dve.memset(bias_sum[:, 0:1, :], 0.0).then_inc(c.prep_v, 1)
        dve.wait_ge(c.loaded, 32)
        for l in range(LAYERS):
            dve.wait_ge(c.prep_v, 2 + l)
            dve.tensor_tensor(bias_sum[:, l + 1, :], bias_sum[:, l, :], proj_b[:, l, :], ALU.add).then_inc(c.prep_v, 1)
        for n in range(PIECES):
            piece_lo(dve, n + 1, 0, n)
        biases_lo(dve, 0, 0)

    c.sync, c.gpsimd, c.scalar, c.vector = sync, gpsimd, scalar, vector
    return c


def linear_attention_layers(nc, d, keep, c0, ahead):
    state, pair, bias_sum = keep["state"], keep["chan_a"], keep["bias_sum"]
    with ExitStack() as ctx:
        def sb(name, shape, dt=F32):
            return ctx.enter_context(nc.sbuf_tensor(name, shape, dt))

        def psum(name, shape, dt=F32):
            return ctx.enter_context(nc.psum_tensor(name, shape, dt))

        def sem(name):
            return ctx.enter_context(nc.semaphore(name))

        w_pair, kv_b_rows, q_b, ones, own, mask = c0.w_pair, c0.kv_b_rows, c0.q_b, c0.ones, c0.own, c0.mask
        w_loaded, w_split, b_split = c0.w_loaded, c0.w_split, c0.b_split
        k_pair = sb("k_pair_g", [PT, CP, 2, D], F16)
        v_pair = sb("v_pair_g", [PT, CP, 2, 2, D], F16)
        q_pair = sb("q_pair_g", [P, 2, 2, DC, CT], F16)
        outer = sb("outer", [P, CP, 2, DC, P])
        outer_pair = sb("outer_pair", [P, CP, 2, 2, DC, P], F16)
        y_pair = sb("y_pair", [P, 2, DC, CT], F16)
        ps_kv = psum("ps_kv", [P, 2, 512])
        ps_o = psum("ps_outer", [P, 2, 2, DC, P])
        ps_y = psum("ps_y_g", [P, DC, 512])
        ps_x = psum("ps_q_or_x", [P, DC, 512])

        kv_summed, q_summed, outer_summed, applied, x_summed = sem("kv_summed"), sem("q_summed"), sem("outer_summed"), sem("applied"), sem("x_summed")
        kv_hi, q_hi, outer_hi, y_hi, x_hi = sem("kv_hi"), sem("q_hi"), sem("outer_hi"), sem("y_hi"), sem("g_x_hi")
        kv_split, q_split, outer_masked, outer_split = sem("kv_split"), sem("q_split"), sem("outer_masked"), sem("outer_split")
        y_split, x_made, x_split, passed = sem("y_split"), sem("g_x_made"), sem("g_x_split"), keep["passed"]
        block = ctx.enter_context(nc.Block())

        def all_steps(eng, step):
            def layer(l, s):
                for c in (0, 1):
                    step(CHUNKS * l + c, l, s, c, c)
                in_loop(eng, 2, CHUNKS, lambda c, parity: step(CHUNKS * l + c, l, s, c, parity))

            layer(0, 0)
            with eng.Fori(0, (LAYERS - 2) // 2) as j:
                layer(1 + 2 * j, 1)
                layer(2 + 2 * j, 0)
            layer(LAYERS - 1, 1)
            step(CHUNKS * LAYERS, LAYERS, 0, 0, 0)
            step(CHUNKS * LAYERS + 1, LAYERS, 0, 1, 1)

        def known(value, least):
            return not isinstance(value, int) or value >= least

        def has(g, l, c, back):
            if isinstance(l, int) and l == 0 and isinstance(c, int) and c < back:
                return None
            if isinstance(l, int) and l == LAYERS and c >= back:
                return None
            if isinstance(c, int) and c < back:
                return c - back + CHUNKS, 1
            return c - back, 0

        @block.sync
        def _(sp):
            ahead.sync(sp)
            in_loop(sp, 1, LAYERS, lambda l, s: c0.load(sp, l))

        @block.gpsimd
        def _(pool):
            ahead.gpsimd(pool)

            def step(g, l, s, c, parity):
                if has(g, l, c, 1) is None:
                    return
                for p in range(CP):
                    q = CP * (g - 1) + p
                    pool.wait_ge(outer_hi, q + 1)
                    pool.tensor_tensor(outer_pair[:, p, LO], outer[:, p], outer_pair[:, p, HI], ALU.subtract).then_inc(outer_split, 1)

            all_steps(pool, step)

        @block.scalar
        def _(act):
            def split_next_hi(l, s, c):
                act.wait_ge(w_loaded, 32 * l + 64)
                c0.piece_hi(act, 1 - s, c)
                if isinstance(c, int) and c == 1:
                    c0.biases_hi(act, l + 1, 1 - s)

            def step(g, l, s, c, parity):
                first = has(g, l, c, 0)
                older, oldest = has(g, l, c, 1), has(g, l, c, 2)

                def outer_to_hi(p):
                    if older:
                        q = CP * (g - 1) + p
                        act.wait_ge(outer_masked, q + 1)
                        if known(q, CP):
                            act.wait_ge(applied, q - CP + 1)
                        act.activation(outer_pair[:, p, HI], outer[:, p], ACT.Copy).then_inc(outer_hi, 1)

                def kv_to_hi(p):
                    if first:
                        act.wait_ge(kv_summed, CP * g + p + 1)
                        act.activation(k_pair[:, p, HI, :], ps_kv[0:PT, p % 2, 0:D], ACT.Copy, scale=1.0 / WS)
                        for i in range(2):
                            out = act.activation(v_pair[:, p, HI, i, :], ps_kv[0:PT, p % 2, D:2 * D], ACT.Copy, scale=own[:, i:i + 1])
                        out.then_inc(kv_hi, 1)

                def y_to_hi():
                    if oldest:
                        act.wait_ge(applied, CP * (g - 1))
                        if known(g, 3):
                            act.wait_ge(x_summed, g - 2)
                        act.activation(y_pair[:, HI], ps_y[:, :, 0:CT], ACT.Copy, scale=1.0 / WS).then_inc(y_hi, 1)

                def x_to_hi():
                    if oldest:
                        chunk, back = oldest
                        wait_apart(act, x_made, g - 1, passed)
                        for m in range(DC):
                            out = act.activation(pair[:, HI, m, bass.ds(chunk * CT, CT)], state[:, m, bass.ds(chunk * CT, CT)], ACT.Identity,
                                                 bias=bias_sum[:, bass.ds(l - back + 1, 1), m:m + 1].rearrange("p a b -> p (a b)"))
                        out.then_inc(x_hi, 1)

                def q_to_hi():
                    if first:
                        if known(g, 2):
                            act.wait_ge(applied, CP * (g - 1))
                        wait_apart(act, q_summed, g + 1, passed)
                        for m in range(DC):
                            out = act.activation(q_pair[:, parity, HI, m, :], ps_x[:, m, 0:CT], ACT.Identity,
                                                 bias=q_b[:, bass.ds(l, 1), m:m + 1].rearrange("p a b -> p (a b)"))
                        out.then_inc(q_hi, 1)

                kv_to_hi(0)
                outer_to_hi(0)
                y_to_hi()
                kv_to_hi(1)
                outer_to_hi(1)
                kv_to_hi(2)
                outer_to_hi(2)
                if first and not (isinstance(l, int) and l == LAYERS - 1):
                    split_next_hi(l, s, c)
                outer_to_hi(3)
                x_to_hi()
                kv_to_hi(3)
                q_to_hi()

            all_steps(act, step)
            ahead.scalar(act)

        @block.vector
        def _(dve):
            def step(g, l, s, c, parity):
                first = has(g, l, c, 0)
                older, oldest = has(g, l, c, 1), has(g, l, c, 2)

                def mask_outer(p):
                    if older:
                        q = CP * (g - 1) + p
                        dve.wait_ge(outer_summed, q + 1)
                        if known(q, CP):
                            dve.wait_ge(outer_split, q - CP + 1)
                        dve.tensor_tensor(outer[:, p], ps_o[:, p % 2], mask[:, :, :, :], ALU.mult).then_inc(outer_masked, 1)

                def kv_to_lo(p):
                    if first:
                        dve.wait_ge(kv_hi, CP * g + p + 1)
                        dve.scalar_tensor_tensor(k_pair[:, p, LO, :], ps_kv[0:PT, p % 2, 0:D], 1.0 / WS, k_pair[:, p, HI, :],
                                                 ALU.mult, ALU.subtract)
                        for i in range(2):
                            out = dve.scalar_tensor_tensor(v_pair[:, p, LO, i, :], ps_kv[0:PT, p % 2, D:2 * D], own[:, i:i + 1],
                                                           v_pair[:, p, HI, i, :], ALU.mult, ALU.subtract)
                        out.then_inc(kv_split, 1)

                def y_to_lo():
                    if oldest:
                        dve.wait_ge(y_hi, g - 1)
                        dve.scalar_tensor_tensor(y_pair[:, LO], ps_y[:, :, 0:CT], 1.0 / WS, y_pair[:, HI],
                                                 ALU.mult, ALU.subtract).then_inc(y_split, 1)

                def make_x():
                    if oldest:
                        chunk, back = oldest
                        dve.wait_ge(x_summed, g - 1)
                        x = state[:, :, bass.ds(chunk * CT, CT)]
                        dve.scalar_tensor_tensor(x, ps_x[:, :, 0:CT], 1.0 / WS, x, ALU.mult, ALU.add).then_inc(x_made, 1)

                def x_to_lo():
                    if oldest:
                        chunk, back = oldest
                        dve.wait_ge(x_hi, g - 1)
                        for m in range(DC):
                            out = dve.scalar_tensor_tensor(pair[:, LO, m, bass.ds(chunk * CT, CT)], state[:, m, bass.ds(chunk * CT, CT)],
                                                           bias_sum[:, bass.ds(l - back + 1, 1), m:m + 1].rearrange("p a b -> p (a b)"),
                                                           pair[:, HI, m, bass.ds(chunk * CT, CT)], ALU.add, ALU.subtract)
                        out.then_inc(x_split, 1)

                def q_to_lo():
                    if first:
                        dve.wait_ge(q_hi, g + 1)
                        for m in range(DC):
                            out = dve.scalar_tensor_tensor(q_pair[:, parity, LO, m, :], ps_x[:, m, 0:CT],
                                                           q_b[:, bass.ds(l, 1), m:m + 1].rearrange("p a b -> p (a b)"),
                                                           q_pair[:, parity, HI, m, :], ALU.add, ALU.subtract)
                        out.then_inc(q_split, 1)

                mask_outer(0)
                kv_to_lo(0)
                mask_outer(1)
                y_to_lo()
                kv_to_lo(1)
                mask_outer(2)
                kv_to_lo(2)
                mask_outer(3)
                make_x()
                x_to_lo()
                kv_to_lo(3)
                if first and not (isinstance(l, int) and l == LAYERS - 1):
                    c0.piece_lo(dve, PIECES * (l + 1) + c + 1, 1 - s, c)
                    if isinstance(c, int) and c == 1:
                        c0.biases_lo(dve, l + 1, 1 - s)
                q_to_lo()

            all_steps(dve, step)
            ahead.vector(dve)

        @block.tensor
        def _(pe):
            def step(g, l, s, c, parity):
                first = has(g, l, c, 0)
                older, oldest = has(g, l, c, 1), has(g, l, c, 2)
                w_qkv = w_pair[:, s, :, 0:6 * PIECE].rearrange("p a (c n) -> p a c n", c=DC)

                def outer_products(p):
                    q = CP * (g - 1) + p
                    pe.wait_ge(kv_split, q + 1)
                    if known(q, 2):
                        pe.wait_ge(outer_masked, q - 1)
                    for m in range(DC):
                        mm = split_matmuls(pe, ps_o[:, p % 2, :, m, :], lambda a, _: k_pair[:, p, a, m * P:(m + 1) * P],
                                           lambda b, _: v_pair[:, p, b, :, m * P:(m + 1) * P], 1,
                                           first_start=(m == 0), check=False)
                    mm.then_inc(outer_summed, 1)

                def keys_and_values(p):
                    if known(CP * g + p, 2):
                        pe.wait_ge(kv_split, CP * g + p - 1)
                    pe.matmul(ps_kv[0:PT, p % 2, :], ones[:, 0:PT], kv_b_rows[:, s, :], start=True, stop=False)
                    for n, (m, a, b) in enumerate((m, a, b) for m in range(DC) for a, b in ((HI, HI), (HI, LO), (LO, HI))):
                        mm = pe.matmul(ps_kv[0:PT, p % 2, :], pair[:, a, m, bass.ds(c * CT + p * PT, PT)], w_qkv[:, b, m, D:3 * D],
                                       start=False, stop=(n == 3 * DC - 1))
                    mm.then_inc(kv_summed, 1)

                def queries():
                    if known(g, 2):
                        pe.wait_ge(x_made, g - 1)
                    for m in range(DC):
                        mm = split_matmuls(pe, ps_x[:, m, 0:CT], lambda a, k: w_qkv[:, a, k, m * P:(m + 1) * P],
                                           lambda b, k: pair[:, b, k, bass.ds(c * CT, CT)], DC)
                    mm.then_inc(q_summed, 1)

                def apply(p, back):
                    pe.wait_ge(outer_split, CP * (g - back) + p + 1)
                    if p == 0:
                        pe.wait_ge(q_split, g)
                        if known(g, 2):
                            pe.wait_ge(y_split, g - 1)
                    for i in range(2):
                        cols = slice((2 * p + i) * TOK, (2 * p + i + 1) * TOK)
                        for m in range(DC):
                            mm = split_matmuls(pe, ps_y[:, m, cols], lambda a, _: outer_pair[:, p, a, i, m, :],
                                               lambda b, _: q_pair[:, (parity - back) % 2, b, m, cols], 1,
                                               first_start=(p == 0 and i == 0), check=False)
                    mm.then_inc(applied, 1)

                def project():
                    chunk, back = oldest
                    slot = s if back == 0 else 1 - s
                    w_proj = w_pair[:, slot, :, 6 * PIECE:8 * PIECE].rearrange("p a (c n) -> p a c n", c=DC)
                    pe.wait_ge(w_split, PIECES * (l - back + 1))
                    pe.wait_ge(y_split, g - 1)
                    pe.wait_ge(q_split, g if older else g - 1)
                    for m in range(DC):
                        mm = split_matmuls(pe, ps_x[:, m, 0:CT], lambda a, k: w_proj[:, a, k, m * P:(m + 1) * P],
                                           lambda b, k: y_pair[:, b, k, :], DC)
                    mm.then_inc(x_summed, 1)

                if first:
                    if isinstance(c, int) and c == 0:
                        pe.wait_ge(w_split, PIECES * l + 6)
                        pe.wait_ge(b_split, l + 1)
                    if not (isinstance(l, int) and l == 0):
                        pe.wait_ge(x_split, g - CHUNKS + 1)
                for p in range(CP):
                    if older:
                        outer_products(p)
                    if p == 3 and oldest:
                        project()
                    if p == 1 and oldest:
                        apply(3, 2)
                    if first:
                        keys_and_values(p)
                    if p == 0 and oldest:
                        apply(2, 2)
                    if p >= 2 and older:
                        apply(p - 2, 1)
                if first:
                    queries()

            all_steps(pe, step)


GATED = 8
RANK = 8


MIX = RANK + GATED


def final_constants(nc, ctx, d):
    def sb(name, shape, dt=F32):
        return ctx.enter_context(nc.sbuf_tensor(name, shape, dt))

    base_raw = sb("base_raw", [P, DC, D])
    mix_raw = sb("mix_raw", [P, DC, MIX])
    lora_raw = sb("lora_raw", [P, D])
    b_raw = sb("final_b_raw", [33, D + MIX])
    b_hi = sb("final_b_hi", [33, D + MIX], F16)
    c = Prepared()
    c.base_pair = sb("base_pair", [P, 2, DC, D], F16)
    c.mix_pair = sb("mix_pair", [P, 2, DC, MIX], F16)
    c.lora_pair = sb("lora_pair", [P, 2, D], F16)
    c.b_rows = sb("final_b_rows", [P, D + MIX], F16)
    c.ones = sb("ones_h", [P, P], F16)
    c.ident = sb("ident_h", [P, P])
    c.power = sb("power_h", [P, 1])
    c.gated = sb("gated", [P, 2, P])
    loaded, prep = [ctx.enter_context(nc.semaphore(name)) for name in ("h_loaded", "h_prep")]

    def sync(sp):
        sp.wait_ge(prep, 2)
        sp.dma_start(base_raw[:, :, :], d["base_w"]).then_inc(loaded, 16)
        sp.dma_start(mix_raw[:, :, 0:RANK], d["lora_a"]).then_inc(loaded, 16)
        sp.dma_start(mix_raw[:, :, RANK:MIX], d["router_w"]).then_inc(loaded, 16)
        sp.dma_start(lora_raw[0:GATED * RANK, :], d["lora_b"]).then_inc(loaded, 16)
        for row in (0, 32):
            sp.dma_start(b_raw[row:row + 1, 0:D], d["base_b"]).then_inc(loaded, 16)
            sp.dma_start(b_raw[row:row + 1, D + RANK:D + MIX], d["router_b"]).then_inc(loaded, 16)

    def gpsimd(pool):
        pool.memset(lora_raw[:, :], 0.0).then_inc(prep, 1)
        pool.memset(b_raw[:, :], 0.0).then_inc(prep, 1)
        pool.memset(c.ident[:, :], 0.0).then_inc(prep, 1)
        pool.wait_ge(prep, 3)
        pool.affine_select(out=c.ident[:, :], in_=c.ident[:, :], compare_op=ALU.not_equal, fill=1.0,
                           base=0, pattern=[[-1, P]], channel_multiplier=1)
        pool.memset(c.power[:, :], -0.5)
        pool.memset(c.ones[:, :], 1.0)
        pool.memset(c.gated[:, :, :], 0.0)
        pool.memset(c.b_rows[:, :], 0.0).then_inc(prep, 1)

    def scalar(act):
        act.wait_ge(prep, 4)
        act.wait_ge(loaded, 128)
        act.activation(c.base_pair[:, HI], base_raw[:, :, :], ACT.Copy, scale=WS)
        act.activation(c.mix_pair[:, HI], mix_raw[:, :, :], ACT.Copy, scale=WS)
        act.activation(c.lora_pair[:, HI, :], lora_raw[:, :], ACT.Copy, scale=2.0 * WS)
        act.activation(c.b_rows[0:1, :], b_raw[0:1, :], ACT.Copy, scale=WS)
        act.activation(b_hi[32:33, :], b_raw[32:33, :], ACT.Copy, scale=WS).then_inc(prep, 1)

    def vector(dve):
        dve.wait_ge(prep, 5)
        dve.scalar_tensor_tensor(c.base_pair[:, LO], base_raw[:, :, :], WS, c.base_pair[:, HI], ALU.mult, ALU.subtract)
        dve.scalar_tensor_tensor(c.mix_pair[:, LO], mix_raw[:, :, :], WS, c.mix_pair[:, HI], ALU.mult, ALU.subtract)
        dve.scalar_tensor_tensor(c.lora_pair[:, LO, :], lora_raw[:, :], 2.0 * WS, c.lora_pair[:, HI, :], ALU.mult, ALU.subtract)
        dve.scalar_tensor_tensor(c.b_rows[32:33, :], b_raw[32:33, :], WS, b_hi[32:33, :], ALU.mult, ALU.subtract)

    c.sync, c.gpsimd, c.scalar, c.vector = sync, gpsimd, scalar, vector
    return c


def final_block(nc, d, keep, c):
    residual, state, bias_sum = keep["residual"], keep["state"], keep["bias_sum"]
    with ExitStack() as ctx:
        def sb(name, shape, dt=F32):
            return ctx.enter_context(nc.sbuf_tensor(name, shape, dt))

        def psum(name, shape, dt=F32):
            return ctx.enter_context(nc.psum_tensor(name, shape, dt))

        def sem(name):
            return ctx.enter_context(nc.semaphore(name))

        base_pair, mix_pair, lora_pair, b_rows = c.base_pair, c.mix_pair, c.lora_pair, c.b_rows
        ones, ident, power, gated = c.ones, c.ident, c.power, c.gated
        xb = sb("x_with_bias", [P, 2, DC, P])
        stats = sb("stats_h", [P, 2, 6])
        mean_var = sb("mean_var_h", [P, 2, 2])
        var_eps = sb("var_eps_h", [P, 2])
        rstd = sb("rstd_h", [P, 2])
        x3 = sb("x3", [P, 2, D])
        x3_pair = sb("x3_pair", [P, 2, 2, DC, P], F16)
        top = sb("top_h", [P, 2])
        neg_top = sb("neg_top_h", [P, 2])
        exps = sb("exps_h", [P, 2, GATED])
        sums = sb("sums_h", [P, 2])
        inv = sb("inv_h", [P, 2])
        gates = sb("gates", [P, 2, GATED], mybir.dt.bfloat16)
        mid = sb("mid", [P, 2, RANK])
        gated_pair = sb("gated_pair", [P, 2, 2, P], F16)
        out_tile = sb("out_tile", [P, 2, D])
        ps_x = psum("ps_x_back", [P, 2, 512])
        ps_t = psum("ps_x3_t", [P, 2, 512])
        ps_m = psum("ps_mixed", [P, 2, MIX])
        ps_g = psum("ps_gated_t", [P, 2, P])
        ps_b = psum("ps_out", [P, 2, 512])

        xb_made, turned_back, h_made = sem("xb_made"), sem("turned_back"), sem("h_h_made")
        rstd_made, x3_made = sem("h_rstd"), sem("x3_made")
        turned, x3_hi, x3_split, mixed = sem("h_turned"), sem("x3_hi"), sem("x3_split"), sem("mixed")
        h_summed, h_known, eps_added = sem("h_h_summed"), sem("h_h_known"), sem("h_eps_added")
        top_found, top_negated, exp_made = sem("top_found"), sem("top_negated"), sem("h_exp_made")
        mid_made, inv_made, gates_made, gated_made = sem("mid_made"), sem("inv_made"), sem("gates_made"), sem("gated_made")
        gated_turned, gated_hi, gated_split = sem("gated_turned"), sem("gated_hi"), sem("gated_split")
        based, summed, out_made = sem("based"), sem("out_summed"), sem("out_made")
        passed = keep["passed"]
        stored = [sem("stored0"), sem("stored1")]
        block = ctx.enter_context(nc.Block())

        @block.sync
        def _(sp):
            def store(t, s):
                rows = P if not isinstance(t, int) else min(P, N - t * P)
                sp.wait_ge(out_made, t + 1)
                sp.dma_start(d["out"][bass.ds(t * P, rows), :], out_tile[0:rows, s, :]).then_inc(stored[s], 16)

            in_loop(sp, 0, TILES - 1, store)
            store(TILES - 1, (TILES - 1) % 2)
            sp.wait_ge(stored[0], 16 * ((TILES + 1) // 2))
            sp.wait_ge(stored[1], 16 * (TILES // 2))

        @block.gpsimd
        def _(pool):
            def inverse_root(t, s):
                pool.wait_ge(eps_added, t + 1)
                if later(t):
                    pool.wait_ge(x3_made, t - 1)
                pool.tensor_tensor(rstd[:, s:s + 1], var_eps[:, s:s + 1], power[:, :], ALU.pow).then_inc(rstd_made, 1)

            skewed(pool, TILES, (0, inverse_root))

        @block.scalar
        def _(act):
            def add_bias(t, s):
                if later(t):
                    act.wait_ge(turned_back, t - 1)
                for m in range(DC):
                    out = act.activation(xb[:, s, m, :], state[:, m, bass.ds(t * P, P)], ACT.Identity,
                                         bias=bias_sum[:, LAYERS, m:m + 1])
                out.then_inc(xb_made, 1)

            def turned_hi(t, s):
                act.wait_ge(turned, t + 1)
                if later(t):
                    act.wait_ge(based, t - 1)
                act.activation(x3_pair[:, s, HI], ps_t[:, s, 0:D].rearrange("p (c t) -> p c t", c=DC), ACT.Copy).then_inc(x3_hi, 1)

            def exp(t, s):
                act.wait_ge(top_negated, t + 1)
                if later(t):
                    act.wait_ge(gates_made, t - 1)
                act.activation(exps[:, s, :], ps_m[:, s, RANK:MIX], ACT.Exp, bias=neg_top[:, s:s + 1], scale=1.0 / WS,
                               accum_out=sums[:, s:s + 1]).then_inc(exp_made, 1)

            def gated_to_hi(t, s):
                act.wait_ge(gated_turned, t + 1)
                if later(t):
                    act.wait_ge(summed, t - 1)
                act.activation(gated_pair[:, s, HI, :], ps_g[:, s, :], ACT.Copy).then_inc(gated_hi, 1)

            skewed(act, TILES, (5, turned_hi), (0, add_bias), (6, gated_to_hi), (5, exp))

        @block.vector
        def _(dve):
            def add_x(t, s):
                dve.wait_ge(turned_back, t + 1)
                h = residual[:, bass.ds(t, 1), :]
                dve.tensor_tensor(h, h, ps_x[:, s:s + 1, 0:D], ALU.add).then_inc(h_made, 1)

            def h_stats(t, s):
                wait_apart(dve, h_made, t + 1, passed)
                dve.bn_stats(stats[:, s, :], residual[:, bass.ds(t, 1), :]).then_inc(h_summed, 1)

            def h_mean_var(t, s):
                if later(t):
                    dve.wait_ge(x3_made, t - 1)
                wait_apart(dve, h_summed, t + 1, passed)
                dve.bn_aggr(mean_var[:, s, :], stats[:, s, :]).then_inc(h_known, 1)

            def plus_eps(t, s):
                dve.wait_ge(h_known, t + 1)
                if later(t):
                    dve.wait_ge(rstd_made, t - 1)
                dve.tensor_scalar(var_eps[:, s:s + 1], mean_var[:, s, 1:2], EPS, None, ALU.add).then_inc(eps_added, 1)

            def norm(t, s):
                dve.wait_ge(rstd_made, t + 1)
                if later(t):
                    dve.wait_ge(turned, t - 1)
                dve.tensor_scalar(x3[:, s:s + 1, :], residual[:, bass.ds(t, 1), :], mean_var[:, s, 0:1], rstd[:, s:s + 1],
                                  ALU.subtract, ALU.mult).then_inc(x3_made, 1)

            def turned_lo(t, s):
                dve.wait_ge(x3_hi, t + 1)
                dve.tensor_tensor(x3_pair[:, s, LO], ps_t[:, s, 0:D].rearrange("p (c t) -> p c t", c=DC), x3_pair[:, s, HI],
                                  ALU.subtract).then_inc(x3_split, 1)

            def highest(t, s):
                dve.wait_ge(mixed, t + 1)
                dve.tensor_reduce(top[:, s:s + 1], ps_m[:, s, RANK:MIX], AX.X, ALU.max).then_inc(top_found, 1)

            def negate_top(t, s):
                dve.wait_ge(top_found, t + 1)
                if later(t):
                    dve.wait_ge(exp_made, t - 1)
                dve.tensor_scalar(neg_top[:, s:s + 1], top[:, s:s + 1], -1.0 / WS, None, ALU.mult).then_inc(top_negated, 1)

            def keep_mid(t, s):
                dve.wait_ge(exp_made, t + 1)
                if later(t):
                    dve.wait_ge(gated_made, t - 1)
                dve.tensor_scalar(mid[:, s, :], ps_m[:, s, 0:RANK], 1.0 / WS, None, ALU.mult).then_inc(mid_made, 1)

            def invert_sum(t, s):
                dve.wait_ge(exp_made, t + 1)
                if later(t):
                    dve.wait_ge(gates_made, t - 1)
                dve.reciprocal(inv[:, s:s + 1], sums[:, s:s + 1]).then_inc(inv_made, 1)

            def make_gates(t, s):
                dve.wait_ge(inv_made, t + 1)
                if later(t):
                    dve.wait_ge(gated_made, t - 1)
                dve.tensor_scalar(gates[:, s, :], exps[:, s, :], inv[:, s:s + 1], None, ALU.mult).then_inc(gates_made, 1)

            def gate(t, s):
                dve.wait_ge(gates_made, t + 1)
                dve.wait_ge(mid_made, t + 1)
                if later(t):
                    dve.wait_ge(gated_turned, t - 1)
                dve.tensor_tensor(gated[:, s, 0:GATED * RANK].rearrange("p (e r) -> p e r", r=RANK),
                                  gates[:, s, :, None].to_broadcast([P, GATED, RANK]),
                                  mid[:, s, None, :].to_broadcast([P, GATED, RANK]), ALU.mult).then_inc(gated_made, 1)

            def gated_to_lo(t, s):
                dve.wait_ge(gated_hi, t + 1)
                dve.tensor_tensor(gated_pair[:, s, LO, :], ps_g[:, s, :], gated_pair[:, s, HI, :], ALU.subtract).then_inc(gated_split, 1)

            def finish(t, s):
                dve.wait_ge(summed, t + 1)
                if later(t):
                    dve.wait_ge(stored[s], 8 * t - 8 * s)
                dve.scalar_tensor_tensor(out_tile[:, s:s + 1, :], ps_b[:, s:s + 1, 0:D], 1.0 / WS, residual[:, bass.ds(t, 1), :],
                                         ALU.mult, ALU.add).then_inc(out_made, 1)

            skewed(dve, TILES, (6, invert_sum), (4, norm), (6, make_gates), (2, add_x), (6, keep_mid), (5, turned_lo),
                   (6, gate), (2, h_stats), (7, finish), (5, highest), (2, h_mean_var), (5, negate_top), (2, plus_eps),
                   (6, gated_to_lo))

        @block.tensor
        def _(pe):
            def turn_back(t, s):
                pe.wait_ge(xb_made, t + 1)
                if later(t):
                    pe.wait_ge(h_made, t - 1)
                for c in range(DC):
                    mm = pe.transpose(ps_x[:, s, c * P:(c + 1) * P], xb[:, s, c, :], ident[:, :])
                mm.then_inc(turned_back, 1)

            def turn(t, s):
                pe.wait_ge(x3_made, t + 1)
                if later(t):
                    pe.wait_ge(x3_split, t - 1)
                for c in range(DC):
                    mm = pe.transpose(ps_t[:, s, c * P:(c + 1) * P], x3[:, s, c * P:(c + 1) * P], ident[:, :])
                mm.then_inc(turned, 1)

            def mix(t, s):
                pe.wait_ge(x3_split, t + 1)
                if later(t):
                    pe.wait_ge(exp_made, t - 1)
                    pe.wait_ge(mid_made, t - 1)
                pe.matmul(ps_m[:, s, :], ones[:, :], b_rows[:, D:D + MIX], start=True, stop=False)
                split_matmuls(pe, ps_m[:, s, :], lambda a, c: x3_pair[:, s, a, c, :], lambda b, c: mix_pair[:, b, c, :], DC,
                              first_start=False).then_inc(mixed, 1)

            def base(t, s):
                if later(t):
                    pe.wait_ge(out_made, t - 1)
                pe.matmul(ps_b[:, s, 0:D], ones[:, :], b_rows[:, 0:D], start=True, stop=False, skip_group_check=True)
                for n, (c, a, b) in enumerate((c, a, b) for c in range(DC) for a, b in ((HI, HI), (HI, LO), (LO, HI))):
                    mm = pe.matmul(ps_b[:, s, 0:D], x3_pair[:, s, a, c, :], base_pair[:, b, c, :], start=False, stop=False,
                                   skip_group_check=True)
                mm.then_inc(based, 1)

            def turn_gated(t, s):
                pe.wait_ge(gated_made, t + 1)
                if later(t):
                    pe.wait_ge(gated_split, t - 1)
                pe.transpose(ps_g[:, s, :], gated[:, s, :], ident[:, :]).then_inc(gated_turned, 1)

            def add_lora(t, s):
                pe.wait_ge(gated_split, t + 1)
                split_matmuls(pe, ps_b[:, s, 0:D], lambda a, _: gated_pair[:, s, a, :], lambda b, _: lora_pair[:, b, :], 1,
                              first_start=False, check=False).then_inc(summed, 1)

            skewed(pe, TILES, (7, add_lora), (6, base), (5, mix), (6, turn_gated), (0, turn_back), (4, turn))


def vit_tower(nc, d):
    keep = {
        "queue": nc.dram_tensor("queue", (QUEUE_TILES * ROWS, D), F32, kind="Internal").ap(),
        "answers": nc.dram_tensor("answers", (QUEUE_TILES * ROWS, D), F32, kind="Internal").ap(),
    }

    def hold(ctx, name, shape, dt=F32):
        keep[name] = ctx.enter_context(nc.sbuf_tensor(name, shape, dt))

    with ExitStack() as whole:
        keep["passed"] = whole.enter_context(nc.semaphore("passed"))
        hold(whole, "residual", [P, TILES, D])
        hold(whole, "chan_a", [P, 2, DC, NPAD], F16)
        hold(whole, "weights", [P, TOP, TILES])
        hold(whole, "places", [P, TOP, TILES], I32)
        hold(whole, "bounds", [P, 2, EXPERTS], I32)
        hold(whole, "bias_sum", [P, LAYERS + 1, DC])
        embed_and_norm(nc, d, keep)
        with ExitStack() as early:
            hold(early, "chan_b", [P, 2, DC, NPAD], F16)
            channel_attention(nc, d, keep)
            hold(early, "rows", [P, TILES, D])
            of_experts = expert_constants(nc, early, d)
            project_and_route(nc, d, keep, of_experts)
            experts(nc, d, keep, of_experts)
        hold(whole, "state", [P, DC, NPAD])
        of_layers = layer_constants(nc, whole, d, keep)
        gather_and_norm(nc, d, keep, of_layers)
        of_final = final_constants(nc, whole, d)
        linear_attention_layers(nc, d, keep, of_layers, of_final)
        final_block(nc, d, keep, of_final)




def lay_out(x, L0_tok_W, L0_tok_b, L0_attn_norm_w, L0_attn_norm_b, L0_attn_qkv_w, L0_attn_qkv_b, L0_attn_proj_w,
            L0_attn_proj_b, L0_ffn_W_gate, L0_ffn_W_in, L0_ffn_b_in, L0_ffn_W_out, L0_ffn_b_out, L1_attn_Wqkv,
            L1_attn_bqkv, L1_attn_Wproj, L1_attn_bproj, L1_ffn_base_w, L1_ffn_base_b, L1_ffn_lora_A, L1_ffn_lora_B,
            L1_ffn_router_w, L1_ffn_router_b):
    def rows(w):
        return w.reshape(-1, P, w.shape[-1]).transpose(1, 0, 2)

    patches = x.reshape(IMAGES, CHANS, SIDE, PATCH, SIDE, PATCH).transpose(0, 2, 4, 1, 3, 5).reshape(N, FEAT)
    padded = np.zeros((NPAD, FEAT), x.dtype)
    padded[:N] = patches
    return {
        "patches": padded.reshape(TILES, P, FC, P).transpose(0, 3, 2, 1).reshape(TILES, P, FC * P),
        "tok_w": rows(L0_tok_W.T), "tok_b": L0_tok_b,
        "norm_w": L0_attn_norm_w, "norm_b": L0_attn_norm_b,
        "qkv0_w": rows(L0_attn_qkv_w.T), "qkv0_b": L0_attn_qkv_b.reshape(1, -1),
        "qkv0_bcol": L0_attn_qkv_b.reshape(-1, P).T,
        "proj0_w": rows(L0_attn_proj_w.T), "proj0_b": L0_attn_proj_b.reshape(1, -1),
        "gate_w": rows(L0_ffn_W_gate),
        "in_w": np.stack([rows(w) for w in L0_ffn_W_in]), "in_b": L0_ffn_b_in.reshape(-1, 8, P).transpose(2, 0, 1),
        "out_w": np.stack([rows(w) for w in L0_ffn_W_out]), "out_b": L0_ffn_b_out.reshape(1, -1),
        "qkv1_w": np.stack([rows(w.T) for w in L1_attn_Wqkv]), "qkv1_b": L1_attn_bqkv,
        "q1_bcol": L1_attn_bqkv[:, :D].reshape(-1, DC, P).transpose(2, 0, 1),
        "proj1_w": np.stack([rows(w.T) for w in L1_attn_Wproj]),
        "proj1_bcol": L1_attn_bproj.reshape(-1, DC, P).transpose(2, 0, 1),
        "base_w": rows(L1_ffn_base_w.T), "base_b": L1_ffn_base_b.reshape(1, -1),
        "lora_a": rows(L1_ffn_lora_A), "lora_b": L1_ffn_lora_B.reshape(-1, D),
        "router_w": rows(L1_ffn_router_w.T), "router_b": L1_ffn_router_b.reshape(1, -1),
    }


def kernel(**inputs):
    import concourse.bacc as bacc
    from concourse.bass_utils import run_bass_kernel_spmd

    nc = bacc.Bacc("TRN2", target_bir_lowering=False, num_devices=1)
    arrays, d = {}, {}
    for name, a in lay_out(**{k: np.asarray(v) for k, v in inputs.items()}).items():
        a = np.ascontiguousarray(a)
        arrays[f"in_{name}_dram"] = a
        d[name] = nc.dram_tensor(f"in_{name}_dram", a.shape, mybir.dt.from_np(a.dtype), kind="ExternalInput").ap()
    d["out"] = nc.dram_tensor("out_dram", (N, D), F32, kind="ExternalOutput").ap()
    vit_tower(nc, d)
    r = run_bass_kernel_spmd(nc, [arrays], core_ids=[0])
    return r.results[0]["out_dram"].reshape(IMAGES, TOK, D)
```
